# Optimizing a Trainium2 kernel written in Bass

```python
import numpy as np
import jax
import jax.numpy as jnp

def _softmax(x, axis=-1):
    return jax.nn.softmax(x, axis=axis)

def _gelu(x):
    return jax.nn.gelu(x, approximate=True)

def _silu(x):
    return jax.nn.silu(x)

def _sigmoid(x):
    return jax.nn.sigmoid(x)

def _layernorm(x, axis=-1, eps=1e-05):
    m = jnp.mean(x, axis=axis, keepdims=True)
    v = jnp.var(x, axis=axis, keepdims=True)
    return (x - m) / jnp.sqrt(v + eps)

def _scatter_add(tgt, idx, src, axis=0):
    return tgt.at[idx].add(src)

def _segment_sum(src, seg, n):
    return jax.ops.segment_sum(src, seg, n)
kernel_name = 'mk_hybrid_d2_jaxref_r8_6826d5'

def setup_inputs(seed: int=0):
    np.random.seed(seed)
    _w = jnp.asarray

    def _L0_attn_a_setup():
        import jax, jax.numpy as jnp
        import numpy as np
        B, T, E, H = (2, 256, 128, 16)
        D = E // H
        key = jax.random.key(seed)
        k = jax.random.split(key, 6)
        return {'x': jax.random.normal(k[0], (B, T, E), dtype=jnp.float32), 'w_att_val': jax.random.normal(k[1], (H, D, D), dtype=jnp.float32) * (6.0 / D) ** 0.5, 'wv_w': jax.random.normal(k[2], (E, E), dtype=jnp.float32) * E ** (-0.5), 'wv_b': jnp.zeros((E,), dtype=jnp.float32), 'out_w': jax.random.normal(k[3], (E, E), dtype=jnp.float32) * E ** (-0.5), 'out_b': jnp.zeros((E,), dtype=jnp.float32)}
    _L0_attn_a_in = _L0_attn_a_setup()

    def _L0_attn_b_setup():
        import jax, jax.numpy as jnp
        import numpy as np
        D = 128
        H = 16
        KVH = 4
        HD = D // H
        LAT = 32
        WIN = 32
        B, S = (1, 256)
        BASE_G, BASE_L = (1000000.0, 10000.0)
        EPS = 1e-06

        def rmsnorm(x, w):
            return x * jax.lax.rsqrt(jnp.mean(x * x, axis=-1, keepdims=True) + EPS) * w

        def qk_norm(x):
            return x * jax.lax.rsqrt(jnp.mean(x * x, axis=-1, keepdims=True) + EPS)

        def rope(x, base):
            s, hd = (x.shape[-2], x.shape[-1])
            inv_freq = 1.0 / base ** (jnp.arange(0, hd, 2, dtype=jnp.float32) / hd)
            freqs = jnp.arange(s, dtype=jnp.float32)[:, None] * inv_freq[None, :]
            cos, sin = (jnp.cos(freqs), jnp.sin(freqs))
            xe, xo = (x[..., ::2], x[..., 1::2])
            out = jnp.stack([xe * cos - xo * sin, xe * sin + xo * cos], axis=-1)
            return out.reshape(x.shape)

        def split_heads(x, n_heads):
            b, s, _ = x.shape
            return x.reshape(b, s, n_heads, HD).transpose(0, 2, 1, 3)

        def repeat_kv(x):
            return jnp.repeat(x, H // KVH, axis=1)

        def sdpa(q, k, v, mask):
            scores = jnp.einsum('bhqd,bhkd->bhqk', q, k) / np.sqrt(HD).astype(np.float32)
            scores = jnp.where(mask, scores, jnp.float32(-1e+30))
            probs = jax.nn.softmax(scores, axis=-1)
            return jnp.einsum('bhqk,bhkd->bhqd', probs, v)

        def merge_heads(x):
            b, h, s, hd = x.shape
            return x.transpose(0, 2, 1, 3).reshape(b, s, h * hd)

        def global_latent_attn(x, wq, w_kv_down, w_k_up, w_v_up, wo):
            q = split_heads(x @ wq, H)
            latent = x @ w_kv_down
            k = split_heads(latent @ w_k_up, KVH)
            v = split_heads(latent @ w_v_up, KVH)
            q, k = (rope(q, BASE_G), rope(k, BASE_G))
            q, k = (qk_norm(q), qk_norm(k))
            k, v = (repeat_kv(k), repeat_kv(v))
            i = jnp.arange(x.shape[1])
            causal = i[:, None] >= i[None, :]
            return merge_heads(sdpa(q, k, v, causal)) @ wo

        def local_gqa_attn(x, wq, wk, wv, wo):
            q = split_heads(x @ wq, H)
            k = split_heads(x @ wk, KVH)
            v = split_heads(x @ wv, KVH)
            q, k = (rope(q, BASE_L), rope(k, BASE_L))
            q, k = (qk_norm(q), qk_norm(k))
            k, v = (repeat_kv(k), repeat_kv(v))
            i = jnp.arange(x.shape[1])
            diff = i[:, None] - i[None, :]
            mask = (diff >= 0) & (diff < WIN)
            return merge_heads(sdpa(q, k, v, mask)) @ wo
        key = jax.random.key(seed)
        ks = jax.random.split(key, 12)
        std = 0.02
        return {'hidden': jax.random.normal(ks[0], (B, S, D), dtype=jnp.float32), 'norm1_w': jnp.ones((D,), jnp.float32), 'norm2_w': jnp.ones((D,), jnp.float32), 'g_wq': jax.random.normal(ks[1], (D, H * HD), jnp.float32) * std, 'g_kv_down': jax.random.normal(ks[2], (D, LAT), jnp.float32) * std, 'g_k_up': jax.random.normal(ks[3], (LAT, KVH * HD), jnp.float32) * std, 'g_v_up': jax.random.normal(ks[4], (LAT, KVH * HD), jnp.float32) * std, 'g_wo': jax.random.normal(ks[5], (D, D), jnp.float32) * std, 'l_wq': jax.random.normal(ks[6], (D, H * HD), jnp.float32) * std, 'l_wk': jax.random.normal(ks[7], (D, KVH * HD), jnp.float32) * std, 'l_wv': jax.random.normal(ks[8], (D, KVH * HD), jnp.float32) * std, 'l_wo': jax.random.normal(ks[9], (D, D), jnp.float32) * std}
    _L0_attn_b_in = _L0_attn_b_setup()

    def _L0_ffn_setup():
        import jax, jax.numpy as jnp
        import numpy as np
        HIDDEN = 128
        INTER = 512
        key = jax.random.key(seed)
        k1, k2, k3, k4, k5 = jax.random.split(key, 5)
        hidden_states = jax.random.normal(k1, (4, 256, HIDDEN), dtype=jnp.float32)
        W1 = jax.random.normal(k2, (HIDDEN, INTER), dtype=jnp.float32) * (1.0 / np.sqrt(HIDDEN))
        b1 = jax.random.normal(k3, (INTER,), dtype=jnp.float32) * 0.02
        W2 = jax.random.normal(k4, (INTER, HIDDEN), dtype=jnp.float32) * (1.0 / np.sqrt(INTER))
        b2 = jax.random.normal(k5, (HIDDEN,), dtype=jnp.float32) * 0.02
        return {'hidden_states': hidden_states, 'W1': W1, 'b1': b1, 'W2': W2, 'b2': b2}
    _L0_ffn_in = _L0_ffn_setup()

    def _L1_attn_a_setup():
        import jax, jax.numpy as jnp
        import numpy as np
        DIM = 128
        NUM_HEADS = 16
        NUM_KV_HEADS = 2
        HEAD_DIM = DIM // NUM_HEADS
        REPEATS = NUM_HEADS // NUM_KV_HEADS
        WINDOW = 32
        HALF = WINDOW // 2
        BATCH, SEQ = (2, 256)
        key = jax.random.key(seed)
        ks = jax.random.split(key, 9)
        sc = 1.0 / np.sqrt(DIM)
        return {'x': jax.random.normal(ks[0], (BATCH, SEQ, DIM), jnp.float32), 'Wq': jax.random.normal(ks[1], (DIM, NUM_HEADS * HEAD_DIM), jnp.float32) * sc, 'bq': jax.random.normal(ks[2], (NUM_HEADS * HEAD_DIM,), jnp.float32) * 0.01, 'Wk': jax.random.normal(ks[3], (DIM, NUM_KV_HEADS * HEAD_DIM), jnp.float32) * sc, 'bk': jax.random.normal(ks[4], (NUM_KV_HEADS * HEAD_DIM,), jnp.float32) * 0.01, 'Wv': jax.random.normal(ks[5], (DIM, NUM_KV_HEADS * HEAD_DIM), jnp.float32) * sc, 'bv': jax.random.normal(ks[6], (NUM_KV_HEADS * HEAD_DIM,), jnp.float32) * 0.01, 'Wo': jax.random.normal(ks[7], (DIM, DIM), jnp.float32) * sc, 'bo': jax.random.normal(ks[8], (DIM,), jnp.float32) * 0.01}
    _L1_attn_a_in = _L1_attn_a_setup()

    def _L1_attn_b_setup():
        import jax, jax.numpy as jnp
        import numpy as np
        D_MODEL = 128
        N_HEADS = 8
        N_KV_HEADS = 4
        HEAD_DIM = D_MODEL // N_HEADS
        N_REP = N_HEADS // N_KV_HEADS
        WINDOW = 128
        SINKS = 4
        ROPE_BASE = 10000.0
        SCALE = 1.0 / np.sqrt(HEAD_DIM)

        def _trigram_dirs():
            t = np.array([[s0, s1, s2] for s0 in (1.0, -1.0) for s1 in (1.0, -1.0) for s2 in (1.0, -1.0)], dtype=np.float32)
            t = t / np.linalg.norm(t, axis=1, keepdims=True)
            return jnp.asarray(t[:N_HEADS])

        def _rope_tables(T):
            inv_freq = 1.0 / ROPE_BASE ** (jnp.arange(0, HEAD_DIM, 2, dtype=jnp.float32) / HEAD_DIM)
            freqs = jnp.arange(T, dtype=jnp.float32)[:, None] * inv_freq[None, :]
            return (jnp.cos(freqs), jnp.sin(freqs))

        def _apply_rope(t, cos, sin):
            t1, t2 = jnp.split(t, 2, axis=-1)
            c = cos[None, None, :, :]
            s = sin[None, None, :, :]
            return jnp.concatenate([t1 * c - t2 * s, t2 * c + t1 * s], axis=-1)
        key = jax.random.key(seed)
        ks = jax.random.split(key, 6)
        B, T = (2, 256)
        std = 0.02
        x = jax.random.normal(ks[0], (B, T, D_MODEL), jnp.float32)
        Wq = jax.random.normal(ks[1], (D_MODEL, N_HEADS * HEAD_DIM), jnp.float32) * std
        Wk = jax.random.normal(ks[2], (D_MODEL, N_KV_HEADS * HEAD_DIM), jnp.float32) * std
        Wv = jax.random.normal(ks[3], (D_MODEL, N_KV_HEADS * HEAD_DIM), jnp.float32) * std
        Wo = jax.random.normal(ks[4], (D_MODEL, D_MODEL), jnp.float32) * std
        head_scales = jax.random.normal(ks[5], (N_HEADS,), jnp.float32) * 0.1
        head_dirs = _trigram_dirs()
        return {'x': x, 'Wq': Wq, 'Wk': Wk, 'Wv': Wv, 'Wo': Wo, 'head_scales': head_scales, 'head_dirs': head_dirs}
    _L1_attn_b_in = _L1_attn_b_setup()

    def _L1_ffn_setup():
        import jax, jax.numpy as jnp
        import numpy as np
        E, K = (8, 2)
        DM, DE = (128, 352)
        B, S = (1, 256)
        EPS = 1e-06

        def _rmsnorm(x, w):
            var = jnp.mean(jnp.square(x), axis=-1, keepdims=True)
            return x * jax.lax.rsqrt(var + EPS) * w
        key = jax.random.key(seed)
        kx, kg, k1, k2, k3 = jax.random.split(key, 5)

        def kaiming_uniform(k, shape, fan_in):
            bound = 1.0 / np.sqrt(fan_in)
            return jax.random.uniform(k, shape, jnp.float32, -bound, bound)
        return {'x': jax.random.normal(kx, (B, S, DM), jnp.float32), 'gate_w': kaiming_uniform(kg, (E, DM), DM), 'rms_w': jnp.ones((DM,), jnp.float32), 'W1': kaiming_uniform(k1, (E, DE, DM), DE * DM), 'W2': kaiming_uniform(k2, (E, DE, DM), DE * DM), 'W3': kaiming_uniform(k3, (E, DM, DE), DM * DE)}
    _L1_ffn_in = _L1_ffn_setup()
    _d = {'L0_attn_a_x': _L0_attn_a_in['x'], 'L0_attn_a_w_att_val': _L0_attn_a_in['w_att_val'], 'L0_attn_a_wv_w': _L0_attn_a_in['wv_w'], 'L0_attn_a_wv_b': _L0_attn_a_in['wv_b'], 'L0_attn_a_out_w': _L0_attn_a_in['out_w'], 'L0_attn_a_out_b': _L0_attn_a_in['out_b'], 'L0_attn_b_norm1_w': _L0_attn_b_in['norm1_w'], 'L0_attn_b_norm2_w': _L0_attn_b_in['norm2_w'], 'L0_attn_b_g_wq': _L0_attn_b_in['g_wq'], 'L0_attn_b_g_kv_down': _L0_attn_b_in['g_kv_down'], 'L0_attn_b_g_k_up': _L0_attn_b_in['g_k_up'], 'L0_attn_b_g_v_up': _L0_attn_b_in['g_v_up'], 'L0_attn_b_g_wo': _L0_attn_b_in['g_wo'], 'L0_attn_b_l_wq': _L0_attn_b_in['l_wq'], 'L0_attn_b_l_wk': _L0_attn_b_in['l_wk'], 'L0_attn_b_l_wv': _L0_attn_b_in['l_wv'], 'L0_attn_b_l_wo': _L0_attn_b_in['l_wo'], 'L0_ffn_W1': _L0_ffn_in['W1'], 'L0_ffn_b1': _L0_ffn_in['b1'], 'L0_ffn_W2': _L0_ffn_in['W2'], 'L0_ffn_b2': _L0_ffn_in['b2'], 'L1_attn_a_Wq': _L1_attn_a_in['Wq'], 'L1_attn_a_bq': _L1_attn_a_in['bq'], 'L1_attn_a_Wk': _L1_attn_a_in['Wk'], 'L1_attn_a_bk': _L1_attn_a_in['bk'], 'L1_attn_a_Wv': _L1_attn_a_in['Wv'], 'L1_attn_a_bv': _L1_attn_a_in['bv'], 'L1_attn_a_Wo': _L1_attn_a_in['Wo'], 'L1_attn_a_bo': _L1_attn_a_in['bo'], 'L1_attn_b_Wq': _L1_attn_b_in['Wq'], 'L1_attn_b_Wk': _L1_attn_b_in['Wk'], 'L1_attn_b_Wv': _L1_attn_b_in['Wv'], 'L1_attn_b_Wo': _L1_attn_b_in['Wo'], 'L1_attn_b_head_scales': _L1_attn_b_in['head_scales'], 'L1_attn_b_head_dirs': _L1_attn_b_in['head_dirs'], 'L1_ffn_gate_w': _L1_ffn_in['gate_w'], 'L1_ffn_rms_w': _L1_ffn_in['rms_w'], 'L1_ffn_W1': _L1_ffn_in['W1'], 'L1_ffn_W2': _L1_ffn_in['W2'], 'L1_ffn_W3': _L1_ffn_in['W3']}
    _x0 = _d['L0_attn_a_x']
    _d['L0_attn_a_x'] = jax.random.normal(jax.random.fold_in(jax.random.key(seed), 1), (4, 1024, 128), dtype=_x0.dtype)
    del _x0
    return _d

def reference(L0_attn_a_x, L0_attn_a_w_att_val, L0_attn_a_wv_w, L0_attn_a_wv_b, L0_attn_a_out_w, L0_attn_a_out_b, L0_attn_b_norm1_w, L0_attn_b_norm2_w, L0_attn_b_g_wq, L0_attn_b_g_kv_down, L0_attn_b_g_k_up, L0_attn_b_g_v_up, L0_attn_b_g_wo, L0_attn_b_l_wq, L0_attn_b_l_wk, L0_attn_b_l_wv, L0_attn_b_l_wo, L0_ffn_W1, L0_ffn_b1, L0_ffn_W2, L0_ffn_b2, L1_attn_a_Wq, L1_attn_a_bq, L1_attn_a_Wk, L1_attn_a_bk, L1_attn_a_Wv, L1_attn_a_bv, L1_attn_a_Wo, L1_attn_a_bo, L1_attn_b_Wq, L1_attn_b_Wk, L1_attn_b_Wv, L1_attn_b_Wo, L1_attn_b_head_scales, L1_attn_b_head_dirs, L1_ffn_gate_w, L1_ffn_rms_w, L1_ffn_W1, L1_ffn_W2, L1_ffn_W3):

    def _L0_attn_a_ref(x, w_att_val, wv_w, wv_b, out_w, out_b):
        import jax, jax.numpy as jnp
        import numpy as np
        B, T, E, H = (2, 256, 128, 16)
        D = E // H
        b, t, e = x.shape
        h, d, _ = w_att_val.shape
        x_h = x.reshape(b, t, h, d).transpose(0, 2, 1, 3)
        xw = jnp.einsum('bhtd,hde->bhte', x_h, w_att_val)
        att = jnp.einsum('bhte,bhse->bhts', xw, x_h) / jnp.sqrt(jnp.asarray(d, x.dtype))
        att = jax.nn.softmax(att, axis=-1)
        vx = x @ wv_w.T + wv_b
        vx = vx.reshape(b, t, h, d).transpose(0, 2, 1, 3)
        o = jnp.einsum('bhts,bhsd->bhtd', att, vx)
        o = o.transpose(0, 2, 1, 3).reshape(b, t, e)
        return o @ out_w.T + out_b

    def _L0_attn_b_ref(hidden, norm1_w, norm2_w, g_wq, g_kv_down, g_k_up, g_v_up, g_wo, l_wq, l_wk, l_wv, l_wo):
        import jax, jax.numpy as jnp
        import numpy as np
        D = 128
        H = 16
        KVH = 4
        HD = D // H
        LAT = 32
        WIN = 32
        B, S = (1, 256)
        BASE_G, BASE_L = (1000000.0, 10000.0)
        EPS = 1e-06

        def rmsnorm(x, w):
            return x * jax.lax.rsqrt(jnp.mean(x * x, axis=-1, keepdims=True) + EPS) * w

        def qk_norm(x):
            return x * jax.lax.rsqrt(jnp.mean(x * x, axis=-1, keepdims=True) + EPS)

        def rope(x, base):
            s, hd = (x.shape[-2], x.shape[-1])
            inv_freq = 1.0 / base ** (jnp.arange(0, hd, 2, dtype=jnp.float32) / hd)
            freqs = jnp.arange(s, dtype=jnp.float32)[:, None] * inv_freq[None, :]
            cos, sin = (jnp.cos(freqs), jnp.sin(freqs))
            xe, xo = (x[..., ::2], x[..., 1::2])
            out = jnp.stack([xe * cos - xo * sin, xe * sin + xo * cos], axis=-1)
            return out.reshape(x.shape)

        def split_heads(x, n_heads):
            b, s, _ = x.shape
            return x.reshape(b, s, n_heads, HD).transpose(0, 2, 1, 3)

        def repeat_kv(x):
            return jnp.repeat(x, H // KVH, axis=1)

        def sdpa(q, k, v, mask):
            scores = jnp.einsum('bhqd,bhkd->bhqk', q, k) / np.sqrt(HD).astype(np.float32)
            scores = jnp.where(mask, scores, jnp.float32(-1e+30))
            probs = jax.nn.softmax(scores, axis=-1)
            return jnp.einsum('bhqk,bhkd->bhqd', probs, v)

        def merge_heads(x):
            b, h, s, hd = x.shape
            return x.transpose(0, 2, 1, 3).reshape(b, s, h * hd)

        def global_latent_attn(x, wq, w_kv_down, w_k_up, w_v_up, wo):
            q = split_heads(x @ wq, H)
            latent = x @ w_kv_down
            k = split_heads(latent @ w_k_up, KVH)
            v = split_heads(latent @ w_v_up, KVH)
            q, k = (rope(q, BASE_G), rope(k, BASE_G))
            q, k = (qk_norm(q), qk_norm(k))
            k, v = (repeat_kv(k), repeat_kv(v))
            i = jnp.arange(x.shape[1])
            causal = i[:, None] >= i[None, :]
            return merge_heads(sdpa(q, k, v, causal)) @ wo

        def local_gqa_attn(x, wq, wk, wv, wo):
            q = split_heads(x @ wq, H)
            k = split_heads(x @ wk, KVH)
            v = split_heads(x @ wv, KVH)
            q, k = (rope(q, BASE_L), rope(k, BASE_L))
            q, k = (qk_norm(q), qk_norm(k))
            k, v = (repeat_kv(k), repeat_kv(v))
            i = jnp.arange(x.shape[1])
            diff = i[:, None] - i[None, :]
            mask = (diff >= 0) & (diff < WIN)
            return merge_heads(sdpa(q, k, v, mask)) @ wo
        x = hidden
        x = x + global_latent_attn(rmsnorm(x, norm1_w), g_wq, g_kv_down, g_k_up, g_v_up, g_wo)
        x = x + local_gqa_attn(rmsnorm(x, norm2_w), l_wq, l_wk, l_wv, l_wo)
        return x

    def _L0_ffn_ref(hidden_states, W1, b1, W2, b2):
        import jax, jax.numpy as jnp
        import numpy as np
        HIDDEN = 128
        INTER = 512
        h = jax.nn.relu(jnp.einsum('bsh,hi->bsi', hidden_states, W1) + b1)
        return jnp.einsum('bsi,ih->bsh', h, W2) + b2

    def _L1_attn_a_ref(x, Wq, bq, Wk, bk, Wv, bv, Wo, bo):
        import jax, jax.numpy as jnp
        import numpy as np
        DIM = 128
        NUM_HEADS = 16
        NUM_KV_HEADS = 2
        HEAD_DIM = DIM // NUM_HEADS
        REPEATS = NUM_HEADS // NUM_KV_HEADS
        WINDOW = 32
        HALF = WINDOW // 2
        BATCH, SEQ = (2, 256)
        b, s, _ = x.shape
        q = (x @ Wq + bq).reshape(b, s, NUM_HEADS, HEAD_DIM).transpose(0, 2, 1, 3)
        k = (x @ Wk + bk).reshape(b, s, NUM_KV_HEADS, HEAD_DIM).transpose(0, 2, 1, 3)
        v = (x @ Wv + bv).reshape(b, s, NUM_KV_HEADS, HEAD_DIM).transpose(0, 2, 1, 3)
        kp = jnp.pad(k, ((0, 0), (0, 0), (HALF, HALF), (0, 0)))
        vp = jnp.pad(v, ((0, 0), (0, 0), (HALF, HALF), (0, 0)))
        idx = jnp.arange(s)[:, None] + jnp.arange(WINDOW)[None, :]
        k_win = kp[:, :, idx]
        v_win = vp[:, :, idx]
        qg = q.reshape(b, NUM_KV_HEADS, REPEATS, s, HEAD_DIM)
        scores = jnp.einsum('bgrsd,bgswd->bgrsw', qg, k_win)
        probs = jax.nn.softmax(scores, axis=-1)
        out = jnp.einsum('bgrsw,bgswd->bgrsd', probs, v_win)
        out = out.reshape(b, NUM_HEADS, s, HEAD_DIM).transpose(0, 2, 1, 3).reshape(b, s, DIM)
        return out @ Wo + bo

    def _L1_attn_b_ref(x, Wq, Wk, Wv, Wo, head_scales, head_dirs):
        import jax, jax.numpy as jnp
        import numpy as np
        D_MODEL = 128
        N_HEADS = 8
        N_KV_HEADS = 4
        HEAD_DIM = D_MODEL // N_HEADS
        N_REP = N_HEADS // N_KV_HEADS
        WINDOW = 128
        SINKS = 4
        ROPE_BASE = 10000.0
        SCALE = 1.0 / np.sqrt(HEAD_DIM)

        def _trigram_dirs():
            t = np.array([[s0, s1, s2] for s0 in (1.0, -1.0) for s1 in (1.0, -1.0) for s2 in (1.0, -1.0)], dtype=np.float32)
            t = t / np.linalg.norm(t, axis=1, keepdims=True)
            return jnp.asarray(t[:N_HEADS])

        def _rope_tables(T):
            inv_freq = 1.0 / ROPE_BASE ** (jnp.arange(0, HEAD_DIM, 2, dtype=jnp.float32) / HEAD_DIM)
            freqs = jnp.arange(T, dtype=jnp.float32)[:, None] * inv_freq[None, :]
            return (jnp.cos(freqs), jnp.sin(freqs))

        def _apply_rope(t, cos, sin):
            t1, t2 = jnp.split(t, 2, axis=-1)
            c = cos[None, None, :, :]
            s = sin[None, None, :, :]
            return jnp.concatenate([t1 * c - t2 * s, t2 * c + t1 * s], axis=-1)
        B, T, C = x.shape
        q = (x @ Wq).reshape(B, T, N_HEADS, HEAD_DIM).transpose(0, 2, 1, 3)
        k = (x @ Wk).reshape(B, T, N_KV_HEADS, HEAD_DIM).transpose(0, 2, 1, 3)
        v = (x @ Wv).reshape(B, T, N_KV_HEADS, HEAD_DIM).transpose(0, 2, 1, 3)
        cos, sin = _rope_tables(T)
        q = _apply_rope(q, cos, sin)
        k = _apply_rope(k, cos, sin)
        k = jnp.repeat(k, N_REP, axis=1)
        v = jnp.repeat(v, N_REP, axis=1)
        scores = jnp.einsum('bhtd,bhsd->bhts', q, k) * SCALE
        qp = jnp.einsum('bhtd,hd->bht', q[..., :3], head_dirs)
        kp = jnp.einsum('bhsd,hd->bhs', k[..., :3], head_dirs)
        scores = scores + head_scales[None, :, None, None] * (qp[..., :, None] * kp[..., None, :])
        i = jnp.arange(T)[:, None]
        j = jnp.arange(T)[None, :]
        allowed = (j <= i) & ((j < SINKS) | (j >= i - WINDOW + 1))
        scores = jnp.where(allowed[None, None, :, :], scores, -jnp.inf)
        attn = jax.nn.softmax(scores, axis=-1)
        out = jnp.einsum('bhts,bhsd->bhtd', attn, v)
        out = out.transpose(0, 2, 1, 3).reshape(B, T, C)
        return out @ Wo

    def _L1_ffn_ref(x, gate_w, rms_w, W1, W2, W3):
        import jax, jax.numpy as jnp
        import numpy as np
        E, K = (8, 2)
        DM, DE = (128, 352)
        B, S = (1, 256)
        EPS = 1e-06

        def _rmsnorm(x, w):
            var = jnp.mean(jnp.square(x), axis=-1, keepdims=True)
            return x * jax.lax.rsqrt(var + EPS) * w
        y = _rmsnorm(x, rms_w)
        logits = jnp.einsum('bsd,ed->bse', y, gate_w)
        vals, idx = jax.lax.top_k(logits, K)
        w = jax.nn.softmax(vals, axis=-1)
        w_full = jnp.einsum('bsk,bske->bse', w, jax.nn.one_hot(idx, E, dtype=x.dtype))
        up = jnp.einsum('bsd,end->bsen', y, W1)
        gate = jnp.einsum('bsd,end->bsen', y, W2)
        h = jax.nn.silu(up) * gate
        out = jnp.einsum('bsen,emn->bsem', h, W3)
        comb = jnp.einsum('bsem,bse->bsm', out, w_full)
        return x + comb
    x = L0_attn_a_x
    x = x + _L0_attn_a_ref(_layernorm(x, axis=-1), L0_attn_a_w_att_val, L0_attn_a_wv_w, L0_attn_a_wv_b, L0_attn_a_out_w, L0_attn_a_out_b)
    x = x + _L0_ffn_ref(_layernorm(x, axis=-1), L0_ffn_W1, L0_ffn_b1, L0_ffn_W2, L0_ffn_b2)
    x = x + _L0_attn_b_ref(_layernorm(x, axis=-1), L0_attn_b_norm1_w, L0_attn_b_norm2_w, L0_attn_b_g_wq, L0_attn_b_g_kv_down, L0_attn_b_g_k_up, L0_attn_b_g_v_up, L0_attn_b_g_wo, L0_attn_b_l_wq, L0_attn_b_l_wk, L0_attn_b_l_wv, L0_attn_b_l_wo)
    x = x + _L0_ffn_ref(_layernorm(x, axis=-1), L0_ffn_W1, L0_ffn_b1, L0_ffn_W2, L0_ffn_b2)
    x = x + _L1_attn_a_ref(_layernorm(x, axis=-1), L1_attn_a_Wq, L1_attn_a_bq, L1_attn_a_Wk, L1_attn_a_bk, L1_attn_a_Wv, L1_attn_a_bv, L1_attn_a_Wo, L1_attn_a_bo)
    x = x + _L1_ffn_ref(_layernorm(x, axis=-1), L1_ffn_gate_w, L1_ffn_rms_w, L1_ffn_W1, L1_ffn_W2, L1_ffn_W3)
    x = x + _L1_attn_b_ref(_layernorm(x, axis=-1), L1_attn_b_Wq, L1_attn_b_Wk, L1_attn_b_Wv, L1_attn_b_Wo, L1_attn_b_head_scales, L1_attn_b_head_dirs)
    x = x + _L1_ffn_ref(_layernorm(x, axis=-1), L1_ffn_gate_w, L1_ffn_rms_w, L1_ffn_W1, L1_ffn_W2, L1_ffn_W3)
    return x

_drawn_inputs = setup_inputs


def setup_inputs(seed=0):
    import zlib

    import numpy as np

    out = dict(_drawn_inputs(seed))
    spreads = {'L0_attn_a_wv_b': (0.0, 0.1),
     'L0_attn_a_out_b': (0.0, 0.1),
     'L0_attn_b_norm1_w': (1.0, 0.6),
     'L0_attn_b_norm2_w': (1.0, 0.6),
     'L1_ffn_rms_w': (1.0, 0.6)}
    factors = {'L0_attn_b_g_wq': 8.0,
     'L0_attn_b_g_kv_down': 8.0,
     'L0_attn_b_g_k_up': 8.0,
     'L0_attn_b_g_v_up': 8.0,
     'L0_attn_b_g_wo': 8.0,
     'L0_attn_b_l_wq': 8.0,
     'L0_attn_b_l_wk': 8.0,
     'L0_attn_b_l_wv': 6.351,
     'L0_attn_b_l_wo': 5.929,
     'L0_ffn_b1': 3.809,
     'L1_attn_a_bq': 8.0,
     'L1_attn_a_bk': 64.0,
     'L1_attn_a_bv': 8.0,
     'L1_attn_a_bo': 8.0,
     'L1_attn_b_Wq': 8.0,
     'L1_attn_b_Wk': 8.0,
     'L1_attn_b_Wv': 8.0,
     'L1_attn_b_Wo': 8.0,
     'L1_attn_b_head_scales': 8.0,
     'L1_attn_b_head_dirs': 8.0,
     'L1_ffn_gate_w': 8.0,
     'L1_ffn_W1': 8.0,
     'L1_ffn_W2': 8.0,
     'L1_ffn_W3': 8.0}
    for name, (base, spread) in spreads.items():
        noise = np.random.default_rng([zlib.crc32(name.encode()), seed]).standard_normal(out[name].shape)
        drawn = base * np.exp(spread * noise) if base else spread * noise
        out[name] = jnp.asarray(drawn.astype(out[name].dtype))
    for name, factor in factors.items():
        out[name] = (out[name] * factor).astype(out[name].dtype)
    return out
```

```python
import concourse.bass as bass
from concourse import mybir
from contextlib import ExitStack

F32 = mybir.dt.float32
BF = mybir.dt.bfloat16
I32 = mybir.dt.int32
U32 = mybir.dt.uint32
ALU = mybir.AluOpType
ACT = mybir.ActivationFunctionType
AX = mybir.AxisListType

NB, T, E = 4, 1024, 128
NT = T // 128
NEXP, DE = 8, 352
RS8 = float(8.0) ** -0.5


class Queue:

    def __init__(self, sem):
        self.sem, self.n, self.items, self.seen = sem, 0, [], {}

    def waits(self, deps):
        need = {}
        todo = list(deps)
        while todo:
            t = todo.pop()
            if t is None:
                continue
            if isinstance(t, list):
                todo.extend(t)
                continue
            sem, v = t
            if self.seen.get(sem.name, 0) < v:
                self.seen[sem.name] = v
                need[sem.name] = (sem, v)
        return list(need.values())

    def __call__(self, fn, *deps):
        self.n += 1
        self.items.append((self.waits(deps), fn, self.sem, 1))
        return (self.sem, self.n)

    def silent(self, fn, *deps):
        self.items.append((self.waits(deps), fn, None, 0))

    def play(self, eng):
        for waits, fn, sem, by in self.items:
            for s, v in waits:
                eng.wait_ge(s, v)
            if fn is None:
                continue
            ins = fn()
            if sem is not None:
                ins.then_inc(sem, by)


class Ring:

    def __init__(self, bufs):
        self.bufs, self.free, self.at = bufs, [[] for _ in bufs], 0

    def take(self):
        i = self.at % len(self.bufs)
        self.at += 1
        assert self.free[i] is not None, "a buffer is taken before its last users are known"
        deps, self.free[i] = self.free[i], None
        return i, self.bufs[i], deps

    def give(self, i, *toks):
        self.free[i] = list(toks)


def weave(main, side, lead=0, rate=2):
    n = 0
    for _ in main:
        n += 1
        if n > lead:
            for _ in range(rate):
                if next(side, 0) == 0:
                    break
    for _ in side:
        pass


def chain(*gens):
    for g in gens:
        yield from g


def program(nc, d, out, scr_q, scr_k, scr_m):
    ctx = ExitStack()
    with ctx:
        def sb(name, shape, dt=F32):
            return ctx.enter_context(nc.sbuf_tensor(name, shape, dt))

        def sem(name):
            return ctx.enter_context(nc.semaphore(name))

        pe, act, dve, pool, sp = (Queue(sem(n)) for n in ("s_pe", "s_act", "s_dve", "s_pool", "s_sp"))
        dma_sems = [sem(f"s_dma{i}") for i in range(48)]
        dma_count = [0] * 48
        dma_at = [0]
        stores = []

        def dma(q, eng, o, i, *deps, store=False):
            k = dma_at[0] % 48
            dma_at[0] += 1
            s = dma_sems[k]
            last = (s, 16 * dma_count[k]) if dma_count[k] else None
            dma_count[k] += 1
            w = q.waits([list(deps), last])
            q.items.append((w, lambda: eng.dma_start(o, i), s, 16))
            tok = (s, 16 * dma_count[k])
            if store:
                stores.append(tok)
            return tok

        mm = nc.tensor.matmul

        PS = ctx.enter_context(nc.psum_tensor("PS", [128, 8, 512], F32))
        RA = Ring([PS[:, 0, :], PS[:, 1, :]])
        RB = Ring([PS[:, 2:4, :], PS[:, 4:6, :]])
        RC = RA
        RP = Ring([PS[:, 6, :], PS[:, 7, :]])

        X = sb("X", [128, NB, NT, 128])
        xtok = [[] for _ in range(NB)]
        XN = sb("XN", [128, NT, 128])
        XNr = Ring([XN])
        XTr = Ring([sb(f"XT{i}", [128, T + 32]) for i in range(2)])
        HBr = Ring([sb(f"HB{i}", [128, NT, 128]) for i in range(2)])
        QK = sb("QK", [128, NT, 192])
        QKr = Ring([QK])
        T1 = sb("T1", [128, 1536])
        T2 = sb("T2", [128, 768])
        Tr = Ring([(T1, T2)])
        PQr = Ring([sb("PQ0", [128, 3, T + 32], BF)])
        VAr = Ring([sb(f"VA{i}", [128, 9, 16 * 9]) for i in range(2)])
        Or = Ring([sb(f"O{i}", [128, NT, 128]) for i in range(2)])
        QOr = Ring([sb(f"QO{i}", [128, 4, T], BF) for i in range(2)])
        KOr = Ring([sb(f"KO{i}", [128, 4, T + 32], BF) for i in range(2)])
        PTr = Ring([sb(f"PT{i}", [128, 8, 512]) for i in range(2)])
        SGr = Ring([sb(f"SG{i}", [128, 512]) for i in range(2)])
        MSr = Ring([sb(f"MS{i}", [128, 32, 2]) for i in range(2)])
        MTr = Ring([(sb("MTa", [128, 32]), sb("MTb", [32, 128]), sb("MTc", [32, 128]), sb("MTd", [32, 3, 128], BF))])
        RCPr = Ring([sb(f"RCP{i}", [128, 8]) for i in range(2)])
        NW = sb("NW", [128, 4, 160])
        NWr = Ring([NW])
        STr = Ring([(sb("ST0", [128, 8, 6]), sb("MV0", [128, 8, 2]))])
        SQ = Ring([sb("SQ0", [128, 160])])

        load_toks = []

        def const(name, dt=F32):
            a = d[name]
            t = sb("c_" + name, list(a.shape), dt)
            load_toks.append(dma(sp, nc.sync, t[tuple(slice(None) for _ in a.shape)], a))
            return t

        for b in range(NB):
            xtok[b].append(dma(act, nc.scalar, X[:, b, :, :], d["x"][b].rearrange("(n p) e -> p n e", p=128)))
        ident = const("ident")
        identb = const("identb", BF)
        wbd = const("wbd")
        wvT = const("wvT")
        outT = const("outT")
        rows = const("rows")
        ones = const("ones")
        fW1 = const("fW1")
        fb1 = const("fb1")
        fW2 = const("fW2")
        n1w = const("n1w")
        gq = const("gq")
        gdown = const("gdown")
        gup = const("gup")
        gwo = const("gwo")
        lqkv = const("lqkv")
        lwo = const("lwo")
        aWq = const("aWq")
        aWkv = const("aWkv")
        aWo = const("aWo")
        abq = const("abq")
        abk = const("abk")
        abv = const("abv")
        bqkv = const("bqkv")
        bWo = const("bWo")
        bE = const("bE")
        bS = const("bS")
        cg = const("cg")
        cb = const("cb")
        mC = const("mC", BF)
        mL = const("mL", BF)
        mA = const("mA", BF)
        mB = const("mB", BF)
        mB0 = const("mB0", BF)
        mBt = const("mBt", BF)
        mBt1 = const("mBt1", BF)
        iota8 = const("iota8")
        gateT = const("gateT")
        rmsw = const("rmsw")
        mW1 = const("mW1")
        mW2 = const("mW2")
        mW3 = sb("mW3s", [128, NEXP, 3, 128])
        L = load_toks

        def newton(v, n, src, mul, add, *deps):
            h, y, t, w = NW[:, 0, 0:n], NW[:, 1, 0:n], NW[:, 2, 0:n], NW[:, 3, 0:n]
            a = dve(lambda: nc.vector.tensor_scalar(w, src, mul, add, ALU.mult, ALU.add), *deps)
            b = dve(lambda: nc.vector.tensor_scalar(t.bitcast(I32), w.bitcast(I32), 1, None, ALU.logical_shift_right), a)
            a = dve(lambda: nc.vector.tensor_scalar(h, w, -0.5, None, ALU.mult), a)
            b = dve(lambda: nc.vector.tensor_scalar(y.bitcast(I32), t.bitcast(I32), -1.0, float(0x5f3759df), ALU.mult, ALU.add), b)
            for _ in range(3):
                b = dve(lambda: nc.vector.tensor_tensor(t, y, y, ALU.mult), b)
                b = dve(lambda: nc.vector.tensor_tensor(t, t, h, ALU.mult), b)
                b = dve(lambda: nc.vector.scalar_tensor_tensor(y, t, 1.5, y, ALU.add, ALU.mult), b)
            return y, b

        def layernorm(src, dst, deps):
            si, (st, mv), sd = STr.take()
            a = None
            for i in range(NT):
                a = dve(lambda i=i: nc.vector.bn_stats(st[:, i, :], src[:, i, :]), deps, sd)
            yield
            for i in range(NT):
                b = dve(lambda i=i: nc.vector.bn_aggr(mv[:, i, :], st[:, i, :]), a)
            ni, _, nd = NWr.take()
            y, b = newton(None, NT, mv[:, :, 1], 1.0, 1e-5, b, nd)
            yield
            for i in range(NT):
                c = dve(lambda i=i: nc.vector.tensor_scalar(dst[:, i, :], src[:, i, :], mv[:, i, 0:1], y[:, i:i + 1],
                                                            ALU.subtract, ALU.mult), b)
            STr.give(si, c)
            NWr.give(ni, c)
            return c

        def rms(src, dst, deps, ddeps):
            qi, ss, qd = SQ.take()
            ji, junk, jd = SGr.take()
            for i in range(NT):
                a = act(lambda i=i: nc.scalar.activation(junk[:, 0:128], src[:, i, :], ACT.Square, accum_out=ss[:, i:i + 1]),
                        deps, qd, jd)
                jd = a
            SGr.give(ji, a)
            yield
            ni, _, nd = NWr.take()
            y, b = newton(None, NT, ss[:, 0:NT], 1.0 / 128, 1e-6, a, nd)
            yield
            for i in range(NT):
                c = dve(lambda i=i: nc.vector.tensor_scalar(dst[:, i, :], src[:, i, :], y[:, i:i + 1], None, ALU.mult),
                        b, ddeps)
            SQ.give(qi, c)
            NWr.give(ni, c)
            return c

        def transposed(src, w, dst, off, deps, ddeps, scale=None):
            toks = []
            for g in range(2):
                ci, ps, cd = RC.take()
                for i in range(4):
                    t = pe(lambda g=g, i=i, ps=ps: nc.tensor.transpose(ps[0:w, 128 * i:128 * i + 128], src(4 * g + i), ident[:, :]),
                           deps, cd, L)
                o = dst[0:w, off + 512 * g:off + 512 * g + 512]
                if scale is None:
                    e = act(lambda o=o, ps=ps: nc.scalar.activation(o, ps[0:w, :], ACT.Copy), t, ddeps)
                else:
                    e = act(lambda o=o, ps=ps: nc.scalar.activation(o, ps[0:w, :], ACT.Copy, scale=scale), t, ddeps, L)
                RC.give(ci, e)
                toks.append(e)
                yield
            return toks

        def split(x, r, n, q, deps, store_to, reuse):
            pi, p, pd = PQr.take()
            ri, (rr, _), rd = Tr.take()
            a = dve(lambda: nc.vector.tensor_copy(p[0:r, 0, 0:n], x), deps, pd)
            b = pool(lambda: nc.gpsimd.tensor_tensor(rr[0:r, 0:n], x, p[0:r, 0, 0:n], ALU.subtract), a, rd)
            yield
            a = dve(lambda: nc.vector.tensor_copy(p[0:r, 1, 0:n], rr[0:r, 0:n]), b)
            c = pool(lambda: nc.gpsimd.tensor_tensor(p[0:r, 2, 0:n], rr[0:r, 0:n], p[0:r, 1, 0:n], ALU.subtract), a)
            yield
            s = dma(sp, nc.sync, store_to.rearrange("a r t -> r a t"), p[0:r, :, 0:n], c, reuse, store=True)
            PQr.give(pi, s)
            Tr.give(ri, c)
            return s, b

        def addrows(bank, first, r, deps):
            return pe.silent(lambda: mm(bank, ones[r:r + 1, :], rows[r:r + 1, :], start=True, stop=False,
                                        tile_position=(r, 0)), deps, L)

        SLOTQ, SLOTK = (0, 0, 1, 0, 1, 2), (0, 1, 0, 2, 1, 0)
        pv = []
        sq_free, sk_free, sm_free = [[], []], [[], []], [[], []]

        def load_unit(A, b, u, st):
            D, G = A["D"], A["group"]
            kv = max(1, 4 // G)
            kv0 = 4 * u // G
            qi, qo, qd = QOr.take()
            ki, ko, kd = KOr.take()
            kn = A["kn"]
            toks = []
            for s in range(6):
                toks.append(dma(sp, nc.sync, qo[D * s:D * s + D, :, :],
                                scr_q[b % 2, SLOTQ[s], 4 * D * u:4 * D * u + 4 * D, :].rearrange("(h d) t -> d h t", d=D),
                                st["qtok"][b], qd))
                toks.append(dma(sp, nc.sync, ko[D * s:D * s + D, 0:kv, 0:kn],
                                scr_k[b % 2, SLOTK[s], D * kv0:D * (kv0 + kv), 0:kn].rearrange("(h d) t -> d h t", d=D),
                                st["ktok"][b], kd))
            st["readers"][b].extend(toks)
            if A["max"]:
                toks.append(dma(sp, nc.sync, ko[6 * D:6 * D + 3, 0:kv, 0:kn], d["onesk"][:, 0:kv, 0:kn], kd))
            return dict(qi=qi, qo=qo, ki=ki, ko=ko, toks=toks, G=G, kv0=kv0, u=u, b=b, sreads=[])

        def maxima(A, U):
            D = A["D"]
            K = 6 * D
            qo, ko = U["qo"], U["ko"]
            mi, ms, md = MSr.take()
            last = []
            for h in range(4):
                kh = (4 * U["u"] + h) // U["G"] - U["kv0"]
                for tt in range(NT):
                    for piece in A["scores"](tt):
                        ai, ps, ad = RA.take()
                        n = 0
                        for (k0, kn, masks) in piece:
                            t = None
                            pe.silent(lambda h=h, tt=tt, ps=ps, n=n, k0=k0, kn=kn, kh=kh, s=masks is None:
                                      mm(ps[:, n:n + kn], qo[0:K, h, 128 * tt:128 * tt + 128], ko[0:K, kh, k0:k0 + kn],
                                         start=True, stop=s), U["toks"], ad, L)
                            if masks is not None:
                                pe.silent(lambda ps=ps, n=n, kn=kn, m=masks:
                                          mm(ps[:, n:n + kn], identb[:, :], m, start=False, stop=True))
                            n += kn
                        it = pe.items[-1]
                        pe.n += 1
                        pe.items[-1] = (it[0], it[1], pe.sem, 1)
                        t = (pe.sem, pe.n)
                        j = A["scores"](tt).index(piece)
                        e = dve(lambda ps=ps, n=n, h=h, tt=tt, j=j:
                                nc.vector.tensor_reduce(ms[:, 8 * h + tt, j:j + 1], ps[:, 0:n], AX.X, ALU.max), t, md)
                        RA.give(ai, e)
                        U["sreads"] = [t]
                    yield
            ti, (ma, mb, mc, mp), td = MTr.take()
            if A["pieces"] == 2:
                e = dve(lambda: nc.vector.tensor_tensor(ma[:, :], ms[:, :, 0], ms[:, :, 1], ALU.max), e, td)
            else:
                e = dve(lambda: nc.vector.tensor_copy(ma[:, :], ms[:, :, 0]), e, td)
            MSr.give(mi, e)
            ci, ps, cd = RC.take()
            t = pe(lambda: nc.tensor.transpose(ps[0:32, 0:128], ma[:, :], ident[:, :]), e, cd, L)
            e = dve(lambda: nc.vector.tensor_scalar(mb[:, :], ps[0:32, 0:128], -1.0, None, ALU.mult), t)
            RC.give(ci, e)
            yield
            e = dve(lambda: nc.vector.tensor_copy(mp[:, 0, :], mb[:, :]), e)
            e = dve(lambda: nc.vector.tensor_tensor(mc[:, :], mb[:, :], mp[:, 0, :], ALU.subtract), e)
            e = dve(lambda: nc.vector.tensor_copy(mp[:, 1, :], mc[:, :]), e)
            e = dve(lambda: nc.vector.tensor_tensor(mp[:, 2, :], mc[:, :], mp[:, 1, :], ALU.subtract), e)
            par = A["mcount"][0] % 2
            A["mcount"][0] += 1
            s = dma(sp, nc.sync, scr_m[par].rearrange("a r t -> r a t"), mp[:, :, :], e, sm_free[par], store=True)
            MTr.give(ti, s)
            s2 = dma(sp, nc.sync, qo[K:K + 3, :, :].rearrange("a h t -> a (h t)"),
                     scr_m[par].rearrange("a r t -> a (r t)"), s)
            sm_free[par] = [s2]
            U["mtok"] = s2
            yield

        def attend(A, U, va, vtok, O, otoks, odeps):
            D = A["D"]
            K = 6 * D + (3 if A["max"] else 0)
            qo, ko = U["qo"], U["ko"]
            deps = [U["toks"], U.get("mtok")]
            for h in range(4):
                head = 4 * U["u"] + h
                kh = head // U["G"] - U["kv0"]
                vh = head // U["G"]
                for chunk in A["chunks"]:
                    pi, pt, pd = PTr.take()
                    etoks = []
                    lastst = None
                    for group in chunk["groups"]:
                        bi, ps, bd = RB.take()
                        psf = ps.rearrange("p a b -> p (a b)")
                        for (k0, kn, t0, tn, at, masks) in group["blocks"]:
                            q = pe.silent
                            ops = [lambda psf=psf, at=at, kn=kn, tn=tn, t0=t0, k0=k0, h=h, kh=kh, s=not masks:
                                   mm(psf[0:kn, at:at + tn], ko[0:K, kh, k0:k0 + kn], qo[0:K, h, t0:t0 + tn],
                                      start=True, stop=s)]
                            for (mo, mn, m) in masks:
                                ops.append(lambda psf=psf, at=at, kn=kn, mo=mo, mn=mn, m=m:
                                           mm(psf[0:kn, at + mo:at + mo + mn], identb[0:kn, 0:kn], m,
                                              start=False, stop=True))
                            for o in ops[:-1]:
                                pe.silent(o, deps, bd, L)
                            lastst = pe(ops[-1], deps, bd, L)
                        ex = []
                        for (r, so, po) in group["exps"]:
                            src = so(psf)
                            dst = po(pt)
                            ex.append(act(lambda src=src, dst=dst: nc.scalar.activation(dst, src, ACT.Exp, scale=A["scale"]),
                                          lastst, pd))
                        RB.give(bi, ex[-1])
                        etoks.append(ex[-1])
                        take = -(-len(pv) // max(1, group.get("left", 1)))
                        for _ in range(min(take, len(pv))):
                            pv.pop(0)()
                        yield
                    while pv:
                        pv.pop(0)()
                    U["last"] = lastst
                    hold = {}

                    def product(i, tt, parts, n, h=h, head=head, vh=vh, pt=pt, pi=pi, etoks=etoks, hold=hold,
                                chunk=chunk):
                        if i == 0:
                            hold["c"] = RP.take()
                        ci, po, cd = hold["c"]
                        for j, (src, kn, m0, mn, vt) in enumerate(parts):
                            f = pe if j == len(parts) - 1 else pe.silent
                            t = f(lambda src=src, kn=kn, m0=m0, mn=mn, vt=vt, j=j, i=i, po=po:
                                  mm(po[m0:m0 + mn, 32 * i:32 * i + D + 1], src(pt)[0:kn, :],
                                     va[0:kn, vt, vh * (D + 1):(vh + 1) * (D + 1)],
                                     start=(j == 0), stop=(j == len(parts) - 1),
                                     skip_group_check=any(x[3] != 128 for x in parts)), etoks, cd, vtok)
                        if i == n - 1:
                            PTr.give(pi, t)
                            v = po[:, 0:32 * n].rearrange("p (a b) -> p a b", b=32)
                            ri, rc, rd = RCPr.take()
                            e = dve(lambda: nc.vector.reciprocal(rc[:, 0:n], v[:, :, D]), t, rd)
                            tt0 = chunk["tts"][0][0]
                            e = dve(lambda: nc.vector.tensor_tensor(
                                O[:, tt0:tt0 + n, head * D:head * D + D], v[:, :, 0:D],
                                rc[:, 0:n].unsqueeze(2).broadcast_to([128, n, D]), ALU.mult), e, odeps)
                            RCPr.give(ri, e)
                            RP.give(ci, e)
                            otoks.append(e)

                    n = len(chunk["tts"])
                    for i, (tt, parts) in enumerate(chunk["tts"]):
                        pv.append(lambda i=i, tt=tt, parts=parts, n=n, f=product: f(i, tt, parts, n))

        def flush():
            while pv:
                pv.pop(0)()

        def project(A, b, O, oi, otoks, target, tdeps, wtoks):
            xi, xt, xd = XTr.take()
            t = yield from transposed(lambda i: O[:, i, :], 128, xt, 0, otoks, xd)
            Or.give(oi, (pe.sem, pe.n))
            for g in range(2):
                ai, ps, ad = RA.take()
                if A["bias"] is not None:
                    addrows(ps, True, A["bias"], ad)
                for i in range(4):
                    p = pe(lambda ps=ps, i=i, g=g: mm(ps[:, 128 * i:128 * i + 128],
                                                      xt[:, 512 * g + 128 * i:512 * g + 128 * i + 128], A["wo"][:, :],
                                                      start=A["bias"] is None, stop=A["bias"] is None or i == 3), t, ad, L)
                e = dve(lambda ps=ps, g=g: nc.vector.tensor_tensor(
                    target[:, 4 * g:4 * g + 4, :], target[:, 4 * g:4 * g + 4, :],
                    ps.rearrange("p (a b) -> p a b", b=128), ALU.add), p, tdeps)
                RA.give(ai, e)
                wtoks.append(e)
                yield
            XTr.give(xi, p)

        def run_attention(A):
            st = dict(qtok={}, ktok={}, readers={b: [] for b in range(NB)})
            A["mcount"] = [0]
            NU = A["units"]
            V = {}
            Os = {}

            def prologue(b):
                if b >= 2:
                    sq_free[b % 2] = st["readers"][b - 2]
                yield from A["prologue"](b, st, V)

            units = [(b, u) for b in range(NB) for u in range(NU)]
            for _ in prologue(0):
                pass
            nxt = load_unit(A, 0, 0, st)
            if A["max"]:
                for _ in maxima(A, nxt):
                    pass
            tail = []
            for n, (b, u) in enumerate(units):
                U = nxt
                sides = list(tail)
                tail = []
                if u == 0:
                    oi, O, od = Or.take()
                    Os[b] = (oi, O, [], od)
                if n + 1 < len(units):
                    nb, nu = units[n + 1]
                    if nb == b:
                        nxt = load_unit(A, nb, nu, st)
                    else:
                        nxt = None
                pre = prologue(b + 1) if (b + 1 < NB and u == 0) else None
                if pre is not None:
                    sides.append(pre)
                if A["max"] and n + 1 < len(units) and nxt is not None:
                    sides.append(maxima(A, nxt))
                oi, O, ot, od = Os[b]
                va, vtok, vi = V[b]
                if n + 1 < len(units) and nxt is None:
                    if NU == 1:
                        for _ in chain(*sides):
                            pass
                        sides = []
                    nxt = load_unit(A, nb, nu, st)
                    if A["max"]:
                        sides.append(maxima(A, nxt))
                weave(attend(A, U, va, vtok, O, ot, od), chain(*sides), A["lead"], A["rate"])
                QOr.give(U["qi"], U["last"], U["sreads"])
                KOr.give(U["ki"], U["last"], U["sreads"])
                if u == NU - 1:
                    flush()
                    VAr.give(vi, (pe.sem, pe.n))
                    tail.append(A["finish"](b, O, oi, ot))
            for g in tail:
                for _ in g:
                    pass
            sq_free[0], sq_free[1] = st["readers"][NB - 2], st["readers"][NB - 1]

        def full_chunks():
            out = []
            for half in range(2):
                groups = []
                for i in range(4):
                    blocks = [(128 * (2 * i + j), 128, 512 * half, 512, 512 * j, []) for j in range(2)]
                    groups.append(dict(blocks=blocks, left=4 - i, exps=[
                        (128, lambda ps: ps, lambda pt, i=i: pt[:, 2 * i:2 * i + 2, :].rearrange("p a b -> p (a b)"))]))
                tts = [(4 * half + i, [(lambda pt, s=s, i=i: pt[:, s, 128 * i:128 * i + 128], 128, 0, 128, s)
                                       for s in range(NT)]) for i in range(4)]
                out.append(dict(groups=groups, tts=tts))
            return out

        def causal_chunks():
            out = []
            for half in range(2):
                groups = []
                npair = 2 if half == 0 else 4
                for i in range(npair):
                    blocks, exps = [], []
                    for j in range(2):
                        s = 2 * i + j
                        off = max(0, 128 * s - 512 * half)
                        masks = [(0, 128, mC[:, :])] if 128 * s >= 512 * half else []
                        if masks:
                            blocks.append((128 * s, 128, 512 * half + off, 128, 512 * j + off, masks))
                            if off < 384:
                                blocks.append((128 * s, 128, 512 * half + off + 128, 384 - off, 512 * j + off + 128, []))
                        else:
                            blocks.append((128 * s, 128, 512 * half, 512, 512 * j, []))
                        exps.append((128, lambda ps, j=j, off=off: ps[:, 512 * j + off:512 * j + 512],
                                     lambda pt, s=s, off=off: pt[:, s, off:512]))
                    if all(not b[5] for b in blocks):
                        exps = [(128, lambda ps: ps, lambda pt, i=i: pt[:, 2 * i:2 * i + 2, :].rearrange("p a b -> p (a b)"))]
                    groups.append(dict(blocks=blocks, left=npair - i, exps=exps))
                tts = [(4 * half + i, [(lambda pt, s=s, i=i: pt[:, s, 128 * i:128 * i + 128], 128, 0, 128, s)
                                       for s in range(4 * half + i + 1)]) for i in range(4)]
                out.append(dict(groups=groups, tts=tts))
            return out

        def ptw(pt):
            return pt[:, :, :].rearrange("p a b -> p (a b)")

        def v3(ap, a, b, w, n):
            return ap[:, a:a + b * n].rearrange("p (n b) -> p n b", b=b)[:, :, 0:w]

        def local_chunks():
            groups = []
            for g in range(2):
                blocks, exps = [], []
                for j in range(4):
                    s = 4 * g + j
                    w = min(160, T - 128 * s)
                    blocks.append((128 * s, 128, 128 * s, w, 256 * j, [(0, w, mL[:, 0:w])]))
                n = 4 if g == 0 else 3
                exps.append((128, lambda ps, n=n: v3(ps, 0, 256, 160, n), lambda pt, g=g, n=n: v3(ptw(pt), 1024 * g, 256, 160, n)))
                if g == 1:
                    exps.append((128, lambda ps: ps[:, 768:896], lambda pt: ptw(pt)[:, 1792:1920]))
                groups.append(dict(blocks=blocks, left=2 - g, exps=exps))
            tts = []
            for tt in range(NT):
                parts = [(lambda pt, tt=tt: ptw(pt)[:, 256 * tt:256 * tt + 128], 128, 0, 128, tt)]
                if tt:
                    parts.append((lambda pt, tt=tt: ptw(pt)[:, 256 * tt - 128:256 * tt - 96], 128, 0, 32, tt - 1))
                tts.append((tt, parts))
            return [dict(groups=groups, tts=tts)]

        def padded_chunks():
            groups = []
            for g in range(2):
                blocks = []
                for j in range(4):
                    s = 4 * g + j
                    t0, w, c0 = (128 * s - 32, 160, 0) if s else (0, 128, 32)
                    blocks.append((128 * s, 128, t0, w, 256 * j + c0, [(0, w, mA[:, c0:c0 + w])]))
                if g == 0:
                    exps = [(128, lambda ps: ps[:, 32:160], lambda pt: ptw(pt)[:, 32:160]),
                            (128, lambda ps: v3(ps, 256, 256, 160, 3), lambda pt: v3(ptw(pt), 256, 256, 160, 3))]
                else:
                    exps = [(128, lambda ps: v3(ps, 0, 256, 160, 4), lambda pt: v3(ptw(pt), 1024, 256, 160, 4))]
                groups.append(dict(blocks=blocks, left=3 - g, exps=exps))
            groups.append(dict(blocks=[(T, 32, T - 32, 32, 0, [(0, 32, mA[0:32, 0:32])])], left=1,
                               exps=[(32, lambda ps: ps[0:32, 0:32], lambda pt: ptw(pt)[0:32, 2048:2080])]))
            tts = []
            for tt in range(NT):
                tts.append((tt, [(lambda pt, tt=tt: ptw(pt)[:, 256 * tt + 32:256 * tt + 160], 128, 0, 128, tt),
                                 (lambda pt, tt=tt: ptw(pt)[:, 256 * tt + 256:256 * tt + 288], 32, 96, 32, tt + 1)]))
            return [dict(groups=groups, tts=tts)]

        def sink_chunks():
            groups = []
            for g in range(2):
                blocks = []
                for j in range(4):
                    s = 4 * g + j
                    w = min(256, T - 128 * s)
                    m = mB0 if s == 0 else mB
                    blocks.append((128 * s, 128, 128 * s, w, 256 * j, [(0, w, m[:, 0:w])]))
                n = 1024 if g == 0 else 896
                groups.append(dict(blocks=blocks, left=3 - g, exps=[
                    (128, lambda ps, n=n: ps[:, 0:n], lambda pt, n=n, g=g: ptw(pt)[:, 1024 * g:1024 * g + n])]))
            groups.append(dict(blocks=[(0, 4, 256, 512, 0, []), (0, 4, 768, 256, 512, [])], left=1,
                               exps=[(4, lambda ps: ps[0:4, 0:768], lambda pt: ptw(pt)[0:4, 2048:2816])]))
            tts = []
            for tt in range(NT):
                parts = [(lambda pt, tt=tt: ptw(pt)[:, 256 * tt:256 * tt + 128], 128, 0, 128, tt)]
                if tt:
                    parts.append((lambda pt, tt=tt: ptw(pt)[:, 256 * tt - 128:256 * tt], 128, 0, 128, tt - 1))
                if tt >= 2:
                    parts.append((lambda pt, tt=tt: ptw(pt)[:, 2048 + 128 * (tt - 2):2048 + 128 * (tt - 1)], 4, 0, 128, 0))
                tts.append((tt, parts))
            return [dict(groups=groups, tts=tts)]

        def scores_full(tt):
            return [[(0, 512, None)], [(512, 512, None)]]

        def scores_padded(tt):
            return [[(128 * tt, 160, mL[:, :])]]

        def scores_sink(tt):
            if tt == 0:
                return [[(0, 128, mBt[:, 128:256])]]
            if tt == 1:
                return [[(0, 256, mBt1[:, :])]]
            return [[(128 * tt - 128, 256, mBt[:, :]), (0, 4, None)]]

        def ones_columns(D, nh):
            toks = []
            for i, va in enumerate(VAr.bufs):
                v = va[:, :, 0:nh * (D + 1)].rearrange("p n (h c) -> p n h c", c=D + 1)
                t = None
                for n in range(9):
                    t = pool(lambda v=v, n=n: nc.gpsimd.memset(v[:, n, :, D:D + 1], 1.0), VAr.free[i])
                VAr.free[i] = [t]

        def va_view(va, D, nh, n0, n):
            return va[:, n0:n0 + n, 0:nh * (D + 1)].rearrange("p n (h c) -> p n h c", c=D + 1)

        def stage1_prologue(b, st, V):
            ni, xn, nd = XNr.take()
            c = yield from layernorm(X[:, b, :, :], xn, [xtok[b], nd])
            xi, xt, xd = XTr.take()
            t = yield from transposed(lambda i: xn[:, i, :], 128, xt, 0, c, xd)
            XNr.give(ni, (pe.sem, pe.n))
            st["ktok"][b], kr = yield from split(xt[:, 0:T], 128, T, None, t, scr_k[b % 2, :, :, 0:T], sq_free[b % 2])
            qi, qf, qd = HBr.take()
            qff = qf[:, :, :].rearrange("p a b -> p (a b)")
            es = []
            for g in range(2):
                ci, ps, cd = RC.take()
                p = pe(lambda g=g, ps=ps: mm(ps, wbd[:, :], xt[:, 512 * g:512 * g + 512], start=True, stop=True), t, cd, L)
                e = act(lambda g=g, ps=ps: nc.scalar.activation(qff[:, 512 * g:512 * g + 512], ps, ACT.Copy), p, qd)
                RC.give(ci, e)
                es.append(e)
                yield
            st["qtok"][b], qr = yield from split(qff, 128, T, None, es, scr_q[b % 2], sq_free[b % 2])
            HBr.give(qi, qr)
            vi, va, vd = VAr.take()
            vt = []
            for g in range(2):
                ci, ps, cd = RC.take()
                addrows(ps, True, 0, cd)
                for i in range(4):
                    p = pe(lambda g=g, i=i, ps=ps: mm(ps[:, 128 * i:128 * i + 128],
                                                      xt[:, 512 * g + 128 * i:512 * g + 128 * i + 128], wvT[:, :],
                                                      start=False, stop=(i == 3)), t, cd, L)
                for i in range(4):
                    e = dve(lambda g=g, i=i, ps=ps: nc.vector.tensor_copy(
                        va_view(va, 8, 16, 4 * g + i, 1)[:, 0, :, 0:8],
                        ps[:, 128 * i:128 * i + 128].rearrange("p (h d) -> p h d", d=8)), p, vd)
                RC.give(ci, e)
                vt.append(e)
                yield
            XTr.give(xi, p, kr)
            V[b] = (va, vt, vi)

        def finish_into_x(A):
            def finish(b, O, oi, ot):
                w = []
                yield from project(A, b, O, oi, ot, X[:, b, :, :], xtok[b], w)
                xtok[b] = w
            return finish

        ones_columns(8, 16)
        A1 = dict(D=8, group=1, kn=T, max=True, pieces=2, scores=scores_full, scale=RS8, chunks=full_chunks(),
                  units=4, wo=outT, bias=32, prologue=stage1_prologue, lead=8, rate=2)
        A1["finish"] = finish_into_x(A1)
        run_attention(A1)

        def ffn():
            pend = []
            for b in range(NB):
                ni, xn, nd = XNr.take()
                for _ in (g := layernorm_run(X[:, b, :, :], xn, [xtok[b], nd])):
                    pass
                c = g_out[0]
                xi, xt, xd = XTr.take()
                tg = run(transposed(lambda i: xn[:, i, :], 128, xt, 0, c, xd))
                XNr.give(ni, (pe.sem, pe.n))
                for g in range(2):
                    hi, hT, hd = PTr.take()
                    hs = []
                    for c4 in range(4):
                        ai, ps, ad = RA.take()
                        p = pe(lambda c4=c4, g=g, ps=ps, xt=xt: mm(ps, fW1[:, 128 * c4:128 * c4 + 128], xt[:, 512 * g:512 * g + 512],
                                                                   start=True, stop=True), tg, ad, L)
                        e = act(lambda c4=c4, ps=ps, hT=hT: nc.scalar.activation(hT[:, c4, :], ps, ACT.Relu, bias=fb1[:, c4:c4 + 1]),
                                p, hd, L)
                        RA.give(ai, e)
                        hs.append(e)
                    while pend:
                        pend.pop(0)()

                    def down(b=b, g=g, hi=hi, hT=hT, hs=hs):
                        ci, ps, cd = RP.take()
                        addrows(ps, True, 64, cd)
                        for i in range(4):
                            for c4 in range(4):
                                f = pe if (c4 == 3) else pe.silent
                                p = f(lambda c4=c4, i=i, ps=ps: mm(ps[:, 128 * i:128 * i + 128], hT[:, c4, 128 * i:128 * i + 128],
                                                                   fW2[:, c4, :], start=False, stop=(c4 == 3 and i == 3)), hs, cd, L)
                        PTr.give(hi, p)
                        e = dve(lambda: nc.vector.tensor_tensor(X[:, b, 4 * g:4 * g + 4, :], X[:, b, 4 * g:4 * g + 4, :],
                                                                ps.rearrange("p (a b) -> p a b", b=128), ALU.add), p)
                        RP.give(ci, e)
                        xtok[b] = [xtok[b], e]
                    pend.append(down)
                XTr.give(xi, p)
            while pend:
                pend.pop(0)()

        g_out = [None]

        def layernorm_run(*a):
            g_out[0] = yield from layernorm(*a)

        def run(gen):
            while True:
                try:
                    next(gen)
                except StopIteration as s:
                    return s.value

        ffn()

        def rope_norm(nh, D, b, interleaved, tab, norm, qi_tok, w):
            ti, (t1, t2), td = Tr.take()
            hd = D // 2
            n3 = [128, NT, nh, hd]
            v = QK[:, :, 0:nh * D].rearrange("p n (h c) -> p n h c", c=D)
            if interleaved:
                ve = v.rearrange("p n h (c two) -> p n h c two", two=2)
                xe, xo = ve[:, :, :, :, 0], ve[:, :, :, :, 1]
            else:
                xe, xo = v[:, :, :, 0:hd], v[:, :, :, hd:D]
            co = tab[:, 0, :, :].unsqueeze(2)
            si = tab[:, 1, :, :].unsqueeze(2)
            w1 = t1[:, 0:NT * nh * hd].rearrange("p (n h c) -> p n h c", n=NT, c=hd)
            w2 = t2[:, 0:NT * nh * hd].rearrange("p (n h c) -> p n h c", n=NT, c=hd)
            m = NT * nh * hd
            assert m <= 768
            u1 = t1[:, 768:768 + m].rearrange("p (n h c) -> p n h c", n=NT, c=hd)
            bc = [128, nh, hd]
            toks = []
            for i in range(NT):
                cb_, sb_ = co[:, i, :, :].broadcast_to(bc), si[:, i, :, :].broadcast_to(bc)
                a = pool(lambda i=i, cb_=cb_: nc.gpsimd.tensor_tensor(w1[:, i], xe[:, i], cb_, ALU.mult), qi_tok, td, L)
                e = dve(lambda i=i, sb_=sb_: nc.vector.tensor_tensor(w2[:, i], xo[:, i], sb_, ALU.mult), qi_tok, td, L)
                a2 = pool(lambda i=i, sb_=sb_: nc.gpsimd.tensor_tensor(u1[:, i], xe[:, i], sb_, ALU.mult), qi_tok, td, L)
                e2 = dve(lambda i=i, cb_=cb_: nc.vector.tensor_tensor(xo[:, i], xo[:, i], cb_, ALU.mult), e)
                toks.append((a2, e, e2))
                if i % 4 == 3:
                    yield
            for i in range(NT):
                a2, e, e2 = toks[i]
                f1 = dve(lambda i=i: nc.vector.tensor_tensor(xe[:, i], w1[:, i], w2[:, i], ALU.subtract), a2, e)
                f2 = dve(lambda i=i: nc.vector.tensor_tensor(xo[:, i], u1[:, i], xo[:, i], ALU.add), a2, e2)
                if i % 4 == 3:
                    yield
            if not norm:
                Tr.give(ti, f2)
                return [f1, f2]
            k = NT * nh
            qv = QK[:, :, 0:nh * D]
            e = dve(lambda: nc.vector.tensor_tensor(t1[:, 0:k * D].rearrange("p (n c) -> p n c", n=NT), qv, qv, ALU.mult), f1, f2)
            si_, ss, sd = SQ.take()
            e = dve(lambda: nc.vector.tensor_reduce(ss[:, 0:k], t1[:, 0:k * D].rearrange("p (k c) -> p k c", c=D), AX.X, ALU.add),
                    e, sd)
            Tr.give(ti, e)
            ni, _, nd = NWr.take()
            y, e = newton(None, k, ss[:, 0:k], 1.0 / D, 1e-6, e, nd)
            yield
            yv = y.rearrange("p (n h) -> p n h", n=NT)
            for i in range(NT):
                e2 = dve(lambda i=i: nc.vector.tensor_tensor(v[:, i], v[:, i], yv[:, i, :].unsqueeze(2).broadcast_to([128, nh, D]),
                                                             ALU.mult), e)
            NWr.give(ni, e2)
            SQ.give(si_, e2)
            return [e2]

        Hs = {}

        def b_common(b, st, wsel, V):
            hb = Hs[b]
            ni, xn, nd = XNr.take()
            c = yield from rms(hb["buf"], xn, hb["toks"], nd)
            xi, xt, xd = XTr.take()
            t = yield from transposed(lambda i: xn[:, i, :], 128, xt, 0, c, xd, scale=n1w[:, wsel:wsel + 1])
            XNr.give(ni, (pe.sem, pe.n))
            return xi, xt, t

        def b_operands(b, st, toks, e_deps):
            fi, ff, fd = XTr.take()
            t = yield from transposed(lambda i: QK[:, i, 0:128], 128, ff, 0, toks, fd)
            st["qtok"][b], r = yield from split(ff[:, 0:T], 128, T, None, t, scr_q[b % 2], sq_free[b % 2])
            XTr.give(fi, r)
            return None

        def k_operand(b, st, toks, c0, w):
            fi, ff, fd = XTr.take()
            t = yield from transposed(lambda i: QK[:, i, c0:c0 + w], w, ff, 0, toks, fd)
            st["ktok"][b], r = yield from split(ff[0:w, 0:T], w, T, None, t, scr_k[b % 2, :, 0:w, 0:T], sq_free[b % 2])
            XTr.give(fi, r)

        def global_prologue(b, st, V):
            hi, hb, hd = HBr2[b]
            c = yield from layernorm(X[:, b, :, :], hb, [xtok[b], hd])
            Hs[b] = dict(buf=hb, toks=[c])
            xi, xt, t = yield from b_common(b, st, 0, V)
            qi, _, qd = QKr.take()
            qe = []
            for g in range(2):
                ci, ps, cd = RC.take()
                for i in range(4):
                    p = pe(lambda g=g, i=i, ps=ps: mm(ps[:, 128 * i:128 * i + 128],
                                                      xt[:, 512 * g + 128 * i:512 * g + 128 * i + 128], gq[:, :],
                                                      start=True, stop=True), t, cd, L)
                e = act(lambda g=g, ps=ps: nc.scalar.activation(QK[:, 4 * g:4 * g + 4, 0:128],
                                                                ps.rearrange("p (a b) -> p a b", b=128), ACT.Copy), p, qd)
                RC.give(ci, e)
                qe.append(e)
                yield
            li, (lt, _), ld = Tr.take()
            le = []
            for g in range(2):
                ci, ps, cd = RC.take()
                p = pe(lambda g=g, ps=ps: mm(ps[0:32, :], gdown[:, :], xt[:, 512 * g:512 * g + 512], start=True, stop=True), t, cd, L)
                e = act(lambda g=g, ps=ps: nc.scalar.activation(lt[0:32, 512 * g:512 * g + 512], ps[0:32, :], ACT.Copy), p, ld)
                RC.give(ci, e)
                le.append(e)
            XTr.give(xi, p)
            yield
            vi, va, vd = VAr.take()
            ci, ps, cd = RC.take()
            for i in range(8):
                p = pe(lambda i=i, ps=ps: mm(ps[:, 64 * i:64 * i + 64], lt[0:32, 128 * i:128 * i + 128], gup[:, :],
                                             start=True, stop=True), le, cd, L)
            Tr.give(li, p)
            psv = ps.rearrange("p (a b) -> p a b", b=64)
            e = dve(lambda: nc.vector.tensor_copy(QK[:, :, 128:160], psv[:, :, 0:32]), p, qd)
            qe.append(e)
            for i in range(8):
                e = dve(lambda i=i: nc.vector.tensor_copy(va_view(va, 8, 4, i, 1)[:, 0, :, 0:8],
                                                          psv[:, i, 32:64].rearrange("p (h c) -> p h c", c=8)), p, vd)
            RC.give(ci, e)
            V[b] = (va, [e], vi)
            yield
            rt = yield from rope_norm(20, 8, b, True, cgg, True, qe, None)
            yield from b_operands(b, st, rt, None)
            yield from k_operand(b, st, rt, 128, 32)
            QKr.give(qi, (pe.sem, pe.n))

        def wide_qkv(b, xt, xi, t, W, n, qw, vw, D, qd, V):
            vi, va, vd = VAr.take()
            qe, ve = [], []
            for g in range(4):
                ci, ps, cd = RC.take()
                for i in range(2):
                    tt = 2 * g + i
                    p = pe(lambda tt=tt, i=i, ps=ps: mm(ps[:, 256 * i:256 * i + n], xt[:, 128 * tt:128 * tt + 128], W[:, :],
                                                        start=True, stop=True), t, cd, L)
                pv3 = ps.rearrange("p (a b) -> p a b", b=256)
                e = dve(lambda g=g, pv3=pv3: nc.vector.tensor_copy(QK[:, 2 * g:2 * g + 2, 0:qw], pv3[:, :, 0:qw]), p, qd)
                qe.append(e)
                for i in range(2):
                    e = dve(lambda g=g, i=i, pv3=pv3: nc.vector.tensor_copy(
                        va_view(va, D, vw // D, 2 * g + i, 1)[:, 0, :, 0:D],
                        pv3[:, i, qw:qw + vw].rearrange("p (h c) -> p h c", c=D)), p, vd)
                RC.give(ci, e)
                ve.append(e)
                yield
            XTr.give(xi, p)
            V[b] = (va, ve, vi)
            return qe

        def local_prologue(b, st, V):
            xi, xt, t = yield from b_common(b, st, 1, V)
            qi, _, qd = QKr.take()
            qe = yield from wide_qkv(b, xt, xi, t, lqkv, 192, 160, 32, 8, qd, V)
            rt = yield from rope_norm(20, 8, b, True, cgl, True, qe, None)
            yield from b_operands(b, st, rt, None)
            yield from k_operand(b, st, rt, 128, 32)
            QKr.give(qi, (pe.sem, pe.n))

        cgg = cg[:, 0]
        cgl = cg[:, 1]
        H4 = mW3[:, :, :, :].rearrange("p a b c -> p (a b c)")[:, 0:2048].rearrange("p (a b c) -> p a b c", a=2, b=NT)
        HBr2 = {b: (b, HBr.bufs[b], HBr.free[b]) if b < 2 else (b, H4[:, b - 2], []) for b in range(NB)}
        HBr.free = [None, None]

        def finish_h(A):
            def finish(b, O, oi, ot):
                w = []
                yield from project(A, b, O, oi, ot, Hs[b]["buf"], Hs[b]["toks"], w)
                Hs[b]["toks"] = w
            return finish

        def finish_hx(A):
            def finish(b, O, oi, ot):
                w = []
                yield from project(A, b, O, oi, ot, Hs[b]["buf"], Hs[b]["toks"], w)
                e = pool(lambda b=b: nc.gpsimd.tensor_tensor(X[:, b, :, :], X[:, b, :, :], Hs[b]["buf"][:, :, :], ALU.add),
                         w, xtok[b])
                xtok[b] = [e]
                if b < 2:
                    HBr.free[b] = [e]
            return finish

        ones_columns(8, 4)
        A3 = dict(D=8, group=4, kn=T, max=False, scale=RS8, chunks=causal_chunks(), units=4, wo=gwo, bias=None,
                  prologue=global_prologue, lead=0, rate=1)
        A3["finish"] = finish_h(A3)
        run_attention(A3)
        A4 = dict(D=8, group=4, kn=T, max=False, scale=RS8, chunks=local_chunks(), units=4, wo=lwo, bias=None,
                  prologue=local_prologue, lead=0, rate=2)
        A4["finish"] = finish_hx(A4)
        run_attention(A4)
        L3 = dma(sp, nc.sync, mW3[:, :, :, :], d["mW3"], xtok[2], xtok[3])
        ffn()

        def padded_prologue(b, st, V):
            ni, xn, nd = XNr.take()
            c = yield from layernorm(X[:, b, :, :], xn, [xtok[b], nd])
            xi, xt, xd = XTr.take()
            z = pool(lambda xt=xt: nc.gpsimd.memset(xt[:, 0:16], 0.0), xd)
            z = pool(lambda xt=xt: nc.gpsimd.memset(xt[:, T + 16:T + 32], 0.0), xd)
            t = yield from transposed(lambda i: xn[:, i, :], 128, xt, 16, c, xd)
            XNr.give(ni, (pe.sem, pe.n))
            qi, qf, qd = HBr.take()
            qff = qf[:, :, :].rearrange("p a b -> p (a b)")
            fi, ff, fd = XTr.take()
            es, ks = [], []
            ks.append(pool(lambda ff=ff: nc.gpsimd.memset(ff[0:16, 0:16], 0.0), fd))
            ks.append(pool(lambda ff=ff: nc.gpsimd.memset(ff[0:16, T + 16:T + 32], 0.0), fd))
            for g in range(2):
                ci, ps, cd = RC.take()
                p = pe(lambda g=g, ps=ps: mm(ps, aWq[:, :], xt[:, 16 + 512 * g:16 + 512 * g + 512], start=True, stop=True), t, cd, L)
                e = act(lambda g=g, ps=ps: nc.scalar.activation(qff[:, 512 * g:512 * g + 512], ps, ACT.Identity,
                                                                bias=abq[:, 0:1]), p, qd, L)
                RC.give(ci, e)
                es.append(e)
                ci, ps, cd = RC.take()
                p = pe(lambda g=g, ps=ps: mm(ps[0:16, :], aWkv[:, 0:16], xt[:, 16 + 512 * g:16 + 512 * g + 512],
                                             start=True, stop=True), t, cd, L)
                e = act(lambda g=g, ps=ps, ff=ff: nc.scalar.activation(ff[0:16, 16 + 512 * g:16 + 512 * g + 512], ps[0:16, :],
                                                                       ACT.Identity, bias=abk[:, 0:1]), p, fd, L)
                RC.give(ci, e)
                ks.append(e)
                yield
            vi, va, vd = VAr.take()
            ci, ps, cd = RC.take()
            for j in range(9):
                n = 128 if j < 8 else 32
                pe.silent(lambda j=j, n=n, ps=ps: mm(ps[0:n, 16 * j:16 * j + 16], xt[:, 128 * j:128 * j + n], aWkv[:, 16:32],
                                                     start=True, stop=False), t, z, cd, L)
                valid = abv[:, 0:128] if j == 0 else abv[:, 128:160] if j == 8 else ones[0:1, :]
                p = pe(lambda j=j, n=n, ps=ps, valid=valid: mm(ps[0:n, 16 * j:16 * j + 16], valid, abv[:, 160:176],
                                                               start=False, stop=True))
            psv = ps[:, 0:144].rearrange("p (n h c) -> p n h c", n=9, c=8)
            for j in range(9):
                n = 128 if j < 8 else 32
                e = dve(lambda j=j, n=n: nc.vector.tensor_copy(va_view(va, 8, 2, j, 1)[0:n, 0, :, 0:8], psv[0:n, j]), p, vd)
            RC.give(ci, e)
            XTr.give(xi, p)
            V[b] = (va, [e], vi)
            yield
            st["ktok"][b], r = yield from split(ff[0:16, 0:T + 32], 16, T + 32, None, ks, scr_k[b % 2, :, 0:16, 0:T + 32],
                                                sq_free[b % 2])
            XTr.give(fi, r)
            st["qtok"][b], r = yield from split(qff, 128, T, None, es, scr_q[b % 2], sq_free[b % 2])
            HBr.give(qi, r)

        ones_columns(8, 2)
        A5 = dict(D=8, group=8, kn=T + 32, max=True, pieces=1, scores=scores_padded, scale=1.0, chunks=padded_chunks(),
                  units=4, wo=aWo, bias=96, prologue=padded_prologue, lead=2, rate=5)
        A5["finish"] = finish_into_x(A5)
        run_attention(A5)

        wfr = Ring([sb("WF0", [128, 8, 8])])
        LG = sb("LG", [128, 8, 8])
        MX = sb("MX", [128, 8, 8])
        IX = sb("IX", [128, 8, 8], U32)
        IXF = sb("IXF", [128, 8, 2])
        WW = sb("WW", [128, 3, 8])
        OH = sb("OH", [128, 8, 8])

        def moe(store):
            for b in range(NB):
                hi_, hb, hd = HBr.take()
                c = run(layernorm(X[:, b, :, :], hb, [xtok[b], hd]))
                ni, xn, nd = XNr.take()
                c2 = run(rms(hb, xn, c, nd))
                xi, xt, xd = XTr.take()
                t = run(transposed(lambda i: xn[:, i, :], 128, xt, 0, c2, xd, scale=rmsw[:, 0:1]))
                XNr.give(ni, (pe.sem, pe.n))
                a = pool(lambda b=b, hb=hb: nc.gpsimd.tensor_tensor(X[:, b, :, :], X[:, b, :, :], hb[:, :, :], ALU.add), c, xtok[b])
                HBr.give(hi_, a, c2)
                xa = [a]
                ci, ps, cd = RC.take()
                for i in range(NT):
                    p = pe(lambda i=i, ps=ps, xt=xt: mm(ps[:, 8 * i:8 * i + 8], xt[:, 128 * i:128 * i + 128], gateT[:, :],
                                                        start=True, stop=True), t, cd, L)
                wi, WF, wd = wfr.take()
                e = dve(lambda ps=ps: nc.vector.tensor_copy(LG[:, :, :].rearrange("p a b -> p (a b)"), ps[:, 0:64]), p, wd)
                RC.give(ci, e)
                for i in range(NT):
                    e1 = dve(lambda i=i: nc.vector.max(MX[:, i, :], LG[:, i, :]), e)
                for i in range(NT):
                    e2 = dve(lambda i=i: nc.vector.max_index(IX[:, i, :], MX[:, i, :], LG[:, i, :]), e1)
                e2 = dve(lambda: nc.vector.tensor_copy(IXF[:, :, :], IX[:, :, 0:2]), e2)
                e1 = dve(lambda: nc.vector.tensor_tensor(WW[:, 0, :], MX[:, :, 1], MX[:, :, 0], ALU.subtract), e1)
                a1 = act(lambda: nc.scalar.activation(WW[:, 1, :], WW[:, 0, :], ACT.Exp), e1)
                e1 = dve(lambda: nc.vector.tensor_scalar(WW[:, 0, :], WW[:, 1, :], 1.0, None, ALU.add), a1)
                e1 = dve(lambda: nc.vector.reciprocal(WW[:, 2, :], WW[:, 0, :]), e1)
                e1 = dve(lambda: nc.vector.tensor_tensor(WW[:, 1, :], WW[:, 1, :], WW[:, 2, :], ALU.mult), e1)
                bc = [128, 8, 8]
                io = iota8[:, :].unsqueeze(1)
                e3 = dve(lambda WF=WF: nc.vector.tensor_tensor(WF[:, :, :], io.broadcast_to(bc), IXF[:, :, 0:1].broadcast_to(bc),
                                                               ALU.is_equal), e2, L)
                e3 = dve(lambda WF=WF: nc.vector.tensor_tensor(WF[:, :, :], WF[:, :, :],
                                                               WW[:, 2, :].unsqueeze(2).broadcast_to(bc), ALU.mult), e1, e3)
                e4 = dve(lambda: nc.vector.tensor_tensor(OH[:, :, :], io.broadcast_to(bc), IXF[:, :, 1:2].broadcast_to(bc),
                                                         ALU.is_equal), e2)
                e4 = dve(lambda: nc.vector.tensor_tensor(OH[:, :, :], OH[:, :, :],
                                                         WW[:, 1, :].unsqueeze(2).broadcast_to(bc), ALU.mult), e1, e4)
                wt = dve(lambda WF=WF: nc.vector.tensor_tensor(WF[:, :, :], WF[:, :, :], OH[:, :, :], ALU.add), e3, e4)
                pend = []
                fin = []
                for g in range(2):
                    prev = [None] * 4
                    for ex in range(NEXP):
                        hi, hT, hdd = PTr.take()
                        hs = []
                        for c in range(3):
                            n = min(128, DE - 128 * c)
                            o = DE * ex + 128 * c
                            bi, pb, bd = RB.take()
                            pe.silent(lambda o=o, n=n, pb=pb, g=g, xt=xt: mm(pb[0:n, 0, :], mW1[:, o:o + n], xt[:, 512 * g:512 * g + 512],
                                                                             start=True, stop=True), t, bd, L)
                            pe.n += 1
                            it = pe.items[-1]
                            pe.items[-1] = (it[0], it[1], pe.sem, 1)
                            pu = (pe.sem, pe.n)
                            pg = pe(lambda o=o, n=n, pb=pb, g=g, xt=xt: mm(pb[0:n, 1, :], mW2[:, o:o + n], xt[:, 512 * g:512 * g + 512],
                                                                           start=True, stop=True))
                            si, sg, sd = SGr.take()
                            a = act(lambda n=n, pb=pb, sg=sg: nc.scalar.activation(sg[0:n, :], pb[0:n, 0, :], ACT.Silu), pu, sd)
                            e = dve(lambda n=n, pb=pb, sg=sg, hT=hT, c=c: nc.vector.tensor_tensor(hT[0:n, c, :], pb[0:n, 1, :], sg[0:n, :], ALU.mult),
                                    a, pg, hdd)
                            SGr.give(si, e)
                            RB.give(bi, e)
                            hs.append(e)
                        while pend:
                            pend.pop(0)()

                        def down(b=b, g=g, ex=ex, hi=hi, hT=hT, hs=hs, prev=prev):
                            ci, ps, cd = RP.take()
                            for i in range(4):
                                for c in range(3):
                                    n = min(128, DE - 128 * c)
                                    f = pe if c == 2 else pe.silent
                                    p = f(lambda c=c, i=i, n=n, ps=ps: mm(ps[:, 128 * i:128 * i + 128], hT[0:n, c, 128 * i:128 * i + 128],
                                                                          mW3[0:n, ex, c, :], start=(c == 0), stop=(c == 2)), hs, cd, L, L3)
                            PTr.give(hi, p)
                            for i in range(4):
                                tt = 4 * g + i
                                e = dve(lambda i=i, tt=tt, ps=ps, WF=WF: nc.vector.scalar_tensor_tensor(
                                    X[:, b, tt, :], ps[:, 128 * i:128 * i + 128], WF[:, tt, ex:ex + 1], X[:, b, tt, :],
                                    ALU.mult, ALU.add), p, wt, xa, prev[i])
                                prev[i] = e
                            RP.give(ci, e)
                            fin.append(e)
                        pend.append(down)
                while pend:
                    pend.pop(0)()
                XTr.give(xi, (pe.sem, pe.n))
                wfr.give(wi, fin[-1])
                xtok[b] = [fin[-1]]
                if store:
                    dma(sp, nc.sync, out[b].rearrange("(n p) e -> p n e", p=128), X[:, b, :, :], xtok[b], store=True)

        moe(False)

        MBD = sb("MBD", [128, 128])
        BE2 = sb("BE2", [8, 128])
        e = dve(lambda: nc.vector.tensor_scalar(BE2[:, :], bE[:, :], bS[:, 0:1], None, ALU.mult), L)
        ci, ps, cd = RC.take()
        p = pe(lambda ps=ps: mm(ps[:, 0:128], bE[:, :], BE2[:, :], start=True, stop=True), e, cd, L)
        mbd = dve(lambda ps=ps: nc.vector.scalar_tensor_tensor(MBD[:, :], ident[:, :], 0.25, ps[:, 0:128], ALU.mult, ALU.add), p)
        RC.give(ci, mbd)

        def sink_prologue(b, st, V):
            ni, xn, nd = XNr.take()
            c = yield from layernorm(X[:, b, :, :], xn, [xtok[b], nd])
            xi, xt, xd = XTr.take()
            t = yield from transposed(lambda i: xn[:, i, :], 128, xt, 0, c, xd)
            XNr.give(ni, (pe.sem, pe.n))
            qi, _, qd = QKr.take()
            qe = yield from wide_qkv(b, xt, xi, t, bqkv, 256, 192, 64, 16, qd, V)
            rt = yield from rope_norm(12, 16, b, False, cb, False, qe, None)
            yield from k_operand(b, st, rt, 128, 64)
            fi, ff, fd = XTr.take()
            t = yield from transposed(lambda i: QK[:, i, 0:128], 128, ff, 0, rt, fd)
            QKr.give(qi, (pe.sem, pe.n))
            gi, qf, gd = HBr.take()
            qff = qf[:, :, :].rearrange("p a b -> p (a b)")
            es = []
            for g in range(2):
                ci, ps, cd = RC.take()
                p = pe(lambda g=g, ps=ps: mm(ps, MBD[:, :], ff[:, 512 * g:512 * g + 512], start=True, stop=True), t, cd, mbd)
                e = act(lambda g=g, ps=ps: nc.scalar.activation(qff[:, 512 * g:512 * g + 512], ps, ACT.Copy), p, gd)
                RC.give(ci, e)
                es.append(e)
                yield
            XTr.give(fi, p)
            st["qtok"][b], r = yield from split(qff, 128, T, None, es, scr_q[b % 2], sq_free[b % 2])
            HBr.give(gi, r)

        ones_columns(16, 4)
        A7 = dict(D=16, group=2, kn=T, max=True, pieces=1, scores=scores_sink, scale=1.0, chunks=sink_chunks(),
                  units=2, wo=bWo, bias=None, prologue=sink_prologue, lead=2, rate=5)
        A7["finish"] = finish_into_x(A7)
        run_attention(A7)
        moe(True)

        sp.items.append((sp.waits(stores), None, None, 0))

        with nc.Block() as block:
            @block.sync
            def _(eng):
                sp.play(eng)

            @block.tensor
            def _(eng):
                pe.play(eng)

            @block.vector
            def _(eng):
                dve.play(eng)

            @block.scalar
            def _(eng):
                act.play(eng)

            @block.gpsimd
            def _(eng):
                pool.play(eng)


def tables():
    import numpy as np

    def bf16(x):
        return (np.ascontiguousarray(x, np.float32).view(np.uint32) >> 16).astype(np.uint16)

    neg = np.float32(-1e30)
    i = np.arange(128)[:, None]

    def mask(allowed):
        return bf16(np.where(allowed, np.float32(0), neg))

    def rope(base, hd):
        inv = (np.float32(1.0) / np.float32(base) ** (np.arange(0, hd, 2, dtype=np.float32) / np.float32(hd))).astype(np.float32)
        f = np.arange(T, dtype=np.float32)[:, None] * inv[None, :]
        cs = np.stack([np.cos(f), np.sin(f)]).astype(np.float32)
        return np.ascontiguousarray(cs.reshape(2, NT, 128, hd // 2).transpose(2, 0, 1, 3))

    c160, c256 = np.arange(160)[None, :], np.arange(256)[None, :]
    c = {
        "ident": np.eye(128, dtype=np.float32), "identb": bf16(np.eye(128)),
        "ones": np.ones((128, 128), np.float32),
        "onesk": bf16(np.ones((3, 4, T + 32))),
        "mC": mask(np.arange(128)[None, :] >= i),
        "mL": mask((c160 - i >= 0) & (c160 - i < 32)),
        "mA": mask((i + 32 - c160 >= 0) & (i + 32 - c160 <= 31)),
        "mB": mask((c256 - i >= 0) & (c256 - i <= 127)),
        "mB0": mask((c256 - i >= 0) & ((c256 - i <= 127) | (i < 4))),
        "mBt": mask((i + 128 - c256 >= 0) & (i + 128 - c256 <= 127)),
        "mBt1": mask((i + 128 - c256 >= 0) & ((i + 128 - c256 <= 127) | (c256 < 4))),
        "cg": np.ascontiguousarray(np.stack([rope(1000000.0, 8), rope(10000.0, 8)], axis=1)),
        "cb": rope(10000.0, 16),
        "iota8": np.broadcast_to(np.arange(8, dtype=np.float32), (128, 8)).copy(),
    }
    return c


def laid_out(a):
    import numpy as np

    g = {k: np.asarray(v) for k, v in a.items()}
    f = np.float32
    o = {"x": g["L0_attn_a_x"]}
    wbd = np.zeros((128, 128), f)
    for h in range(16):
        wbd[8 * h:8 * h + 8, 8 * h:8 * h + 8] = g["L0_attn_a_w_att_val"][h]
    o["wbd"] = wbd
    o["wvT"] = g["L0_attn_a_wv_w"].T
    o["outT"] = g["L0_attn_a_out_w"].T
    rows = np.zeros((128, 512), f)
    for r, n in ((0, "L0_attn_a_wv_b"), (32, "L0_attn_a_out_b"), (64, "L0_ffn_b2"), (96, "L1_attn_a_bo")):
        for i in range(4):
            rows[r, 128 * i:128 * i + 128] = g[n]
    o["rows"] = rows
    o["fW1"] = g["L0_ffn_W1"]
    o["fb1"] = g["L0_ffn_b1"].reshape(4, 128).T
    o["fW2"] = g["L0_ffn_W2"].reshape(4, 128, 128).transpose(1, 0, 2)
    o["n1w"] = np.stack([g["L0_attn_b_norm1_w"], g["L0_attn_b_norm2_w"]], axis=1)
    o["gq"] = g["L0_attn_b_g_wq"]
    o["gdown"] = g["L0_attn_b_g_kv_down"]
    o["gup"] = np.concatenate([g["L0_attn_b_g_k_up"], g["L0_attn_b_g_v_up"]], axis=1)
    o["gwo"] = g["L0_attn_b_g_wo"]
    o["lqkv"] = np.concatenate([g["L0_attn_b_l_wq"], g["L0_attn_b_l_wk"], g["L0_attn_b_l_wv"]], axis=1)
    o["lwo"] = g["L0_attn_b_l_wo"]
    o["aWq"] = g["L1_attn_a_Wq"]
    o["aWkv"] = np.concatenate([g["L1_attn_a_Wk"], g["L1_attn_a_Wv"]], axis=1)
    o["aWo"] = g["L1_attn_a_Wo"]
    o["abq"] = g["L1_attn_a_bq"][:, None]
    o["abk"] = g["L1_attn_a_bk"][:, None]
    abv = np.zeros((1, 176), f)
    abv[0, 16:144] = 1.0
    abv[0, 160:] = g["L1_attn_a_bv"]
    o["abv"] = abv
    o["bqkv"] = np.concatenate([g["L1_attn_b_Wq"], g["L1_attn_b_Wk"], g["L1_attn_b_Wv"]], axis=1)
    o["bWo"] = g["L1_attn_b_Wo"]
    bE = np.zeros((8, 128), f)
    for h in range(8):
        bE[h, 16 * h:16 * h + 3] = g["L1_attn_b_head_dirs"][h]
    o["bE"] = bE
    o["bS"] = g["L1_attn_b_head_scales"][:, None]
    o["gateT"] = g["L1_ffn_gate_w"].T
    o["rmsw"] = g["L1_ffn_rms_w"][:, None]
    o["mW1"] = g["L1_ffn_W1"].transpose(2, 0, 1).reshape(128, NEXP * DE)
    o["mW2"] = g["L1_ffn_W2"].transpose(2, 0, 1).reshape(128, NEXP * DE)
    w3 = np.zeros((128, NEXP, 3, 128), f)
    for e in range(NEXP):
        for c in range(3):
            n = min(128, DE - 128 * c)
            w3[0:n, e, c, :] = g["L1_ffn_W3"][e][:, 128 * c:128 * c + n].T
    o["mW3"] = w3
    return o


def kernel(**inputs):
    import numpy as _np
    import concourse.bacc as _bacc
    from concourse import mybir as _mybir
    from concourse.bass_utils import run_bass_kernel_spmd as _run

    nc = _bacc.Bacc("TRN2", target_bir_lowering=False, num_devices=1)
    arrays, args = {}, {}
    for name, a in {**laid_out(inputs), **tables()}.items():
        a = _np.ascontiguousarray(a)
        arrays[f"in_{name}"] = a
        args[name] = nc.dram_tensor(f"in_{name}", a.shape, _mybir.dt.from_np(a.dtype), kind="ExternalInput").ap()
        if a.dtype == _np.uint16:
            args[name] = args[name].bitcast(_mybir.dt.bfloat16)
    out = nc.dram_tensor("out_0", (NB, T, E), _mybir.dt.float32, kind="ExternalOutput").ap()
    scr_q = nc.dram_tensor("scr_q", (2, 3, 128, T), _mybir.dt.bfloat16, kind="Internal").ap()
    scr_k = nc.dram_tensor("scr_k", (2, 3, 128, T + 32), _mybir.dt.bfloat16, kind="Internal").ap()
    scr_m = nc.dram_tensor("scr_m", (2, 3, 32, 128), _mybir.dt.bfloat16, kind="Internal").ap()
    program(nc, args, out, scr_q, scr_k, scr_m)
    r = _run(nc, [arrays], core_ids=[0])
    return r.results[0]["out_0"]
```

```python
import concourse.bass as bass
from concourse import mybir
from contextlib import ExitStack

F32 = mybir.dt.float32
BF = mybir.dt.bfloat16
I32 = mybir.dt.int32
U32 = mybir.dt.uint32
ALU = mybir.AluOpType
ACT = mybir.ActivationFunctionType
AX = mybir.AxisListType

NB, T, E = 4, 1024, 128
NT = T // 128
NEXP, DE = 8, 352
RS8 = float(8.0) ** -0.5


class Queue:

    def __init__(self, sem):
        self.sem, self.n, self.items, self.seen = sem, 0, [], {}

    def waits(self, deps):
        need = {}
        todo = list(deps)
        while todo:
            t = todo.pop()
            if t is None:
                continue
            if isinstance(t, list):
                todo.extend(t)
                continue
            sem, v = t
            if self.seen.get(sem.name, 0) < v:
                self.seen[sem.name] = v
                need[sem.name] = (sem, v)
        return list(need.values())

    def __call__(self, fn, *deps):
        self.n += 1
        self.items.append((self.waits(deps), fn, self.sem, 1))
        return (self.sem, self.n)

    def silent(self, fn, *deps):
        self.items.append((self.waits(deps), fn, None, 0))

    def play(self, eng):
        for waits, fn, sem, by in self.items:
            for s, v in waits:
                eng.wait_ge(s, v)
            if fn is None:
                continue
            ins = fn()
            if sem is not None:
                ins.then_inc(sem, by)


class Ring:

    def __init__(self, bufs):
        self.bufs, self.free, self.at = bufs, [[] for _ in bufs], 0

    def take(self):
        i = self.at % len(self.bufs)
        self.at += 1
        assert self.free[i] is not None, "a buffer is taken before its last users are known"
        deps, self.free[i] = self.free[i], None
        return i, self.bufs[i], deps

    def give(self, i, *toks):
        self.free[i] = list(toks)


def weave(main, side, lead=0, rate=2):
    n = 0
    for _ in main:
        n += 1
        if n > lead:
            for _ in range(rate):
                if next(side, 0) == 0:
                    break
    for _ in side:
        pass


def chain(*gens):
    for g in gens:
        yield from g


def program(nc, d, out, scr_q, scr_k, scr_m):
    ctx = ExitStack()
    with ctx:
        def sb(name, shape, dt=F32):
            return ctx.enter_context(nc.sbuf_tensor(name, shape, dt))

        def sem(name):
            return ctx.enter_context(nc.semaphore(name))

        pe, act, dve, pool, sp = (Queue(sem(n)) for n in ("s_pe", "s_act", "s_dve", "s_pool", "s_sp"))
        dma_sems = [sem(f"s_dma{i}") for i in range(48)]
        dma_count = [0] * 48
        dma_at = [0]
        stores = []

        def dma(q, eng, o, i, *deps, store=False):
            k = dma_at[0] % 48
            dma_at[0] += 1
            s = dma_sems[k]
            last = (s, 16 * dma_count[k]) if dma_count[k] else None
            dma_count[k] += 1
            w = q.waits([list(deps), last])
            q.items.append((w, lambda: eng.dma_start(o, i), s, 16))
            tok = (s, 16 * dma_count[k])
            if store:
                stores.append(tok)
            return tok

        mm = nc.tensor.matmul

        PS = ctx.enter_context(nc.psum_tensor("PS", [128, 8, 512], F32))
        RA = Ring([PS[:, 0, :], PS[:, 1, :]])
        RB = Ring([PS[:, 2:4, :], PS[:, 4:6, :]])
        RC = RA
        RP = Ring([PS[:, 6, :], PS[:, 7, :]])

        X = sb("X", [128, NB, NT, 128])
        xtok = [[] for _ in range(NB)]
        XN = sb("XN", [128, NT, 128])
        XNr = Ring([XN])
        XTr = Ring([sb(f"XT{i}", [128, T + 32]) for i in range(2)])
        HBr = Ring([sb(f"HB{i}", [128, NT, 128]) for i in range(2)])
        QK = sb("QK", [128, NT, 192])
        QKr = Ring([QK])
        T1 = sb("T1", [128, 1536])
        T2 = sb("T2", [128, 768])
        Tr = Ring([(T1, T2)])
        PQr = Ring([sb("PQ0", [128, 3, T + 32], BF)])
        VAr = Ring([sb(f"VA{i}", [128, 9, 16 * 9]) for i in range(2)])
        Or = Ring([sb(f"O{i}", [128, NT, 128]) for i in range(2)])
        QOr = Ring([sb(f"QO{i}", [128, 4, T], BF) for i in range(2)])
        KOr = Ring([sb(f"KO{i}", [128, 4, T + 32], BF) for i in range(2)])
        PTr = Ring([sb(f"PT{i}", [128, 8, 512]) for i in range(2)])
        SGr = Ring([sb(f"SG{i}", [128, 512]) for i in range(2)])
        MSr = Ring([sb(f"MS{i}", [128, 32, 2]) for i in range(2)])
        MTr = Ring([(sb("MTa", [128, 32]), sb("MTb", [32, 128]), sb("MTc", [32, 128]), sb("MTd", [32, 3, 128], BF))])
        RCPr = Ring([sb(f"RCP{i}", [128, 16]) for i in range(2)])
        NW = sb("NW", [128, 4, 160])
        NWr = Ring([NW])
        OBr = Ring([sb("OB0", [128, 512])])
        RPT = Ring([b[:, 2 * j:2 * j + 2, :].rearrange("p a b -> p (a b)") for b in PTr.bufs for j in range(4)])
        Z = [dve(lambda i=i: nc.vector.memset(RP.bufs[i], 0.0)) for i in range(2)]

        def attention_buffers():
            for j in range(8):
                RPT.free[j] = list(PTr.free[j // 4])

        def hidden_buffers():
            for i in range(2):
                PTr.free[i] = [t for j in range(4) for t in RPT.free[4 * i + j]]

        STr = Ring([(sb("ST0", [128, 8, 6]), sb("MV0", [128, 8, 2]))])
        SQ = Ring([sb("SQ0", [128, 160])])

        load_toks = []

        def const(name, dt=F32):
            a = d[name]
            t = sb("c_" + name, list(a.shape), dt)
            load_toks.append(dma(sp, nc.sync, t[tuple(slice(None) for _ in a.shape)], a))
            return t

        for b in range(NB):
            xtok[b].append(dma(act, nc.scalar, X[:, b, :, :], d["x"][b].rearrange("(n p) e -> p n e", p=128)))
        ident = const("ident")
        identb = const("identb", BF)
        wbd = const("wbd")
        wvT = const("wvT")
        outT = const("outT")
        rows = const("rows")
        ones = const("ones")
        fW1 = const("fW1")
        fb1 = const("fb1")
        fW2 = const("fW2")
        n1w = const("n1w")
        gq = const("gq")
        gdown = const("gdown")
        gup = const("gup")
        gwo = const("gwo")
        lqkv = const("lqkv")
        lwo = const("lwo")
        aWq = const("aWq")
        aWkv = const("aWkv")
        aWo = const("aWo")
        abq = const("abq")
        abk = const("abk")
        abv = const("abv")
        bqkv = const("bqkv")
        bWo = const("bWo")
        bE = const("bE")
        bS = const("bS")
        cg = const("cg")
        cb = const("cb")
        mC = const("mC", BF)
        mL = const("mL", BF)
        mA = const("mA", BF)
        mB = const("mB", BF)
        mB0 = const("mB0", BF)
        mBt = const("mBt", BF)
        mBt1 = const("mBt1", BF)
        iota8 = const("iota8")
        gateT = const("gateT")
        rmsw = const("rmsw")
        mW1 = const("mW1")
        mW2 = const("mW2")
        mW3 = sb("mW3s", [128, NEXP, 3, 128])
        L = load_toks

        def newton(v, n, src, mul, add, *deps):
            h, y, t, w = NW[:, 0, 0:n], NW[:, 1, 0:n], NW[:, 2, 0:n], NW[:, 3, 0:n]
            a = dve(lambda: nc.vector.tensor_scalar(w, src, mul, add, ALU.mult, ALU.add), *deps)
            b = dve(lambda: nc.vector.tensor_scalar(t.bitcast(I32), w.bitcast(I32), 1, None, ALU.logical_shift_right), a)
            a = dve(lambda: nc.vector.tensor_scalar(h, w, -0.5, None, ALU.mult), a)
            b = dve(lambda: nc.vector.tensor_scalar(y.bitcast(I32), t.bitcast(I32), -1.0, float(0x5f3759df), ALU.mult, ALU.add), b)
            for _ in range(3):
                b = dve(lambda: nc.vector.tensor_tensor(t, y, y, ALU.mult), b)
                b = dve(lambda: nc.vector.tensor_tensor(t, t, h, ALU.mult), b)
                b = dve(lambda: nc.vector.scalar_tensor_tensor(y, t, 1.5, y, ALU.add, ALU.mult), b)
            return y, b

        def layernorm(src, dst, deps):
            si, (st, mv), sd = STr.take()
            a = None
            for i in range(NT):
                a = dve(lambda i=i: nc.vector.bn_stats(st[:, i, :], src[:, i, :]), deps, sd)
            yield
            for i in range(NT):
                b = dve(lambda i=i: nc.vector.bn_aggr(mv[:, i, :], st[:, i, :]), a)
            ni, _, nd = NWr.take()
            y, b = newton(None, NT, mv[:, :, 1], 1.0, 1e-5, b, nd)
            yield
            for i in range(NT):
                c = dve(lambda i=i: nc.vector.tensor_scalar(dst[:, i, :], src[:, i, :], mv[:, i, 0:1], y[:, i:i + 1],
                                                            ALU.subtract, ALU.mult), b)
            STr.give(si, c)
            NWr.give(ni, c)
            return c

        def rms(src, dst, deps, ddeps):
            qi, ss, qd = SQ.take()
            ji, junk, jd = SGr.take()
            for i in range(NT):
                a = act(lambda i=i: nc.scalar.activation(junk[:, 0:128], src[:, i, :], ACT.Square, accum_out=ss[:, i:i + 1]),
                        deps, qd, jd)
                jd = a
            SGr.give(ji, a)
            yield
            ni, _, nd = NWr.take()
            y, b = newton(None, NT, ss[:, 0:NT], 1.0 / 128, 1e-6, a, nd)
            yield
            for i in range(NT):
                c = dve(lambda i=i: nc.vector.tensor_scalar(dst[:, i, :], src[:, i, :], y[:, i:i + 1], None, ALU.mult),
                        b, ddeps)
            SQ.give(qi, c)
            NWr.give(ni, c)
            return c

        def transposed(src, w, dst, off, deps, ddeps, scale=None):
            toks = []
            for g in range(2):
                ci, ps, cd = RC.take()
                for i in range(4):
                    t = pe(lambda g=g, i=i, ps=ps: nc.tensor.transpose(ps[0:w, 128 * i:128 * i + 128], src(4 * g + i), ident[:, :]),
                           deps, cd, L)
                o = dst[0:w, off + 512 * g:off + 512 * g + 512]
                if scale is None:
                    e = act(lambda o=o, ps=ps: nc.scalar.activation(o, ps[0:w, :], ACT.Copy), t, ddeps)
                else:
                    e = act(lambda o=o, ps=ps: nc.scalar.activation(o, ps[0:w, :], ACT.Copy, scale=scale), t, ddeps, L)
                RC.give(ci, e)
                toks.append(e)
                yield
            return toks

        def split(x, r, n, q, deps, store_to, reuse):
            pi, p, pd = PQr.take()
            ri, (rr, _), rd = Tr.take()
            a = dve(lambda: nc.vector.tensor_copy(p[0:r, 0, 0:n], x), deps, pd)
            b = pool(lambda: nc.gpsimd.tensor_tensor(rr[0:r, 0:n], x, p[0:r, 0, 0:n], ALU.subtract), a, rd)
            yield
            a = dve(lambda: nc.vector.tensor_copy(p[0:r, 1, 0:n], rr[0:r, 0:n]), b)
            c = pool(lambda: nc.gpsimd.tensor_tensor(p[0:r, 2, 0:n], rr[0:r, 0:n], p[0:r, 1, 0:n], ALU.subtract), a)
            yield
            s = dma(sp, nc.sync, store_to.rearrange("a r t -> r a t"), p[0:r, :, 0:n], c, reuse, store=True)
            PQr.give(pi, s)
            Tr.give(ri, c)
            return s, b

        def addrows(bank, first, r, deps):
            return pe.silent(lambda: mm(bank, ones[r:r + 1, :], rows[r:r + 1, :], start=True, stop=False,
                                        tile_position=(r, 0)), deps, L)

        SLOTQ, SLOTK = (0, 0, 1, 0, 1, 2), (0, 1, 0, 2, 1, 0)
        pv = []
        sq_free, sk_free, sm_free = [[], []], [[], []], [[], []]

        def load_unit(A, b, u, st):
            D, G = A["D"], A["group"]
            kv = max(1, 4 // G)
            kv0 = 4 * u // G
            qi, qo, qd = QOr.take()
            ki, ko, kd = KOr.take()
            kn = A["kn"]
            toks = []
            for s in range(6):
                toks.append(dma(sp, nc.sync, qo[D * s:D * s + D, :, :],
                                scr_q[b % 2, SLOTQ[s], 4 * D * u:4 * D * u + 4 * D, :].rearrange("(h d) t -> d h t", d=D),
                                st["qtok"][b], qd))
                toks.append(dma(sp, nc.sync, ko[D * s:D * s + D, 0:kv, 0:kn],
                                scr_k[b % 2, SLOTK[s], D * kv0:D * (kv0 + kv), 0:kn].rearrange("(h d) t -> d h t", d=D),
                                st["ktok"][b], kd))
            st["readers"][b].extend(toks)
            if A["max"]:
                toks.append(dma(sp, nc.sync, ko[6 * D:6 * D + 3, 0:kv, 0:kn], d["onesk"][:, 0:kv, 0:kn], kd))
            return dict(qi=qi, qo=qo, ki=ki, ko=ko, toks=toks, G=G, kv0=kv0, u=u, b=b, sreads=[])

        def maxima(A, U):
            D = A["D"]
            K = 6 * D
            qo, ko = U["qo"], U["ko"]
            mi, ms, md = MSr.take()
            last = []
            for h in range(4):
                kh = (4 * U["u"] + h) // U["G"] - U["kv0"]
                for tt in range(NT):
                    for piece in A["scores"](tt):
                        ai, ps, ad = RA.take()
                        n = 0
                        for (k0, kn, masks) in piece:
                            t = None
                            pe.silent(lambda h=h, tt=tt, ps=ps, n=n, k0=k0, kn=kn, kh=kh, s=masks is None:
                                      mm(ps[:, n:n + kn], qo[0:K, h, 128 * tt:128 * tt + 128], ko[0:K, kh, k0:k0 + kn],
                                         start=True, stop=s), U["toks"], ad, L)
                            if masks is not None:
                                pe.silent(lambda ps=ps, n=n, kn=kn, m=masks:
                                          mm(ps[:, n:n + kn], identb[:, :], m, start=False, stop=True))
                            n += kn
                        it = pe.items[-1]
                        pe.n += 1
                        pe.items[-1] = (it[0], it[1], pe.sem, 1)
                        t = (pe.sem, pe.n)
                        j = A["scores"](tt).index(piece)
                        e = dve(lambda ps=ps, n=n, h=h, tt=tt, j=j:
                                nc.vector.tensor_reduce(ms[:, 8 * h + tt, j:j + 1], ps[:, 0:n], AX.X, ALU.max), t, md)
                        RA.give(ai, e)
                        U["sreads"] = [t]
                    yield
            ti, (ma, mb, mc, mp), td = MTr.take()
            if A["pieces"] == 2:
                e = dve(lambda: nc.vector.tensor_tensor(ma[:, :], ms[:, :, 0], ms[:, :, 1], ALU.max), e, td)
            else:
                e = dve(lambda: nc.vector.tensor_copy(ma[:, :], ms[:, :, 0]), e, td)
            MSr.give(mi, e)
            ci, ps, cd = RC.take()
            t = pe(lambda: nc.tensor.transpose(ps[0:32, 0:128], ma[:, :], ident[:, :]), e, cd, L)
            e = dve(lambda: nc.vector.tensor_scalar(mb[:, :], ps[0:32, 0:128], -1.0, None, ALU.mult), t)
            RC.give(ci, e)
            yield
            e = dve(lambda: nc.vector.tensor_copy(mp[:, 0, :], mb[:, :]), e)
            e = dve(lambda: nc.vector.tensor_tensor(mc[:, :], mb[:, :], mp[:, 0, :], ALU.subtract), e)
            e = dve(lambda: nc.vector.tensor_copy(mp[:, 1, :], mc[:, :]), e)
            e = dve(lambda: nc.vector.tensor_tensor(mp[:, 2, :], mc[:, :], mp[:, 1, :], ALU.subtract), e)
            par = A["mcount"][0] % 2
            A["mcount"][0] += 1
            s = dma(sp, nc.sync, scr_m[par].rearrange("a r t -> r a t"), mp[:, :, :], e, sm_free[par], store=True)
            MTr.give(ti, s)
            s2 = dma(sp, nc.sync, qo[K:K + 3, :, :].rearrange("a h t -> a (h t)"),
                     scr_m[par].rearrange("a r t -> a (r t)"), s)
            sm_free[par] = [s2]
            U["mtok"] = s2
            yield

        def attend(A, U, va, vtok, O, otoks, odeps):
            D = A["D"]
            K = 6 * D + (3 if A["max"] else 0)
            qo, ko = U["qo"], U["ko"]
            deps = [U["toks"], U.get("mtok")]
            for half in range(2):
                groups = A["chunks"][half]
                ri, po, rd = RP.take()
                for h in range(4):
                    head = 4 * U["u"] + h
                    kh = head // U["G"] - U["kv0"]
                    vh = head // U["G"]
                    for gi, group in enumerate(groups):
                        bi, ps, bd = RB.take()
                        psf = ps.rearrange("p a b -> p (a b)")
                        for (k0, kn, t0, tn, at, m, vt) in group["blocks"]:
                            mw = 0 if m is None else min(tn, m.shape[1])
                            if m is not None:
                                pe.silent(lambda psf=psf, at=at, kn=kn, mw=mw, t0=t0, k0=k0, h=h, kh=kh:
                                          mm(psf[0:kn, at:at + mw], ko[0:K, kh, k0:k0 + kn], qo[0:K, h, t0:t0 + mw],
                                             start=True, stop=False), deps, bd, L)
                                st_tok = pe(lambda psf=psf, at=at, kn=kn, mw=mw, m=m:
                                            mm(psf[0:kn, at:at + mw], identb[0:kn, 0:kn], m[0:kn, 0:mw],
                                               start=False, stop=True))
                            if mw < tn:
                                st_tok = pe(lambda psf=psf, at=at, kn=kn, tn=tn, mw=mw, t0=t0, k0=k0, h=h, kh=kh:
                                            mm(psf[0:kn, at + mw:at + tn], ko[0:K, kh, k0:k0 + kn],
                                               qo[0:K, h, t0 + mw:t0 + tn], start=True, stop=True), deps, bd, L)
                        pi, pt, pd = RPT.take()
                        for (r, a, b) in group["exps"]:
                            ex = act(lambda psf=psf, pt=pt, r=r, a=a, b=b:
                                     nc.scalar.activation(pt[0:r, a:b], psf[0:r, a:b], ACT.Exp, scale=A["scale"]), st_tok, pd)
                        RB.give(bi, ex)
                        U["last"] = st_tok
                        while pv:
                            pv.pop(0)()

                        def product(h=h, gi=gi, group=group, pt=pt, pi=pi, ex=ex, po=po, rd=rd, vh=vh, half=half,
                                    groups=groups, ri=ri):
                            r = 32 * h
                            for bi_, (k0, kn, t0, tn, at, m, vt) in enumerate(group["blocks"]):
                                c0 = t0 - 512 * half
                                first = gi == 0 and bi_ == 0
                                last = gi == len(groups) - 1 and bi_ == len(group["blocks"]) - 1
                                f = pe if bi_ == len(group["blocks"]) - 1 else pe.silent
                                t = f(lambda kn=kn, tn=tn, at=at, vt=vt, c0=c0, first=first, last=last:
                                      mm(po[r:r + D + 1, c0:c0 + tn], va[0:kn, vt, vh * (D + 1):(vh + 1) * (D + 1)],
                                         pt[0:kn, at:at + tn], start=first, stop=last, skip_group_check=not A["whole"],
                                         tile_position=(0, r)), ex, rd, vtok, Z)
                            RPT.give(pi, t)
                            if last and h == 3:
                                normalise(t, po, ri, half)

                        def normalise(t, po, ri, half):
                            oi_, ob, od_ = OBr.take()
                            e = act(lambda: nc.scalar.activation(ob[:, :], po, ACT.Copy), t, od_)
                            RP.give(ri, e)
                            pv.append(lambda: normalise2(e, ob, oi_, half))

                        def normalise2(e, ob, oi_, half):
                            ci, ps_, cd = RA.take()
                            for i in range(4):
                                t = pe(lambda i=i: nc.tensor.transpose(ps_[:, 128 * i:128 * i + 128],
                                                                       ob[:, 128 * i:128 * i + 128], ident[:, :]), e, cd, L)
                            OBr.give(oi_, t)
                            v = ps_.rearrange("p (a b) -> p a b", b=32)
                            wi, rc, wd = RCPr.take()
                            e = dve(lambda: nc.vector.reciprocal(rc[:, :], v[:, :, D]), t, wd)
                            v4 = ps_.rearrange("p (n g b) -> p n g b", n=4, b=32)
                            e = dve(lambda: nc.vector.tensor_tensor(
                                O[:, 4 * half:4 * half + 4, 4 * D * U["u"]:4 * D * U["u"] + 4 * D].rearrange(
                                    "p n (g c) -> p n g c", c=D),
                                v4[:, :, :, 0:D],
                                rc[:, :].rearrange("p (n g) -> p n g", g=4).unsqueeze(3).broadcast_to([128, 4, 4, D]),
                                ALU.mult), e, odeps)
                            RCPr.give(wi, e)
                            RA.give(ci, e)
                            otoks.append(e)

                        pv.append(product)
                        yield

        def flush():
            while pv:
                pv.pop(0)()

        def project(A, b, O, oi, otoks, target, tdeps, wtoks):
            xi, xt, xd = XTr.take()
            t = yield from transposed(lambda i: O[:, i, :], 128, xt, 0, otoks, xd)
            Or.give(oi, (pe.sem, pe.n))
            for g in range(2):
                ai, ps, ad = RA.take()
                if A["bias"] is not None:
                    addrows(ps, True, A["bias"], ad)
                for i in range(4):
                    p = pe(lambda ps=ps, i=i, g=g: mm(ps[:, 128 * i:128 * i + 128],
                                                      xt[:, 512 * g + 128 * i:512 * g + 128 * i + 128], A["wo"][:, :],
                                                      start=A["bias"] is None, stop=A["bias"] is None or i == 3), t, ad, L)
                e = dve(lambda ps=ps, g=g: nc.vector.tensor_tensor(
                    target[:, 4 * g:4 * g + 4, :], target[:, 4 * g:4 * g + 4, :],
                    ps.rearrange("p (a b) -> p a b", b=128), ALU.add), p, tdeps)
                RA.give(ai, e)
                wtoks.append(e)
                yield
            XTr.give(xi, p)

        def run_attention(A):
            st = dict(qtok={}, ktok={}, readers={b: [] for b in range(NB)})
            A["mcount"] = [0]
            attention_buffers()
            NU = A["units"]
            V = {}
            Os = {}

            def prologue(b):
                if b >= 2:
                    sq_free[b % 2] = st["readers"][b - 2]
                yield from A["prologue"](b, st, V)

            units = [(b, u) for b in range(NB) for u in range(NU)]
            for _ in prologue(0):
                pass
            nxt = load_unit(A, 0, 0, st)
            if A["max"]:
                for _ in maxima(A, nxt):
                    pass
            tail = []
            for n, (b, u) in enumerate(units):
                U = nxt
                sides = list(tail)
                tail = []
                if u == 0:
                    oi, O, od = Or.take()
                    Os[b] = (oi, O, [], od)
                if n + 1 < len(units):
                    nb, nu = units[n + 1]
                    if nb == b:
                        nxt = load_unit(A, nb, nu, st)
                    else:
                        nxt = None
                pre = prologue(b + 1) if (b + 1 < NB and u == 0) else None
                if pre is not None:
                    sides.append(pre)
                if A["max"] and n + 1 < len(units) and nxt is not None:
                    sides.append(maxima(A, nxt))
                oi, O, ot, od = Os[b]
                va, vtok, vi = V[b]
                if n + 1 < len(units) and nxt is None:
                    if NU == 1:
                        for _ in chain(*sides):
                            pass
                        sides = []
                    nxt = load_unit(A, nb, nu, st)
                    if A["max"]:
                        sides.append(maxima(A, nxt))
                weave(attend(A, U, va, vtok, O, ot, od), chain(*sides), A["lead"], A["rate"])
                QOr.give(U["qi"], U["last"], U["sreads"])
                KOr.give(U["ki"], U["last"], U["sreads"])
                if u == NU - 1:
                    flush()
                    flush()
                    VAr.give(vi, (pe.sem, pe.n))
                    tail.append(A["finish"](b, O, oi, ot))
            for g in tail:
                for _ in g:
                    pass
            hidden_buffers()
            sq_free[0], sq_free[1] = st["readers"][NB - 2], st["readers"][NB - 1]

        def group(blocks, *exps):
            return dict(blocks=blocks, exps=exps)

        def full_chunks():
            return [[group([(128 * s, 128, 512 * half, 512, 512 * (s % 2), None, s) for s in (2 * i, 2 * i + 1)],
                           (128, 0, 1024)) for i in range(4)] for half in range(2)]

        def causal_chunks():
            out = []
            for half in range(2):
                g = [group([(128 * s, 128, 512 * half, 512, 512 * (s % 2), None, s) for s in (2 * i, 2 * i + 1)],
                           (128, 0, 1024)) for i in range(2 * half)]
                b = 4 * half
                g.append(group([(128 * b, 128, 128 * b, 512, 0, mC, b),
                                (128 * (b + 1), 128, 128 * (b + 1), 384, 512, mC, b + 1),
                                (128 * (b + 3), 128, 128 * (b + 3), 128, 896, mC, b + 3)], (128, 0, 1024)))
                g.append(group([(128 * (b + 2), 128, 128 * (b + 2), 256, 0, mC, b + 2)], (128, 0, 256)))
                out.append(g)
            return out

        def local_chunks():
            a = [(128 * s, 128, 128 * s, 160, 32 + 160 * s, mL, s) for s in range(3)] + [(384, 128, 384, 128, 512, mL, 3)]
            b = [(384, 128, 512, 32, 0, mL[:, 128:160], 3)]
            b += [(128 * s, 128, 128 * s, 160, 32 + 160 * (s - 4), mL, s) for s in range(4, 7)] + [(896, 128, 896, 128, 512, mL, 7)]
            return [[group(a, (128, 32, 640))], [group(b, (128, 0, 640))]]

        def padded_chunks():
            a = [(0, 128, 0, 128, 512, mA[:, 32:160], 0)]
            a += [(128 * s, 128, 128 * s - 32, 160, 160 * (s - 1), mA, s) for s in range(1, 4)]
            a += [(512, 128, 480, 32, 480, mA[:, 0:32], 4)]
            b = [(512, 128, 512, 128, 512, mA[:, 32:160], 4)]
            b += [(128 * s, 128, 128 * s - 32, 160, 32 + 160 * (s - 5), mA, s) for s in range(5, 8)]
            b += [(T, 32, T - 32, 32, 0, mA[:, 0:32], 8)]
            return [[group(a, (128, 0, 640))], [group(b, (128, 32, 640), (32, 0, 32))]]

        def sink_chunks():
            a = [(128 * s, 128, 128 * s, 256 if s < 3 else 128, 256 * s, mB if s else mB0, s) for s in range(4)]
            b = [(384, 128, 512, 128, 0, mB[:, 128:256], 3), (512, 128, 512, 256, 128, mB, 4),
                 (896, 128, 896, 128, 384, mB, 7), (640, 128, 640, 256, 512, mB, 5), (768, 128, 768, 256, 768, mB, 6)]
            return [[group(a, (128, 0, 896)), group([(0, 4, 256, 256, 0, None, 0)], (4, 0, 256))],
                    [group(b, (128, 0, 1024)), group([(0, 4, 512, 512, 0, None, 0)], (4, 0, 512))]]

        def scores_full(tt):
            return [[(0, 512, None)], [(512, 512, None)]]

        def scores_padded(tt):
            return [[(128 * tt, 160, mL[:, :])]]

        def scores_sink(tt):
            if tt == 0:
                return [[(0, 128, mBt[:, 128:256])]]
            if tt == 1:
                return [[(0, 256, mBt1[:, :])]]
            return [[(128 * tt - 128, 256, mBt[:, :]), (0, 4, None)]]

        def ones_columns(D, nh):
            toks = []
            for i, va in enumerate(VAr.bufs):
                v = va[:, :, 0:nh * (D + 1)].rearrange("p n (h c) -> p n h c", c=D + 1)
                t = None
                for n in range(9):
                    t = pool(lambda v=v, n=n: nc.gpsimd.memset(v[:, n, :, D:D + 1], 1.0), VAr.free[i])
                VAr.free[i] = [t]

        def va_view(va, D, nh, n0, n):
            return va[:, n0:n0 + n, 0:nh * (D + 1)].rearrange("p n (h c) -> p n h c", c=D + 1)

        def stage1_prologue(b, st, V):
            ni, xn, nd = XNr.take()
            c = yield from layernorm(X[:, b, :, :], xn, [xtok[b], nd])
            xi, xt, xd = XTr.take()
            t = yield from transposed(lambda i: xn[:, i, :], 128, xt, 0, c, xd)
            XNr.give(ni, (pe.sem, pe.n))
            st["ktok"][b], kr = yield from split(xt[:, 0:T], 128, T, None, t, scr_k[b % 2, :, :, 0:T], sq_free[b % 2])
            qi, qf, qd = HBr.take()
            qff = qf[:, :, :].rearrange("p a b -> p (a b)")
            es = []
            for g in range(2):
                ci, ps, cd = RC.take()
                p = pe(lambda g=g, ps=ps: mm(ps, wbd[:, :], xt[:, 512 * g:512 * g + 512], start=True, stop=True), t, cd, L)
                e = act(lambda g=g, ps=ps: nc.scalar.activation(qff[:, 512 * g:512 * g + 512], ps, ACT.Copy), p, qd)
                RC.give(ci, e)
                es.append(e)
                yield
            st["qtok"][b], qr = yield from split(qff, 128, T, None, es, scr_q[b % 2], sq_free[b % 2])
            HBr.give(qi, qr)
            vi, va, vd = VAr.take()
            vt = []
            for g in range(2):
                ci, ps, cd = RC.take()
                addrows(ps, True, 0, cd)
                for i in range(4):
                    p = pe(lambda g=g, i=i, ps=ps: mm(ps[:, 128 * i:128 * i + 128],
                                                      xt[:, 512 * g + 128 * i:512 * g + 128 * i + 128], wvT[:, :],
                                                      start=False, stop=(i == 3)), t, cd, L)
                for i in range(4):
                    e = dve(lambda g=g, i=i, ps=ps: nc.vector.tensor_copy(
                        va_view(va, 8, 16, 4 * g + i, 1)[:, 0, :, 0:8],
                        ps[:, 128 * i:128 * i + 128].rearrange("p (h d) -> p h d", d=8)), p, vd)
                RC.give(ci, e)
                vt.append(e)
                yield
            XTr.give(xi, p, kr)
            V[b] = (va, vt, vi)

        def finish_into_x(A):
            def finish(b, O, oi, ot):
                w = []
                yield from project(A, b, O, oi, ot, X[:, b, :, :], xtok[b], w)
                xtok[b] = w
            return finish

        ones_columns(8, 16)
        A1 = dict(whole=True, D=8, group=1, kn=T, max=True, pieces=2, scores=scores_full, scale=RS8, chunks=full_chunks(),
                  units=4, wo=outT, bias=32, prologue=stage1_prologue, lead=8, rate=2)
        A1["finish"] = finish_into_x(A1)
        run_attention(A1)

        def ffn():
            pend = []
            for b in range(NB):
                ni, xn, nd = XNr.take()
                for _ in (g := layernorm_run(X[:, b, :, :], xn, [xtok[b], nd])):
                    pass
                c = g_out[0]
                xi, xt, xd = XTr.take()
                tg = run(transposed(lambda i: xn[:, i, :], 128, xt, 0, c, xd))
                XNr.give(ni, (pe.sem, pe.n))
                for g in range(2):
                    hi, hT, hd = PTr.take()
                    hs = []
                    for c4 in range(4):
                        ai, ps, ad = RA.take()
                        p = pe(lambda c4=c4, g=g, ps=ps, xt=xt: mm(ps, fW1[:, 128 * c4:128 * c4 + 128], xt[:, 512 * g:512 * g + 512],
                                                                   start=True, stop=True), tg, ad, L)
                        e = act(lambda c4=c4, ps=ps, hT=hT: nc.scalar.activation(hT[:, c4, :], ps, ACT.Relu, bias=fb1[:, c4:c4 + 1]),
                                p, hd, L)
                        RA.give(ai, e)
                        hs.append(e)
                    while pend:
                        pend.pop(0)()

                    def down(b=b, g=g, hi=hi, hT=hT, hs=hs):
                        ci, ps, cd = RP.take()
                        addrows(ps, True, 64, cd)
                        for i in range(4):
                            for c4 in range(4):
                                f = pe if (c4 == 3) else pe.silent
                                p = f(lambda c4=c4, i=i, ps=ps: mm(ps[:, 128 * i:128 * i + 128], hT[:, c4, 128 * i:128 * i + 128],
                                                                   fW2[:, c4, :], start=False, stop=(c4 == 3 and i == 3)), hs, cd, L)
                        PTr.give(hi, p)
                        e = dve(lambda: nc.vector.tensor_tensor(X[:, b, 4 * g:4 * g + 4, :], X[:, b, 4 * g:4 * g + 4, :],
                                                                ps.rearrange("p (a b) -> p a b", b=128), ALU.add), p)
                        RP.give(ci, e)
                        xtok[b] = [xtok[b], e]
                    pend.append(down)
                XTr.give(xi, p)
            while pend:
                pend.pop(0)()

        g_out = [None]

        def layernorm_run(*a):
            g_out[0] = yield from layernorm(*a)

        def run(gen):
            while True:
                try:
                    next(gen)
                except StopIteration as s:
                    return s.value

        ffn()

        def rope_norm(nh, D, b, interleaved, tab, norm, qi_tok, w):
            ti, (t1, t2), td = Tr.take()
            hd = D // 2
            n3 = [128, NT, nh, hd]
            v = QK[:, :, 0:nh * D].rearrange("p n (h c) -> p n h c", c=D)
            if interleaved:
                ve = v.rearrange("p n h (c two) -> p n h c two", two=2)
                xe, xo = ve[:, :, :, :, 0], ve[:, :, :, :, 1]
            else:
                xe, xo = v[:, :, :, 0:hd], v[:, :, :, hd:D]
            co = tab[:, 0, :, :].unsqueeze(2)
            si = tab[:, 1, :, :].unsqueeze(2)
            w1 = t1[:, 0:NT * nh * hd].rearrange("p (n h c) -> p n h c", n=NT, c=hd)
            w2 = t2[:, 0:NT * nh * hd].rearrange("p (n h c) -> p n h c", n=NT, c=hd)
            m = NT * nh * hd
            assert m <= 768
            u1 = t1[:, 768:768 + m].rearrange("p (n h c) -> p n h c", n=NT, c=hd)
            bc = [128, nh, hd]
            toks = []
            for i in range(NT):
                cb_, sb_ = co[:, i, :, :].broadcast_to(bc), si[:, i, :, :].broadcast_to(bc)
                a = pool(lambda i=i, cb_=cb_: nc.gpsimd.tensor_tensor(w1[:, i], xe[:, i], cb_, ALU.mult), qi_tok, td, L)
                e = dve(lambda i=i, sb_=sb_: nc.vector.tensor_tensor(w2[:, i], xo[:, i], sb_, ALU.mult), qi_tok, td, L)
                a2 = pool(lambda i=i, sb_=sb_: nc.gpsimd.tensor_tensor(u1[:, i], xe[:, i], sb_, ALU.mult), qi_tok, td, L)
                e2 = dve(lambda i=i, cb_=cb_: nc.vector.tensor_tensor(xo[:, i], xo[:, i], cb_, ALU.mult), e)
                toks.append((a2, e, e2))
                if i % 4 == 3:
                    yield
            for i in range(NT):
                a2, e, e2 = toks[i]
                f1 = dve(lambda i=i: nc.vector.tensor_tensor(xe[:, i], w1[:, i], w2[:, i], ALU.subtract), a2, e)
                f2 = dve(lambda i=i: nc.vector.tensor_tensor(xo[:, i], u1[:, i], xo[:, i], ALU.add), a2, e2)
                if i % 4 == 3:
                    yield
            if not norm:
                Tr.give(ti, f2)
                return [f1, f2]
            k = NT * nh
            qv = QK[:, :, 0:nh * D]
            e = dve(lambda: nc.vector.tensor_tensor(t1[:, 0:k * D].rearrange("p (n c) -> p n c", n=NT), qv, qv, ALU.mult), f1, f2)
            si_, ss, sd = SQ.take()
            e = dve(lambda: nc.vector.tensor_reduce(ss[:, 0:k], t1[:, 0:k * D].rearrange("p (k c) -> p k c", c=D), AX.X, ALU.add),
                    e, sd)
            Tr.give(ti, e)
            ni, _, nd = NWr.take()
            y, e = newton(None, k, ss[:, 0:k], 1.0 / D, 1e-6, e, nd)
            yield
            yv = y.rearrange("p (n h) -> p n h", n=NT)
            for i in range(NT):
                e2 = dve(lambda i=i: nc.vector.tensor_tensor(v[:, i], v[:, i], yv[:, i, :].unsqueeze(2).broadcast_to([128, nh, D]),
                                                             ALU.mult), e)
            NWr.give(ni, e2)
            SQ.give(si_, e2)
            return [e2]

        Hs = {}

        def b_common(b, st, wsel, V):
            hb = Hs[b]
            ni, xn, nd = XNr.take()
            c = yield from rms(hb["buf"], xn, hb["toks"], nd)
            xi, xt, xd = XTr.take()
            t = yield from transposed(lambda i: xn[:, i, :], 128, xt, 0, c, xd, scale=n1w[:, wsel:wsel + 1])
            XNr.give(ni, (pe.sem, pe.n))
            return xi, xt, t

        def b_operands(b, st, toks, e_deps):
            fi, ff, fd = XTr.take()
            t = yield from transposed(lambda i: QK[:, i, 0:128], 128, ff, 0, toks, fd)
            st["qtok"][b], r = yield from split(ff[:, 0:T], 128, T, None, t, scr_q[b % 2], sq_free[b % 2])
            XTr.give(fi, r)
            return None

        def k_operand(b, st, toks, c0, w):
            fi, ff, fd = XTr.take()
            t = yield from transposed(lambda i: QK[:, i, c0:c0 + w], w, ff, 0, toks, fd)
            st["ktok"][b], r = yield from split(ff[0:w, 0:T], w, T, None, t, scr_k[b % 2, :, 0:w, 0:T], sq_free[b % 2])
            XTr.give(fi, r)

        def global_prologue(b, st, V):
            hi, hb, hd = HBr2[b]
            c = yield from layernorm(X[:, b, :, :], hb, [xtok[b], hd])
            Hs[b] = dict(buf=hb, toks=[c])
            xi, xt, t = yield from b_common(b, st, 0, V)
            qi, _, qd = QKr.take()
            qe = []
            for g in range(2):
                ci, ps, cd = RC.take()
                for i in range(4):
                    p = pe(lambda g=g, i=i, ps=ps: mm(ps[:, 128 * i:128 * i + 128],
                                                      xt[:, 512 * g + 128 * i:512 * g + 128 * i + 128], gq[:, :],
                                                      start=True, stop=True), t, cd, L)
                e = act(lambda g=g, ps=ps: nc.scalar.activation(QK[:, 4 * g:4 * g + 4, 0:128],
                                                                ps.rearrange("p (a b) -> p a b", b=128), ACT.Copy), p, qd)
                RC.give(ci, e)
                qe.append(e)
                yield
            li, (lt, _), ld = Tr.take()
            le = []
            for g in range(2):
                ci, ps, cd = RC.take()
                p = pe(lambda g=g, ps=ps: mm(ps[0:32, :], gdown[:, :], xt[:, 512 * g:512 * g + 512], start=True, stop=True), t, cd, L)
                e = act(lambda g=g, ps=ps: nc.scalar.activation(lt[0:32, 512 * g:512 * g + 512], ps[0:32, :], ACT.Copy), p, ld)
                RC.give(ci, e)
                le.append(e)
            XTr.give(xi, p)
            yield
            vi, va, vd = VAr.take()
            ci, ps, cd = RC.take()
            for i in range(8):
                p = pe(lambda i=i, ps=ps: mm(ps[:, 64 * i:64 * i + 64], lt[0:32, 128 * i:128 * i + 128], gup[:, :],
                                             start=True, stop=True), le, cd, L)
            Tr.give(li, p)
            psv = ps.rearrange("p (a b) -> p a b", b=64)
            e = dve(lambda: nc.vector.tensor_copy(QK[:, :, 128:160], psv[:, :, 0:32]), p, qd)
            qe.append(e)
            for i in range(8):
                e = dve(lambda i=i: nc.vector.tensor_copy(va_view(va, 8, 4, i, 1)[:, 0, :, 0:8],
                                                          psv[:, i, 32:64].rearrange("p (h c) -> p h c", c=8)), p, vd)
            RC.give(ci, e)
            V[b] = (va, [e], vi)
            yield
            rt = yield from rope_norm(20, 8, b, True, cgg, True, qe, None)
            yield from b_operands(b, st, rt, None)
            yield from k_operand(b, st, rt, 128, 32)
            QKr.give(qi, (pe.sem, pe.n))

        def wide_qkv(b, xt, xi, t, W, n, qw, vw, D, qd, V):
            vi, va, vd = VAr.take()
            qe, ve = [], []
            for g in range(4):
                ci, ps, cd = RC.take()
                for i in range(2):
                    tt = 2 * g + i
                    p = pe(lambda tt=tt, i=i, ps=ps: mm(ps[:, 256 * i:256 * i + n], xt[:, 128 * tt:128 * tt + 128], W[:, :],
                                                        start=True, stop=True), t, cd, L)
                pv3 = ps.rearrange("p (a b) -> p a b", b=256)
                e = dve(lambda g=g, pv3=pv3: nc.vector.tensor_copy(QK[:, 2 * g:2 * g + 2, 0:qw], pv3[:, :, 0:qw]), p, qd)
                qe.append(e)
                for i in range(2):
                    e = dve(lambda g=g, i=i, pv3=pv3: nc.vector.tensor_copy(
                        va_view(va, D, vw // D, 2 * g + i, 1)[:, 0, :, 0:D],
                        pv3[:, i, qw:qw + vw].rearrange("p (h c) -> p h c", c=D)), p, vd)
                RC.give(ci, e)
                ve.append(e)
                yield
            XTr.give(xi, p)
            V[b] = (va, ve, vi)
            return qe

        def local_prologue(b, st, V):
            xi, xt, t = yield from b_common(b, st, 1, V)
            qi, _, qd = QKr.take()
            qe = yield from wide_qkv(b, xt, xi, t, lqkv, 192, 160, 32, 8, qd, V)
            rt = yield from rope_norm(20, 8, b, True, cgl, True, qe, None)
            yield from b_operands(b, st, rt, None)
            yield from k_operand(b, st, rt, 128, 32)
            QKr.give(qi, (pe.sem, pe.n))

        cgg = cg[:, 0]
        cgl = cg[:, 1]
        H4 = mW3[:, :, :, :].rearrange("p a b c -> p (a b c)")[:, 0:2048].rearrange("p (a b c) -> p a b c", a=2, b=NT)
        HBr2 = {b: (b, HBr.bufs[b], HBr.free[b]) if b < 2 else (b, H4[:, b - 2], []) for b in range(NB)}
        HBr.free = [None, None]

        def finish_h(A):
            def finish(b, O, oi, ot):
                w = []
                yield from project(A, b, O, oi, ot, Hs[b]["buf"], Hs[b]["toks"], w)
                Hs[b]["toks"] = w
            return finish

        def finish_hx(A):
            def finish(b, O, oi, ot):
                w = []
                yield from project(A, b, O, oi, ot, Hs[b]["buf"], Hs[b]["toks"], w)
                e = pool(lambda b=b: nc.gpsimd.tensor_tensor(X[:, b, :, :], X[:, b, :, :], Hs[b]["buf"][:, :, :], ALU.add),
                         w, xtok[b])
                xtok[b] = [e]
                if b < 2:
                    HBr.free[b] = [e]
            return finish

        ones_columns(8, 4)
        A3 = dict(whole=False, D=8, group=4, kn=T, max=False, scale=RS8, chunks=causal_chunks(), units=4, wo=gwo, bias=None,
                  prologue=global_prologue, lead=0, rate=1)
        A3["finish"] = finish_h(A3)
        run_attention(A3)
        A4 = dict(whole=False, D=8, group=4, kn=T, max=False, scale=RS8, chunks=local_chunks(), units=4, wo=lwo, bias=None,
                  prologue=local_prologue, lead=0, rate=2)
        A4["finish"] = finish_hx(A4)
        run_attention(A4)
        L3 = dma(sp, nc.sync, mW3[:, :, :, :], d["mW3"], xtok[2], xtok[3])
        ffn()

        def padded_prologue(b, st, V):
            ni, xn, nd = XNr.take()
            c = yield from layernorm(X[:, b, :, :], xn, [xtok[b], nd])
            xi, xt, xd = XTr.take()
            z = pool(lambda xt=xt: nc.gpsimd.memset(xt[:, 0:16], 0.0), xd)
            z = pool(lambda xt=xt: nc.gpsimd.memset(xt[:, T + 16:T + 32], 0.0), xd)
            t = yield from transposed(lambda i: xn[:, i, :], 128, xt, 16, c, xd)
            XNr.give(ni, (pe.sem, pe.n))
            qi, qf, qd = HBr.take()
            qff = qf[:, :, :].rearrange("p a b -> p (a b)")
            fi, ff, fd = XTr.take()
            es, ks = [], []
            ks.append(pool(lambda ff=ff: nc.gpsimd.memset(ff[0:16, 0:16], 0.0), fd))
            ks.append(pool(lambda ff=ff: nc.gpsimd.memset(ff[0:16, T + 16:T + 32], 0.0), fd))
            for g in range(2):
                ci, ps, cd = RC.take()
                p = pe(lambda g=g, ps=ps: mm(ps, aWq[:, :], xt[:, 16 + 512 * g:16 + 512 * g + 512], start=True, stop=True), t, cd, L)
                e = act(lambda g=g, ps=ps: nc.scalar.activation(qff[:, 512 * g:512 * g + 512], ps, ACT.Identity,
                                                                bias=abq[:, 0:1]), p, qd, L)
                RC.give(ci, e)
                es.append(e)
                ci, ps, cd = RC.take()
                p = pe(lambda g=g, ps=ps: mm(ps[0:16, :], aWkv[:, 0:16], xt[:, 16 + 512 * g:16 + 512 * g + 512],
                                             start=True, stop=True), t, cd, L)
                e = act(lambda g=g, ps=ps, ff=ff: nc.scalar.activation(ff[0:16, 16 + 512 * g:16 + 512 * g + 512], ps[0:16, :],
                                                                       ACT.Identity, bias=abk[:, 0:1]), p, fd, L)
                RC.give(ci, e)
                ks.append(e)
                yield
            vi, va, vd = VAr.take()
            ci, ps, cd = RC.take()
            for j in range(9):
                n = 128 if j < 8 else 32
                pe.silent(lambda j=j, n=n, ps=ps: mm(ps[0:n, 16 * j:16 * j + 16], xt[:, 128 * j:128 * j + n], aWkv[:, 16:32],
                                                     start=True, stop=False), t, z, cd, L)
                valid = abv[:, 0:128] if j == 0 else abv[:, 128:160] if j == 8 else ones[0:1, :]
                p = pe(lambda j=j, n=n, ps=ps, valid=valid: mm(ps[0:n, 16 * j:16 * j + 16], valid, abv[:, 160:176],
                                                               start=False, stop=True))
            psv = ps[:, 0:144].rearrange("p (n h c) -> p n h c", n=9, c=8)
            for j in range(9):
                n = 128 if j < 8 else 32
                e = dve(lambda j=j, n=n: nc.vector.tensor_copy(va_view(va, 8, 2, j, 1)[0:n, 0, :, 0:8], psv[0:n, j]), p, vd)
            RC.give(ci, e)
            XTr.give(xi, p)
            V[b] = (va, [e], vi)
            yield
            st["ktok"][b], r = yield from split(ff[0:16, 0:T + 32], 16, T + 32, None, ks, scr_k[b % 2, :, 0:16, 0:T + 32],
                                                sq_free[b % 2])
            XTr.give(fi, r)
            st["qtok"][b], r = yield from split(qff, 128, T, None, es, scr_q[b % 2], sq_free[b % 2])
            HBr.give(qi, r)

        ones_columns(8, 2)
        A5 = dict(whole=False, D=8, group=8, kn=T + 32, max=True, pieces=1, scores=scores_padded, scale=1.0, chunks=padded_chunks(),
                  units=4, wo=aWo, bias=96, prologue=padded_prologue, lead=2, rate=5)
        A5["finish"] = finish_into_x(A5)
        run_attention(A5)

        wfr = Ring([sb("WF0", [128, 8, 8])])
        LG = sb("LG", [128, 8, 8])
        MX = sb("MX", [128, 8, 8])
        IX = sb("IX", [128, 8, 8], U32)
        IXF = sb("IXF", [128, 8, 2])
        WW = sb("WW", [128, 3, 8])
        OH = sb("OH", [128, 8, 8])

        def moe(store):
            for b in range(NB):
                hi_, hb, hd = HBr.take()
                c = run(layernorm(X[:, b, :, :], hb, [xtok[b], hd]))
                ni, xn, nd = XNr.take()
                c2 = run(rms(hb, xn, c, nd))
                xi, xt, xd = XTr.take()
                t = run(transposed(lambda i: xn[:, i, :], 128, xt, 0, c2, xd, scale=rmsw[:, 0:1]))
                XNr.give(ni, (pe.sem, pe.n))
                a = pool(lambda b=b, hb=hb: nc.gpsimd.tensor_tensor(X[:, b, :, :], X[:, b, :, :], hb[:, :, :], ALU.add), c, xtok[b])
                HBr.give(hi_, a, c2)
                xa = [a]
                ci, ps, cd = RC.take()
                for i in range(NT):
                    p = pe(lambda i=i, ps=ps, xt=xt: mm(ps[:, 8 * i:8 * i + 8], xt[:, 128 * i:128 * i + 128], gateT[:, :],
                                                        start=True, stop=True), t, cd, L)
                wi, WF, wd = wfr.take()
                e = dve(lambda ps=ps: nc.vector.tensor_copy(LG[:, :, :].rearrange("p a b -> p (a b)"), ps[:, 0:64]), p, wd)
                RC.give(ci, e)
                for i in range(NT):
                    e1 = dve(lambda i=i: nc.vector.max(MX[:, i, :], LG[:, i, :]), e)
                for i in range(NT):
                    e2 = dve(lambda i=i: nc.vector.max_index(IX[:, i, :], MX[:, i, :], LG[:, i, :]), e1)
                e2 = dve(lambda: nc.vector.tensor_copy(IXF[:, :, :], IX[:, :, 0:2]), e2)
                e1 = dve(lambda: nc.vector.tensor_tensor(WW[:, 0, :], MX[:, :, 1], MX[:, :, 0], ALU.subtract), e1)
                a1 = act(lambda: nc.scalar.activation(WW[:, 1, :], WW[:, 0, :], ACT.Exp), e1)
                e1 = dve(lambda: nc.vector.tensor_scalar(WW[:, 0, :], WW[:, 1, :], 1.0, None, ALU.add), a1)
                e1 = dve(lambda: nc.vector.reciprocal(WW[:, 2, :], WW[:, 0, :]), e1)
                e1 = dve(lambda: nc.vector.tensor_tensor(WW[:, 1, :], WW[:, 1, :], WW[:, 2, :], ALU.mult), e1)
                bc = [128, 8, 8]
                io = iota8[:, :].unsqueeze(1)
                e3 = dve(lambda WF=WF: nc.vector.tensor_tensor(WF[:, :, :], io.broadcast_to(bc), IXF[:, :, 0:1].broadcast_to(bc),
                                                               ALU.is_equal), e2, L)
                e3 = dve(lambda WF=WF: nc.vector.tensor_tensor(WF[:, :, :], WF[:, :, :],
                                                               WW[:, 2, :].unsqueeze(2).broadcast_to(bc), ALU.mult), e1, e3)
                e4 = dve(lambda: nc.vector.tensor_tensor(OH[:, :, :], io.broadcast_to(bc), IXF[:, :, 1:2].broadcast_to(bc),
                                                         ALU.is_equal), e2)
                e4 = dve(lambda: nc.vector.tensor_tensor(OH[:, :, :], OH[:, :, :],
                                                         WW[:, 1, :].unsqueeze(2).broadcast_to(bc), ALU.mult), e1, e4)
                wt = dve(lambda WF=WF: nc.vector.tensor_tensor(WF[:, :, :], WF[:, :, :], OH[:, :, :], ALU.add), e3, e4)
                pend = []
                fin = []
                for g in range(2):
                    prev = [None] * 4
                    for ex in range(NEXP):
                        hi, hT, hdd = PTr.take()
                        hs = []
                        for c in range(3):
                            n = min(128, DE - 128 * c)
                            o = DE * ex + 128 * c
                            bi, pb, bd = RB.take()
                            pe.silent(lambda o=o, n=n, pb=pb, g=g, xt=xt: mm(pb[0:n, 0, :], mW1[:, o:o + n], xt[:, 512 * g:512 * g + 512],
                                                                             start=True, stop=True), t, bd, L)
                            pe.n += 1
                            it = pe.items[-1]
                            pe.items[-1] = (it[0], it[1], pe.sem, 1)
                            pu = (pe.sem, pe.n)
                            pg = pe(lambda o=o, n=n, pb=pb, g=g, xt=xt: mm(pb[0:n, 1, :], mW2[:, o:o + n], xt[:, 512 * g:512 * g + 512],
                                                                           start=True, stop=True))
                            si, sg, sd = SGr.take()
                            a = act(lambda n=n, pb=pb, sg=sg: nc.scalar.activation(sg[0:n, :], pb[0:n, 0, :], ACT.Silu), pu, sd)
                            e = dve(lambda n=n, pb=pb, sg=sg, hT=hT, c=c: nc.vector.tensor_tensor(hT[0:n, c, :], pb[0:n, 1, :], sg[0:n, :], ALU.mult),
                                    a, pg, hdd)
                            SGr.give(si, e)
                            RB.give(bi, e)
                            hs.append(e)
                        while pend:
                            pend.pop(0)()

                        def down(b=b, g=g, ex=ex, hi=hi, hT=hT, hs=hs, prev=prev):
                            ci, ps, cd = RP.take()
                            for i in range(4):
                                for c in range(3):
                                    n = min(128, DE - 128 * c)
                                    f = pe if c == 2 else pe.silent
                                    p = f(lambda c=c, i=i, n=n, ps=ps: mm(ps[:, 128 * i:128 * i + 128], hT[0:n, c, 128 * i:128 * i + 128],
                                                                          mW3[0:n, ex, c, :], start=(c == 0), stop=(c == 2)), hs, cd, L, L3)
                            PTr.give(hi, p)
                            for i in range(4):
                                tt = 4 * g + i
                                e = dve(lambda i=i, tt=tt, ps=ps, WF=WF: nc.vector.scalar_tensor_tensor(
                                    X[:, b, tt, :], ps[:, 128 * i:128 * i + 128], WF[:, tt, ex:ex + 1], X[:, b, tt, :],
                                    ALU.mult, ALU.add), p, wt, xa, prev[i])
                                prev[i] = e
                            RP.give(ci, e)
                            fin.append(e)
                        pend.append(down)
                while pend:
                    pend.pop(0)()
                XTr.give(xi, (pe.sem, pe.n))
                wfr.give(wi, fin[-1])
                xtok[b] = [fin[-1]]
                if store:
                    dma(sp, nc.sync, out[b].rearrange("(n p) e -> p n e", p=128), X[:, b, :, :], xtok[b], store=True)

        moe(False)

        MBD = sb("MBD", [128, 128])
        BE2 = sb("BE2", [8, 128])
        e = dve(lambda: nc.vector.tensor_scalar(BE2[:, :], bE[:, :], bS[:, 0:1], None, ALU.mult), L)
        ci, ps, cd = RC.take()
        p = pe(lambda ps=ps: mm(ps[:, 0:128], bE[:, :], BE2[:, :], start=True, stop=True), e, cd, L)
        mbd = dve(lambda ps=ps: nc.vector.scalar_tensor_tensor(MBD[:, :], ident[:, :], 0.25, ps[:, 0:128], ALU.mult, ALU.add), p)
        RC.give(ci, mbd)

        def sink_prologue(b, st, V):
            ni, xn, nd = XNr.take()
            c = yield from layernorm(X[:, b, :, :], xn, [xtok[b], nd])
            xi, xt, xd = XTr.take()
            t = yield from transposed(lambda i: xn[:, i, :], 128, xt, 0, c, xd)
            XNr.give(ni, (pe.sem, pe.n))
            qi, _, qd = QKr.take()
            qe = yield from wide_qkv(b, xt, xi, t, bqkv, 256, 192, 64, 16, qd, V)
            rt = yield from rope_norm(12, 16, b, False, cb, False, qe, None)
            yield from k_operand(b, st, rt, 128, 64)
            fi, ff, fd = XTr.take()
            t = yield from transposed(lambda i: QK[:, i, 0:128], 128, ff, 0, rt, fd)
            QKr.give(qi, (pe.sem, pe.n))
            gi, qf, gd = HBr.take()
            qff = qf[:, :, :].rearrange("p a b -> p (a b)")
            es = []
            for g in range(2):
                ci, ps, cd = RC.take()
                p = pe(lambda g=g, ps=ps: mm(ps, MBD[:, :], ff[:, 512 * g:512 * g + 512], start=True, stop=True), t, cd, mbd)
                e = act(lambda g=g, ps=ps: nc.scalar.activation(qff[:, 512 * g:512 * g + 512], ps, ACT.Copy), p, gd)
                RC.give(ci, e)
                es.append(e)
                yield
            XTr.give(fi, p)
            st["qtok"][b], r = yield from split(qff, 128, T, None, es, scr_q[b % 2], sq_free[b % 2])
            HBr.give(gi, r)

        ones_columns(16, 4)
        A7 = dict(whole=False, D=16, group=2, kn=T, max=True, pieces=1, scores=scores_sink, scale=1.0, chunks=sink_chunks(),
                  units=2, wo=bWo, bias=None, prologue=sink_prologue, lead=2, rate=5)
        A7["finish"] = finish_into_x(A7)
        run_attention(A7)
        moe(True)

        sp.items.append((sp.waits(stores), None, None, 0))

        with nc.Block() as block:
            @block.sync
            def _(eng):
                sp.play(eng)

            @block.tensor
            def _(eng):
                pe.play(eng)

            @block.vector
            def _(eng):
                dve.play(eng)

            @block.scalar
            def _(eng):
                act.play(eng)

            @block.gpsimd
            def _(eng):
                pool.play(eng)


def tables():
    import numpy as np

    def bf16(x):
        return (np.ascontiguousarray(x, np.float32).view(np.uint32) >> 16).astype(np.uint16)

    neg = np.float32(-1e30)
    i = np.arange(128)[:, None]

    def mask(allowed):
        return bf16(np.where(allowed, np.float32(0), neg))

    def rope(base, hd):
        inv = (np.float32(1.0) / np.float32(base) ** (np.arange(0, hd, 2, dtype=np.float32) / np.float32(hd))).astype(np.float32)
        f = np.arange(T, dtype=np.float32)[:, None] * inv[None, :]
        cs = np.stack([np.cos(f), np.sin(f)]).astype(np.float32)
        return np.ascontiguousarray(cs.reshape(2, NT, 128, hd // 2).transpose(2, 0, 1, 3))

    c160, c256 = np.arange(160)[None, :], np.arange(256)[None, :]
    c = {
        "ident": np.eye(128, dtype=np.float32), "identb": bf16(np.eye(128)),
        "ones": np.ones((128, 128), np.float32),
        "onesk": bf16(np.ones((3, 4, T + 32))),
        "mC": mask(np.arange(128)[None, :] >= i),
        "mL": mask((c160 - i >= 0) & (c160 - i < 32)),
        "mA": mask((i + 32 - c160 >= 0) & (i + 32 - c160 <= 31)),
        "mB": mask((c256 - i >= 0) & (c256 - i <= 127)),
        "mB0": mask((c256 - i >= 0) & ((c256 - i <= 127) | (i < 4))),
        "mBt": mask((i + 128 - c256 >= 0) & (i + 128 - c256 <= 127)),
        "mBt1": mask((i + 128 - c256 >= 0) & ((i + 128 - c256 <= 127) | (c256 < 4))),
        "cg": np.ascontiguousarray(np.stack([rope(1000000.0, 8), rope(10000.0, 8)], axis=1)),
        "cb": rope(10000.0, 16),
        "iota8": np.broadcast_to(np.arange(8, dtype=np.float32), (128, 8)).copy(),
    }
    return c


def laid_out(a):
    import numpy as np

    g = {k: np.asarray(v) for k, v in a.items()}
    f = np.float32
    o = {"x": g["L0_attn_a_x"]}
    wbd = np.zeros((128, 128), f)
    for h in range(16):
        wbd[8 * h:8 * h + 8, 8 * h:8 * h + 8] = g["L0_attn_a_w_att_val"][h]
    o["wbd"] = wbd
    o["wvT"] = g["L0_attn_a_wv_w"].T
    o["outT"] = g["L0_attn_a_out_w"].T
    rows = np.zeros((128, 512), f)
    for r, n in ((0, "L0_attn_a_wv_b"), (32, "L0_attn_a_out_b"), (64, "L0_ffn_b2"), (96, "L1_attn_a_bo")):
        for i in range(4):
            rows[r, 128 * i:128 * i + 128] = g[n]
    o["rows"] = rows
    o["fW1"] = g["L0_ffn_W1"]
    o["fb1"] = g["L0_ffn_b1"].reshape(4, 128).T
    o["fW2"] = g["L0_ffn_W2"].reshape(4, 128, 128).transpose(1, 0, 2)
    o["n1w"] = np.stack([g["L0_attn_b_norm1_w"], g["L0_attn_b_norm2_w"]], axis=1)
    o["gq"] = g["L0_attn_b_g_wq"]
    o["gdown"] = g["L0_attn_b_g_kv_down"]
    o["gup"] = np.concatenate([g["L0_attn_b_g_k_up"], g["L0_attn_b_g_v_up"]], axis=1)
    o["gwo"] = g["L0_attn_b_g_wo"]
    o["lqkv"] = np.concatenate([g["L0_attn_b_l_wq"], g["L0_attn_b_l_wk"], g["L0_attn_b_l_wv"]], axis=1)
    o["lwo"] = g["L0_attn_b_l_wo"]
    o["aWq"] = g["L1_attn_a_Wq"]
    o["aWkv"] = np.concatenate([g["L1_attn_a_Wk"], g["L1_attn_a_Wv"]], axis=1)
    o["aWo"] = g["L1_attn_a_Wo"]
    o["abq"] = g["L1_attn_a_bq"][:, None]
    o["abk"] = g["L1_attn_a_bk"][:, None]
    abv = np.zeros((1, 176), f)
    abv[0, 16:144] = 1.0
    abv[0, 160:] = g["L1_attn_a_bv"]
    o["abv"] = abv
    o["bqkv"] = np.concatenate([g["L1_attn_b_Wq"], g["L1_attn_b_Wk"], g["L1_attn_b_Wv"]], axis=1)
    o["bWo"] = g["L1_attn_b_Wo"]
    bE = np.zeros((8, 128), f)
    for h in range(8):
        bE[h, 16 * h:16 * h + 3] = g["L1_attn_b_head_dirs"][h]
    o["bE"] = bE
    o["bS"] = g["L1_attn_b_head_scales"][:, None]
    o["gateT"] = g["L1_ffn_gate_w"].T
    o["rmsw"] = g["L1_ffn_rms_w"][:, None]
    o["mW1"] = g["L1_ffn_W1"].transpose(2, 0, 1).reshape(128, NEXP * DE)
    o["mW2"] = g["L1_ffn_W2"].transpose(2, 0, 1).reshape(128, NEXP * DE)
    w3 = np.zeros((128, NEXP, 3, 128), f)
    for e in range(NEXP):
        for c in range(3):
            n = min(128, DE - 128 * c)
            w3[0:n, e, c, :] = g["L1_ffn_W3"][e][:, 128 * c:128 * c + n].T
    o["mW3"] = w3
    return o


def kernel(**inputs):
    import numpy as _np
    import concourse.bacc as _bacc
    from concourse import mybir as _mybir
    from concourse.bass_utils import run_bass_kernel_spmd as _run

    nc = _bacc.Bacc("TRN2", target_bir_lowering=False, num_devices=1)
    arrays, args = {}, {}
    for name, a in {**laid_out(inputs), **tables()}.items():
        a = _np.ascontiguousarray(a)
        arrays[f"in_{name}"] = a
        args[name] = nc.dram_tensor(f"in_{name}", a.shape, _mybir.dt.from_np(a.dtype), kind="ExternalInput").ap()
        if a.dtype == _np.uint16:
            args[name] = args[name].bitcast(_mybir.dt.bfloat16)
    out = nc.dram_tensor("out_0", (NB, T, E), _mybir.dt.float32, kind="ExternalOutput").ap()
    scr_q = nc.dram_tensor("scr_q", (2, 3, 128, T), _mybir.dt.bfloat16, kind="Internal").ap()
    scr_k = nc.dram_tensor("scr_k", (2, 3, 128, T + 32), _mybir.dt.bfloat16, kind="Internal").ap()
    scr_m = nc.dram_tensor("scr_m", (2, 3, 32, 128), _mybir.dt.bfloat16, kind="Internal").ap()
    program(nc, args, out, scr_q, scr_k, scr_m)
    r = _run(nc, [arrays], core_ids=[0])
    return r.results[0]["out_0"]
```

```python
import concourse.bass as bass
from concourse import mybir
from contextlib import ExitStack

F32 = mybir.dt.float32
BF = mybir.dt.bfloat16
I32 = mybir.dt.int32
U32 = mybir.dt.uint32
ALU = mybir.AluOpType
ACT = mybir.ActivationFunctionType
AX = mybir.AxisListType

NB, T, E = 4, 1024, 128
NT = T // 128
NEXP, DE = 8, 352
NPT = 5
RS8 = float(8.0) ** -0.5


class Clock:

    def __init__(self):
        self.ends, self.front = {}, 0.0

    def step(self, start, deps, ns):
        todo = list(deps)
        while todo:
            t = todo.pop()
            if isinstance(t, list):
                todo.extend(t)
            elif t is not None:
                start = max(start, self.ends[t[0].name, t[1]] + 100.0)
        self.front = max(self.front, start + ns)
        return start + ns


class Queue:

    def __init__(self, sem, clock, ns):
        self.sem, self.clock, self.ns = sem, clock, ns
        self.n, self.t, self.items, self.seen = 0, 0.0, [], {}

    def waits(self, deps):
        need = {}
        todo = list(deps)
        while todo:
            t = todo.pop()
            if t is None:
                continue
            if isinstance(t, list):
                todo.extend(t)
                continue
            sem, v = t
            if self.seen.get(sem.name, 0) < v:
                self.seen[sem.name] = v
                need[sem.name] = (sem, v)
        return list(need.values())

    def silent(self, fn, *deps, ns=None):
        self.t = self.clock.step(self.t, deps, self.ns if ns is None else ns)
        self.items.append((self.waits(deps), fn, None, 0))

    def sign(self):
        w, fn, _, _ = self.items[-1]
        self.n += 1
        self.items[-1] = (w, fn, self.sem, 1)
        self.clock.ends[self.sem.name, self.n] = self.t
        return (self.sem, self.n)

    def __call__(self, fn, *deps, ns=None):
        self.silent(fn, *deps, ns=ns)
        return self.sign()

    def play(self, eng):
        for waits, fn, sem, by in self.items:
            for s, v in waits:
                eng.wait_ge(s, v)
            if fn is None:
                continue
            ins = fn()
            if sem is not None:
                ins.then_inc(sem, by)


class Pool:

    def __init__(self, bufs):
        self.bufs, self.free, self.ready = bufs, [[] for _ in bufs], list(range(len(bufs)))

    def take(self):
        while not self.ready:
            yield
        i = self.ready.pop(0)
        return i, self.bufs[i], self.free[i]

    def give(self, i, *toks):
        self.free[i] = list(toks)
        self.ready.append(i)


def program(nc, d, out, scr_q, scr_k, scr_m):
    ctx = ExitStack()
    with ctx:
        def sb(name, shape, dt=F32):
            return ctx.enter_context(nc.sbuf_tensor(name, shape, dt))

        def sem(name):
            return ctx.enter_context(nc.semaphore(name))

        clock = Clock()
        pe, act, dve, pool, sp = (Queue(sem(n), clock, ns) for n, ns in (
            ("s_pe", 220), ("s_act", 500), ("s_dve", 200), ("s_pool", 500), ("s_sp", 50)))
        dma_sems = [sem(f"s_dma{i}") for i in range(48)]
        dma_count = [0] * 48
        dma_at = [0]
        stores = []

        def dma(q, eng, o, i, *deps, store=False):
            k = dma_at[0] % 48
            dma_at[0] += 1
            s = dma_sems[k]
            last = (s, 16 * dma_count[k]) if dma_count[k] else None
            dma_count[k] += 1
            clock.ends[s.name, 16 * dma_count[k]] = q.clock.step(q.t, [list(deps), last], 2500)
            w = q.waits([list(deps), last])
            q.items.append((w, lambda: eng.dma_start(o, i), s, 16))
            tok = (s, 16 * dma_count[k])
            if store:
                stores.append(tok)
            return tok

        mm = nc.tensor.matmul

        PS = ctx.enter_context(nc.psum_tensor("PS", [128, 8, 512], F32))
        RA = Pool([PS[:, 0, :], PS[:, 1, :]])
        RB = Pool([PS[:, 2:4, :], PS[:, 4:6, :]])
        RC = RA
        RP = Pool([PS[:, 6, :], PS[:, 7, :]])

        X = sb("X", [128, NB, NT, 128])
        xtok = [[] for _ in range(NB)]
        XN = sb("XN", [128, NT, 128])
        XNr = Pool([XN])
        XTr = Pool([sb(f"XT{i}", [128, T + 32]) for i in range(3)])
        HBr = Pool([sb(f"HB{i}", [128, NT, 128]) for i in range(2)])
        QK = sb("QK", [128, NT, 192])
        QKr = Pool([QK])
        T1 = sb("T1", [128, 1536])
        T2 = sb("T2", [128, 768])
        Tr = Pool([(T1, T2)])
        PQr = Pool([sb("PQ0", [128, 3, T + 32], BF)])
        VAr = Pool([sb(f"VA{i}", [128, 9, 16 * 9]) for i in range(3)])
        Or = Pool([sb(f"O{i}", [128, NT, 128]) for i in range(2)])
        QOr = Pool([sb(f"QO{i}", [128, 4, T], BF) for i in range(2)])
        KOr = Pool([sb(f"KO{i}", [128, 4, T + 32], BF) for i in range(2)])
        RPT = Pool([sb(f"PT{i}", [128, 1024]) for i in range(NPT)])
        SGr = Pool([sb(f"SG{i}", [128, 512]) for i in range(2)])
        MSr = Pool([sb("MS0", [128, 32, 2])])
        MTr = Pool([(sb("MTa", [128, 32]), sb("MTb", [32, 128]), sb("MTc", [32, 128]), sb("MTd", [32, 3, 128], BF))])
        RCPr = Pool([sb(f"RCP{i}", [128, 16]) for i in range(2)])
        NW = sb("NW", [128, 4, 160])
        NWr = Pool([NW])
        OBr = Pool([sb("OB0", [128, 512])])
        Z = [dve(lambda i=i: nc.vector.memset(RP.bufs[i], 0.0)) for i in range(2)]

        STr = Pool([(sb("ST0", [128, 8, 6]), sb("MV0", [128, 8, 2]))])
        SQ = Pool([sb("SQ0", [128, 160])])

        load_toks = []

        def const(name, dt=F32):
            a = d[name]
            t = sb("c_" + name, list(a.shape), dt)
            load_toks.append(dma(sp, nc.sync, t[tuple(slice(None) for _ in a.shape)], a))
            return t

        for b in range(NB):
            xtok[b].append(dma(act, nc.scalar, X[:, b, :, :], d["x"][b].rearrange("(n p) e -> p n e", p=128)))
        ident = const("ident")
        wbd = const("wbd")
        wvT = const("wvT")
        rows = const("rows")
        ones = const("ones")
        outT = const("outT")
        L0 = list(load_toks)
        identb = const("identb", BF)
        fW1 = const("fW1")
        fb1 = const("fb1")
        fW2 = const("fW2")
        n1w = const("n1w")
        gq = const("gq")
        gdown = const("gdown")
        gup = const("gup")
        gwo = const("gwo")
        lqkv = const("lqkv")
        lwo = const("lwo")
        aWq = const("aWq")
        aWkv = const("aWkv")
        aWo = const("aWo")
        abq = const("abq")
        abk = const("abk")
        abv = const("abv")
        bqkv = const("bqkv")
        bWo = const("bWo")
        bE = const("bE")
        bS = const("bS")
        cg = const("cg")
        cb = const("cb")
        mC = const("mC", BF)
        mL = const("mL", BF)
        mA = const("mA", BF)
        mB = const("mB", BF)
        mB0 = const("mB0", BF)
        mBt = const("mBt", BF)
        mBt1 = const("mBt1", BF)
        iota8 = const("iota8")
        gateT = const("gateT")
        rmsw = const("rmsw")
        L = load_toks
        mW1 = const("mW1")
        mW2 = const("mW2")
        mW3 = const("mW3")

        def newton(v, n, src, mul, add, *deps):
            h, y, t, w = NW[:, 0, 0:n], NW[:, 1, 0:n], NW[:, 2, 0:n], NW[:, 3, 0:n]
            a = dve(lambda: nc.vector.tensor_scalar(w, src, mul, add, ALU.mult, ALU.add), *deps)
            b = dve(lambda: nc.vector.tensor_scalar(t.bitcast(I32), w.bitcast(I32), 1, None, ALU.logical_shift_right), a)
            a = dve(lambda: nc.vector.tensor_scalar(h, w, -0.5, None, ALU.mult), a)
            b = dve(lambda: nc.vector.tensor_scalar(y.bitcast(I32), t.bitcast(I32), -1.0, float(0x5f3759df), ALU.mult, ALU.add), b)
            for _ in range(3):
                b = dve(lambda: nc.vector.tensor_tensor(t, y, y, ALU.mult), b)
                b = dve(lambda: nc.vector.tensor_tensor(t, t, h, ALU.mult), b)
                b = dve(lambda: nc.vector.scalar_tensor_tensor(y, t, 1.5, y, ALU.add, ALU.mult), b)
            return y, b

        def layernorm(src, dst, deps):
            si, (st, mv), sd = (yield from STr.take())
            a = None
            for i in range(NT):
                a = dve(lambda i=i: nc.vector.bn_stats(st[:, i, :], src[:, i, :]), deps, sd)
            yield
            for i in range(NT):
                b = dve(lambda i=i: nc.vector.bn_aggr(mv[:, i, :], st[:, i, :]), a)
            ni, _, nd = (yield from NWr.take())
            y, b = newton(None, NT, mv[:, :, 1], 1.0, 1e-5, b, nd)
            yield
            for i in range(NT):
                c = dve(lambda i=i: nc.vector.tensor_scalar(dst[:, i, :], src[:, i, :], mv[:, i, 0:1], y[:, i:i + 1],
                                                            ALU.subtract, ALU.mult), b)
            STr.give(si, c)
            NWr.give(ni, c)
            return c

        def rms(src, dst, deps, ddeps):
            qi, ss, qd = (yield from SQ.take())
            ji, junk, jd = (yield from SGr.take())
            for i in range(NT):
                a = act(lambda i=i: nc.scalar.activation(junk[:, 0:128], src[:, i, :], ACT.Square, accum_out=ss[:, i:i + 1]),
                        deps, qd, jd)
                jd = a
            SGr.give(ji, a)
            yield
            ni, _, nd = (yield from NWr.take())
            y, b = newton(None, NT, ss[:, 0:NT], 1.0 / 128, 1e-6, a, nd)
            yield
            for i in range(NT):
                c = dve(lambda i=i: nc.vector.tensor_scalar(dst[:, i, :], src[:, i, :], y[:, i:i + 1], None, ALU.mult),
                        b, ddeps)
            SQ.give(qi, c)
            NWr.give(ni, c)
            return c

        def transposed(src, w, dst, off, deps, ddeps, scale=None):
            toks = []
            for g in range(2):
                ci, ps, cd = (yield from RC.take())
                for i in range(4):
                    t = pe(lambda g=g, i=i, ps=ps: nc.tensor.transpose(ps[0:w, 128 * i:128 * i + 128], src(4 * g + i), ident[:, :]),
                           deps, cd, L0)
                o = dst[0:w, off + 512 * g:off + 512 * g + 512]
                if scale is None:
                    e = act(lambda o=o, ps=ps: nc.scalar.activation(o, ps[0:w, :], ACT.Copy), t, ddeps)
                else:
                    e = act(lambda o=o, ps=ps: nc.scalar.activation(o, ps[0:w, :], ACT.Copy, scale=scale), t, ddeps, L)
                RC.give(ci, e)
                toks.append(e)
                yield
            return toks

        def split(x, r, n, q, deps, store_to, reuse):
            pi, p, pd = (yield from PQr.take())
            ri, (rr, _), rd = (yield from Tr.take())
            a = dve(lambda: nc.vector.tensor_copy(p[0:r, 0, 0:n], x), deps, pd)
            b = pool(lambda: nc.gpsimd.tensor_tensor(rr[0:r, 0:n], x, p[0:r, 0, 0:n], ALU.subtract), a, rd)
            yield
            a = dve(lambda: nc.vector.tensor_copy(p[0:r, 1, 0:n], rr[0:r, 0:n]), b)
            c = pool(lambda: nc.gpsimd.tensor_tensor(p[0:r, 2, 0:n], rr[0:r, 0:n], p[0:r, 1, 0:n], ALU.subtract), a)
            yield
            s = dma(sp, nc.sync, store_to.rearrange("a r t -> r a t"), p[0:r, :, 0:n], c, reuse, store=True)
            PQr.give(pi, s)
            Tr.give(ri, c)
            return s, b

        def addrows(bank, first, r, deps):
            return pe.silent(lambda: mm(bank, ones[r:r + 1, :], rows[r:r + 1, :], start=True, stop=False,
                                        tile_position=(r, 0)), deps, L0)

        SLOTQ, SLOTK = (0, 0, 1, 0, 1, 2, 1, 2, 2), (0, 1, 0, 2, 1, 0, 2, 1, 2)
        SLOTS = {8: 9, 16: 6}
        sfree = [[] for _ in range(NB)]
        mfree = [[] for _ in range(NB)]

        def load_unit(A, b, u, st):
            D, G = A["D"], A["group"]
            kv = max(1, 4 // G)
            kv0 = 4 * u // G
            qi, qo, qd = (yield from QOr.take())
            ki, ko, kd = (yield from KOr.take())
            kn = A["kn"]
            toks = []
            for s in range(SLOTS[D]):
                toks.append(dma(sp, nc.sync, qo[D * s:D * s + D, :, :],
                                scr_q[b, SLOTQ[s], 4 * D * u:4 * D * u + 4 * D, :].rearrange("(h d) t -> d h t", d=D),
                                st["qtok"][b], qd))
                toks.append(dma(sp, nc.sync, ko[D * s:D * s + D, 0:kv, 0:kn],
                                scr_k[b, SLOTK[s], D * kv0:D * (kv0 + kv), 0:kn].rearrange("(h d) t -> d h t", d=D),
                                st["ktok"][b], kd))
            st["readers"][b].extend(toks)
            if A["max"]:
                toks.append(dma(sp, nc.sync, ko[SLOTS[D] * D:SLOTS[D] * D + 3, 0:kv, 0:kn], d["onesk"][:, 0:kv, 0:kn], kd))

            def where(h, rows):
                return qo[0:rows, h, :], ko[0:rows, (4 * u + h) // G - kv0, :], 0
            return dict(qi=qi, qo=qo, ki=ki, ko=ko, toks=toks, G=G, kv0=kv0, u=u, b=b, sreads=[], where=where)

        def maxima(A, U, b):
            D = A["D"]
            K = SLOTS[D] * D
            qo, ko = U["qo"], U["ko"]
            mi, ms, md = (yield from MSr.take())
            last = []
            for h in range(4):
                kh = (4 * U["u"] + h) // U["G"] - U["kv0"]
                for tt in range(NT):
                    for piece in A["scores"](tt):
                        ai, ps, ad = (yield from RA.take())
                        n = 0
                        for (k0, kn, masks) in piece:
                            t = None
                            pe.silent(lambda h=h, tt=tt, ps=ps, n=n, k0=k0, kn=kn, kh=kh, s=masks is None:
                                      mm(ps[:, n:n + kn], qo[0:K, h, 128 * tt:128 * tt + 128], ko[0:K, kh, k0:k0 + kn],
                                         start=True, stop=s), U["toks"], ad, A["L"], ns=0.42 * kn)
                            if masks is not None:
                                pe.silent(lambda ps=ps, n=n, kn=kn, m=masks:
                                          mm(ps[:, n:n + kn], identb[:, :], m, start=False, stop=True))
                            n += kn
                        t = pe.sign()
                        j = A["scores"](tt).index(piece)
                        e = dve(lambda ps=ps, n=n, h=h, tt=tt, j=j:
                                nc.vector.tensor_reduce(ms[:, 8 * h + tt, j:j + 1], ps[:, 0:n], AX.X, ALU.max), t, md, ns=64 + 1.04 * n)
                        RA.give(ai, e)
                        U["sreads"] = [t]
                    yield
            ti, (ma, mb, mc, mp), td = (yield from MTr.take())
            if A["pieces"] == 2:
                e = dve(lambda: nc.vector.tensor_tensor(ma[:, :], ms[:, :, 0], ms[:, :, 1], ALU.max), e, td)
            else:
                e = dve(lambda: nc.vector.tensor_copy(ma[:, :], ms[:, :, 0]), e, td)
            MSr.give(mi, e)
            ci, ps, cd = (yield from RC.take())
            t = pe(lambda: nc.tensor.transpose(ps[0:32, 0:128], ma[:, :], ident[:, :]), e, cd)
            e = dve(lambda: nc.vector.tensor_scalar(mb[:, :], ps[0:32, 0:128], -1.0, None, ALU.mult), t)
            RC.give(ci, e)
            yield
            e = dve(lambda: nc.vector.tensor_copy(mp[:, 0, :], mb[:, :]), e)
            e = dve(lambda: nc.vector.tensor_tensor(mc[:, :], mb[:, :], mp[:, 0, :], ALU.subtract), e)
            e = dve(lambda: nc.vector.tensor_copy(mp[:, 1, :], mc[:, :]), e)
            e = dve(lambda: nc.vector.tensor_tensor(mp[:, 2, :], mc[:, :], mp[:, 1, :], ALU.subtract), e)
            s = dma(sp, nc.sync, scr_m[b].rearrange("a r t -> r a t"), mp[:, :, :], e, mfree[b], store=True)
            MTr.give(ti, s)
            s2 = dma(sp, nc.sync, qo[K:K + 3, :, :].rearrange("a h t -> a (h t)"),
                     scr_m[b].rearrange("a r t -> a (r t)"), s)
            mfree[b] = [s2]
            U["mtok"] = s2
            yield

        def attend(A, U, va, vtok, O, otoks, odeps):
            D, HU = A["D"], 4
            K = SLOTS[D] * D + (3 if A["max"] else 0)
            deps = [U["toks"], U.get("mtok")]
            for half in range(2):
                groups = A["chunks"][half]
                ri, po, rd = yield from RP.take()
                pv = []
                t = None
                for gi, group in enumerate(groups):
                    slots = []
                    for hp in range(HU // 2):
                        bi, ps, bd = yield from RB.take()
                        for (k0, kn, t0, tn, at, m, vt) in group["blocks"]:
                            mw = 0 if m is None else min(tn, m.shape[1])
                            for h2 in range(2):
                                qv, kv, p = U["where"](2 * hp + h2, K)
                                if mw:
                                    pe.silent(lambda ps=ps, qv=qv, kv=kv, p=p, h2=h2, at=at, kn=kn, mw=mw, t0=t0, k0=k0:
                                              mm(ps[0:kn, h2, at:at + mw], kv[:, k0:k0 + kn], qv[:, t0:t0 + mw],
                                                 start=True, stop=False, tile_position=(p, 0)), deps, bd, A["L"], ns=0.21 * mw)
                            for h2 in range(2):
                                if mw:
                                    pe.silent(lambda ps=ps, h2=h2, at=at, kn=kn, mw=mw, m=m:
                                              mm(ps[0:kn, h2, at:at + mw], identb[0:kn, 0:kn], m[0:kn, 0:mw],
                                                 start=False, stop=True), ns=0.42 * mw)
                            for h2 in range(2):
                                qv, kv, p = U["where"](2 * hp + h2, K)
                                if mw < tn:
                                    pe.silent(lambda ps=ps, qv=qv, kv=kv, p=p, h2=h2, at=at, kn=kn, mw=mw, t0=t0, tn=tn, k0=k0:
                                              mm(ps[0:kn, h2, at + mw:at + tn], kv[:, k0:k0 + kn], qv[:, t0 + mw:t0 + tn],
                                                 start=True, stop=True, tile_position=(p, 0)), deps, bd, A["L"],
                                              ns=0.21 * (tn - mw))
                        st_tok = pe.sign()
                        if pv and not RPT.ready:
                            t = pv.pop(0)()
                        pi, pt, pd = yield from RPT.take()
                        pt = pt[:, :].rearrange("p (a b) -> p a b", a=2)
                        for (r, a, b) in group["exps"]:
                            ex = act(lambda ps=ps, pt=pt, r=r, a=a, b=b:
                                     nc.scalar.activation(pt[0:r, :, a:b], ps[0:r, :, a:b], ACT.Exp, scale=A["scale"]), st_tok, pd,
                                     ns=60 + 1.66 * (b - a))
                        RB.give(bi, ex)
                        slots.append((pi, pt, ex))
                        U["last"] = st_tok
                        if pv:
                            t = pv.pop(0)()
                        yield

                    def product(gi=gi, group=group, slots=slots, po=po, half=half, groups=groups):
                        for bi_, (k0, kn, t0, tn, at, m, vt) in enumerate(group["blocks"]):
                            c0 = t0 - 512 * half
                            first = gi == 0 and bi_ == 0
                            last = gi == len(groups) - 1 and bi_ == len(group["blocks"]) - 1
                            for h in range(HU):
                                vh = (HU * U["u"] + h) // A["group"]
                                _, pt, ex = slots[h // 2]
                                pe.silent(lambda kn=kn, tn=tn, at=at, vt=vt, c0=c0, first=first, last=last, r=32 * h, h=h, pt=pt, vh=vh:
                                          mm(po[r:r + D + 1, c0:c0 + tn], va[0:kn, vt, vh * (D + 1):(vh + 1) * (D + 1)],
                                             pt[0:kn, h % 2, at:at + tn], start=first, stop=last,
                                             skip_group_check=not A["whole"], tile_position=(0, r)),
                                          ex, rd, vtok, Z, ns=0.84 * tn)
                        t = pe.sign()
                        for pi, _, _ in slots:
                            RPT.give(pi, t)
                        return t

                    pv.append(product)
                t = pv.pop(0)()
                assert not pv
                oi_, ob, od_ = yield from OBr.take()
                e = act(lambda po=po, ob=ob: nc.scalar.activation(ob[:, :], po, ACT.Copy), t, od_)
                RP.give(ri, e)
                yield
                ci, ps, cd = yield from RA.take()
                for i in range(4):
                    t = pe(lambda i=i, ps=ps, ob=ob: nc.tensor.transpose(ps[:, 128 * i:128 * i + 128],
                                                                         ob[:, 128 * i:128 * i + 128], ident[:, :]), e, cd)
                OBr.give(oi_, t)
                wi, rc, wd = yield from RCPr.take()
                v4 = ps.rearrange("p (n g b) -> p n g b", n=4, b=32)
                rcv = rc[:, 0:4 * HU].rearrange("p (n g) -> p n g", g=HU)
                e = dve(lambda v4=v4, rcv=rcv: nc.vector.reciprocal(rcv, v4[:, :, 0:HU, D]), t, wd)
                e = dve(lambda v4=v4, rcv=rcv, half=half: nc.vector.tensor_tensor(
                    O[:, 4 * half:4 * half + 4, HU * D * U["u"]:HU * D * U["u"] + HU * D].rearrange(
                        "p n (g c) -> p n g c", c=D),
                    v4[:, :, 0:HU, 0:D], rcv.unsqueeze(3).broadcast_to([128, 4, HU, D]), ALU.mult), e, odeps)
                RCPr.give(wi, e)
                RA.give(ci, e)
                otoks.append(e)

        def project(A, b, O, oi, otoks, target, tdeps, wtoks):
            xi, xt, xd = (yield from XTr.take())
            t = yield from transposed(lambda i: O[:, i, :], 128, xt, 0, otoks, xd)
            Or.give(oi, (pe.sem, pe.n))
            for g in range(2):
                ai, ps, ad = (yield from RA.take())
                if A["bias"] is not None:
                    addrows(ps, True, A["bias"], ad)
                for i in range(4):
                    p = pe(lambda ps=ps, i=i, g=g: mm(ps[:, 128 * i:128 * i + 128],
                                                      xt[:, 512 * g + 128 * i:512 * g + 128 * i + 128], A["wo"][:, :],
                                                      start=A["bias"] is None, stop=A["bias"] is None or i == 3), t, ad, A["L"])
                e = dve(lambda ps=ps, g=g: nc.vector.tensor_tensor(
                    target[:, 4 * g:4 * g + 4, :], target[:, 4 * g:4 * g + 4, :],
                    ps.rearrange("p (a b) -> p a b", b=128), ALU.add), p, tdeps)
                RA.give(ai, e)
                wtoks.append(e)
                yield
            XTr.give(xi, p)

        def attention(A, b):
            st = dict(qtok={}, ktok={}, readers={b: []})
            V = {}
            yield from A["prologue"](b, st, V)
            va, vtok, vi = V[b]
            oi, O, od = yield from Or.take()
            otoks = []
            for u in range(A["units"]):
                U = yield from load_unit(A, b, u, st)
                yield
                if A["max"]:
                    yield from maxima(A, U, b)
                yield from attend(A, U, va, vtok, O, otoks, od)
                QOr.give(U["qi"], U["last"], U["sreads"])
                KOr.give(U["ki"], U["last"], U["sreads"])
            VAr.give(vi, (pe.sem, pe.n))
            sfree[b] = st["readers"][b]
            yield from A["finish"](b, O, oi, otoks)

        def group(blocks, *exps):
            return dict(blocks=blocks, exps=exps)

        def full_chunks():
            return [[group([(128 * s, 128, 512 * half, 512, 0, None, s)], (128, 0, 512)) for s in range(NT)]
                    for half in range(2)]

        def causal_chunks():
            out = []
            for half in range(2):
                b = 4 * half
                g = [group([(128 * s, 128, 512 * half, 512, 0, None, s)], (128, 0, 512)) for s in range(b)]
                g.append(group([(128 * b, 128, 128 * b, 512, 0, mC, b)], (128, 0, 512)))
                g.append(group([(128 * (b + 1), 128, 128 * (b + 1), 384, 0, mC, b + 1),
                                (128 * (b + 3), 128, 128 * (b + 3), 128, 384, mC, b + 3)], (128, 0, 512)))
                g.append(group([(128 * (b + 2), 128, 128 * (b + 2), 256, 0, mC, b + 2)], (128, 0, 256)))
                out.append(g)
            return out

        def local_chunks():
            a = [(128 * s, 128, 128 * s, 160, 160 * s, mL, s) for s in range(3)]
            b = [(384, 128, 512, 32, 0, mL[:, 128:160], 3)]
            b += [(128 * s, 128, 128 * s, 160, 32 + 160 * (s - 4), mL, s) for s in range(4, 7)]
            return [[group(a, (128, 0, 480)), group([(384, 128, 384, 128, 0, mL, 3)], (128, 0, 128))],
                    [group(b, (128, 0, 512)), group([(896, 128, 896, 128, 0, mL, 7)], (128, 0, 128))]]

        def padded_chunks():
            a = [(128 * s, 128, 128 * s - 32, 160, 160 * (s - 1), mA, s) for s in range(1, 4)]
            a += [(512, 128, 480, 32, 480, mA[:, 0:32], 4)]
            b = [(128 * s, 128, 128 * s - 32, 160, 32 + 160 * (s - 5), mA, s) for s in range(5, 8)]
            b += [(T, 32, T - 32, 32, 0, mA[:, 0:32], 8)]
            return [[group(a, (128, 0, 512)), group([(0, 128, 0, 128, 0, mA[:, 32:160], 0)], (128, 0, 128))],
                    [group(b, (128, 32, 512), (32, 0, 32)),
                     group([(512, 128, 512, 128, 0, mA[:, 32:160], 4)], (128, 0, 128))]]

        def sink_chunks():
            return [[group([(0, 128, 0, 256, 0, mB0, 0), (128, 128, 128, 256, 256, mB, 1)], (128, 0, 512)),
                     group([(256, 128, 256, 256, 0, mB, 2), (384, 128, 384, 128, 256, mB, 3)], (128, 0, 384)),
                     group([(0, 4, 256, 256, 0, None, 0)], (4, 0, 256))],
                    [group([(384, 128, 512, 128, 0, mB[:, 128:256], 3), (512, 128, 512, 256, 128, mB, 4),
                            (896, 128, 896, 128, 384, mB, 7)], (128, 0, 512)),
                     group([(640, 128, 640, 256, 0, mB, 5), (768, 128, 768, 256, 256, mB, 6)], (128, 0, 512)),
                     group([(0, 4, 512, 512, 0, None, 0)], (4, 0, 512))]]

        def scores_full(tt):
            return [[(0, 512, None)], [(512, 512, None)]]

        def scores_padded(tt):
            return [[(128 * tt, 160, mL[:, :])]]

        def scores_sink(tt):
            if tt == 0:
                return [[(0, 128, mBt[:, 128:256])]]
            if tt == 1:
                return [[(0, 256, mBt1[:, :])]]
            return [[(128 * tt - 128, 256, mBt[:, :]), (0, 4, None)]]

        def take_v(D, nh):
            vi, va, vd = yield from VAr.take()
            v = va_view(va, D, nh, 0, 9)
            z = pool(lambda: nc.gpsimd.memset(v[:, :, :, D:D + 1], 1.0), vd)
            return vi, va, [vd, z]

        def va_view(va, D, nh, n0, n):
            return va[:, n0:n0 + n, 0:nh * (D + 1)].rearrange("p n (h c) -> p n h c", c=D + 1)

        def stage1_prologue(b, st, V):
            ni, xn, nd = (yield from XNr.take())
            c = yield from layernorm(X[:, b, :, :], xn, [xtok[b], nd])
            xi, xt, xd = (yield from XTr.take())
            t = yield from transposed(lambda i: xn[:, i, :], 128, xt, 0, c, xd)
            XNr.give(ni, (pe.sem, pe.n))
            st["ktok"][b], kr = yield from split(xt[:, 0:T], 128, T, None, t, scr_k[b, :, :, 0:T], sfree[b])
            qi, qf, qd = (yield from HBr.take())
            qff = qf[:, :, :].rearrange("p a b -> p (a b)")
            es = []
            for g in range(2):
                ci, ps, cd = (yield from RC.take())
                p = pe(lambda g=g, ps=ps: mm(ps, wbd[:, :], xt[:, 512 * g:512 * g + 512], start=True, stop=True), t, cd, L0, ns=860)
                e = act(lambda g=g, ps=ps: nc.scalar.activation(qff[:, 512 * g:512 * g + 512], ps, ACT.Copy), p, qd)
                RC.give(ci, e)
                es.append(e)
                yield
            st["qtok"][b], qr = yield from split(qff, 128, T, None, es, scr_q[b], sfree[b])
            HBr.give(qi, qr)
            vi, va, vd = (yield from take_v(8, 16))
            vt = []
            for g in range(2):
                ci, ps, cd = (yield from RC.take())
                addrows(ps, True, 0, cd)
                for i in range(4):
                    p = pe(lambda g=g, i=i, ps=ps: mm(ps[:, 128 * i:128 * i + 128],
                                                      xt[:, 512 * g + 128 * i:512 * g + 128 * i + 128], wvT[:, :],
                                                      start=False, stop=(i == 3)), t, cd, L0)
                for i in range(4):
                    e = dve(lambda g=g, i=i, ps=ps: nc.vector.tensor_copy(
                        va_view(va, 8, 16, 4 * g + i, 1)[:, 0, :, 0:8],
                        ps[:, 128 * i:128 * i + 128].rearrange("p (h d) -> p h d", d=8)), p, vd)
                RC.give(ci, e)
                vt.append(e)
                yield
            XTr.give(xi, p, kr)
            V[b] = (va, vt, vi)

        def finish_into_x(A):
            def finish(b, O, oi, ot):
                w = []
                yield from project(A, b, O, oi, ot, X[:, b, :, :], xtok[b], w)
                xtok[b] = w
            return finish

        A1 = dict(L=L0, whole=True, D=8, group=1, kn=T, max=True, pieces=2, scores=scores_full, scale=RS8, chunks=full_chunks(),
                  units=4, wo=outT, bias=32, prologue=stage1_prologue, lead=8, rate=2)
        A1["finish"] = finish_into_x(A1)

        def ffn(b):
            ni, xn, nd = yield from XNr.take()
            c = yield from layernorm(X[:, b, :, :], xn, [xtok[b], nd])
            xi, xt, xd = yield from XTr.take()
            tg = yield from transposed(lambda i: xn[:, i, :], 128, xt, 0, c, xd)
            XNr.give(ni, (pe.sem, pe.n))
            for g in range(2):
                hid, hs = [], []
                for c4 in range(4):
                    if c4 % 2 == 0:
                        hid.append((yield from RPT.take()))
                    _, hT, hd = hid[-1]
                    ai, ps, ad = yield from RA.take()
                    p = pe(lambda c4=c4, ps=ps, g=g: mm(ps, fW1[:, 128 * c4:128 * c4 + 128], xt[:, 512 * g:512 * g + 512],
                                                   start=True, stop=True), tg, ad, L, ns=860)
                    e = act(lambda c4=c4, ps=ps, hT=hT: nc.scalar.activation(
                        hT[:, 512 * (c4 % 2):512 * (c4 % 2) + 512], ps, ACT.Relu, bias=fb1[:, c4:c4 + 1]), p, hd, L)
                    RA.give(ai, e)
                    hs.append(e)
                    yield
                ci, ps, cd = yield from RP.take()
                addrows(ps, True, 64, cd)
                for i in range(4):
                    for c4 in range(4):
                        o = 512 * (c4 % 2) + 128 * i
                        pe.silent(lambda c4=c4, i=i, o=o, ps=ps, hT=hid[c4 // 2][1]: mm(ps[:, 128 * i:128 * i + 128], hT[:, o:o + 128],
                                                                    fW2[:, c4, :], start=False, stop=(c4 == 3 and i == 3)), hs, cd, L)
                    p = pe.sign()
                for k in range(2):
                    RPT.give(hid[k][0], p)
                e = dve(lambda g=g, ps=ps: nc.vector.tensor_tensor(X[:, b, 4 * g:4 * g + 4, :], X[:, b, 4 * g:4 * g + 4, :],
                                                                   ps.rearrange("p (a b) -> p a b", b=128), ALU.add), p)
                RP.give(ci, e)
                xtok[b] = [xtok[b], e]
                yield
            XTr.give(xi, p)

        def rope_norm(nh, D, b, interleaved, tab, norm, qi_tok, w):
            ti, (t1, t2), td = (yield from Tr.take())
            hd = D // 2
            n3 = [128, NT, nh, hd]
            v = QK[:, :, 0:nh * D].rearrange("p n (h c) -> p n h c", c=D)
            if interleaved:
                ve = v.rearrange("p n h (c two) -> p n h c two", two=2)
                xe, xo = ve[:, :, :, :, 0], ve[:, :, :, :, 1]
            else:
                xe, xo = v[:, :, :, 0:hd], v[:, :, :, hd:D]
            co = tab[:, 0, :, :].unsqueeze(2)
            si = tab[:, 1, :, :].unsqueeze(2)
            w1 = t1[:, 0:NT * nh * hd].rearrange("p (n h c) -> p n h c", n=NT, c=hd)
            w2 = t2[:, 0:NT * nh * hd].rearrange("p (n h c) -> p n h c", n=NT, c=hd)
            m = NT * nh * hd
            assert m <= 768
            u1 = t1[:, 768:768 + m].rearrange("p (n h c) -> p n h c", n=NT, c=hd)
            bc = [128, nh, hd]
            toks = []
            for i in range(NT):
                cb_, sb_ = co[:, i, :, :].broadcast_to(bc), si[:, i, :, :].broadcast_to(bc)
                a = pool(lambda i=i, cb_=cb_: nc.gpsimd.tensor_tensor(w1[:, i], xe[:, i], cb_, ALU.mult), qi_tok, td, L)
                e = dve(lambda i=i, sb_=sb_: nc.vector.tensor_tensor(w2[:, i], xo[:, i], sb_, ALU.mult), qi_tok, td, L)
                a2 = pool(lambda i=i, sb_=sb_: nc.gpsimd.tensor_tensor(u1[:, i], xe[:, i], sb_, ALU.mult), qi_tok, td, L)
                e2 = dve(lambda i=i, cb_=cb_: nc.vector.tensor_tensor(xo[:, i], xo[:, i], cb_, ALU.mult), e)
                toks.append((a2, e, e2))
                if i % 4 == 3:
                    yield
            for i in range(NT):
                a2, e, e2 = toks[i]
                f1 = dve(lambda i=i: nc.vector.tensor_tensor(xe[:, i], w1[:, i], w2[:, i], ALU.subtract), a2, e)
                f2 = dve(lambda i=i: nc.vector.tensor_tensor(xo[:, i], u1[:, i], xo[:, i], ALU.add), a2, e2)
                if i % 4 == 3:
                    yield
            if not norm:
                Tr.give(ti, f2)
                return [f1, f2]
            k = NT * nh
            qv = QK[:, :, 0:nh * D]
            e = dve(lambda: nc.vector.tensor_tensor(t1[:, 0:k * D].rearrange("p (n c) -> p n c", n=NT), qv, qv, ALU.mult), f1, f2)
            si_, ss, sd = (yield from SQ.take())
            e = dve(lambda: nc.vector.tensor_reduce(ss[:, 0:k], t1[:, 0:k * D].rearrange("p (k c) -> p k c", c=D), AX.X, ALU.add),
                    e, sd)
            Tr.give(ti, e)
            ni, _, nd = (yield from NWr.take())
            y, e = newton(None, k, ss[:, 0:k], 1.0 / D, 1e-6, e, nd)
            yield
            yv = y.rearrange("p (n h) -> p n h", n=NT)
            for i in range(NT):
                e2 = dve(lambda i=i: nc.vector.tensor_tensor(v[:, i], v[:, i], yv[:, i, :].unsqueeze(2).broadcast_to([128, nh, D]),
                                                             ALU.mult), e)
            NWr.give(ni, e2)
            SQ.give(si_, e2)
            return [e2]

        Hs = {}

        def b_common(b, st, wsel, V):
            hb = Hs[b]
            ni, xn, nd = (yield from XNr.take())
            c = yield from rms(hb["buf"], xn, hb["toks"], nd)
            xi, xt, xd = (yield from XTr.take())
            t = yield from transposed(lambda i: xn[:, i, :], 128, xt, 0, c, xd, scale=n1w[:, wsel:wsel + 1])
            XNr.give(ni, (pe.sem, pe.n))
            return xi, xt, t

        def b_operands(b, st, toks, e_deps):
            fi, ff, fd = (yield from XTr.take())
            t = yield from transposed(lambda i: QK[:, i, 0:128], 128, ff, 0, toks, fd)
            st["qtok"][b], r = yield from split(ff[:, 0:T], 128, T, None, t, scr_q[b], sfree[b])
            XTr.give(fi, r)
            return None

        def k_operand(b, st, toks, c0, w):
            fi, ff, fd = (yield from XTr.take())
            t = yield from transposed(lambda i: QK[:, i, c0:c0 + w], w, ff, 0, toks, fd)
            st["ktok"][b], r = yield from split(ff[0:w, 0:T], w, T, None, t, scr_k[b, :, 0:w, 0:T], sfree[b])
            XTr.give(fi, r)

        def global_prologue(b, st, V):
            hi, hb, hd = yield from HBr.take()
            c = yield from layernorm(X[:, b, :, :], hb, [xtok[b], hd])
            Hs[b] = dict(buf=hb, toks=[c], i=hi)
            xi, xt, t = yield from b_common(b, st, 0, V)
            qi, _, qd = (yield from QKr.take())
            qe = []
            for g in range(2):
                ci, ps, cd = (yield from RC.take())
                for i in range(4):
                    p = pe(lambda g=g, i=i, ps=ps: mm(ps[:, 128 * i:128 * i + 128],
                                                      xt[:, 512 * g + 128 * i:512 * g + 128 * i + 128], gq[:, :],
                                                      start=True, stop=True), t, cd, L)
                e = act(lambda g=g, ps=ps: nc.scalar.activation(QK[:, 4 * g:4 * g + 4, 0:128],
                                                                ps.rearrange("p (a b) -> p a b", b=128), ACT.Copy), p, qd)
                RC.give(ci, e)
                qe.append(e)
                yield
            li, (lt, _), ld = (yield from Tr.take())
            le = []
            for g in range(2):
                ci, ps, cd = (yield from RC.take())
                p = pe(lambda g=g, ps=ps: mm(ps[0:32, :], gdown[:, :], xt[:, 512 * g:512 * g + 512], start=True, stop=True), t, cd, L)
                e = act(lambda g=g, ps=ps: nc.scalar.activation(lt[0:32, 512 * g:512 * g + 512], ps[0:32, :], ACT.Copy), p, ld)
                RC.give(ci, e)
                le.append(e)
            XTr.give(xi, p)
            yield
            vi, va, vd = (yield from take_v(8, 4))
            ci, ps, cd = (yield from RC.take())
            for i in range(8):
                p = pe(lambda i=i, ps=ps: mm(ps[:, 64 * i:64 * i + 64], lt[0:32, 128 * i:128 * i + 128], gup[:, :],
                                             start=True, stop=True), le, cd, L)
            Tr.give(li, p)
            psv = ps.rearrange("p (a b) -> p a b", b=64)
            e = dve(lambda: nc.vector.tensor_copy(QK[:, :, 128:160], psv[:, :, 0:32]), p, qd)
            qe.append(e)
            for i in range(8):
                e = dve(lambda i=i: nc.vector.tensor_copy(va_view(va, 8, 4, i, 1)[:, 0, :, 0:8],
                                                          psv[:, i, 32:64].rearrange("p (h c) -> p h c", c=8)), p, vd)
            RC.give(ci, e)
            V[b] = (va, [e], vi)
            yield
            rt = yield from rope_norm(20, 8, b, True, cgg, True, qe, None)
            yield from b_operands(b, st, rt, None)
            yield from k_operand(b, st, rt, 128, 32)
            QKr.give(qi, (pe.sem, pe.n))

        def wide_qkv(b, xt, xi, t, W, n, qw, vw, D, qd, V):
            vi, va, vd = (yield from take_v(D, vw // D))
            qe, ve = [], []
            for g in range(4):
                ci, ps, cd = (yield from RC.take())
                for i in range(2):
                    tt = 2 * g + i
                    p = pe(lambda tt=tt, i=i, ps=ps: mm(ps[:, 256 * i:256 * i + n], xt[:, 128 * tt:128 * tt + 128], W[:, :],
                                                        start=True, stop=True), t, cd, L)
                pv3 = ps.rearrange("p (a b) -> p a b", b=256)
                e = dve(lambda g=g, pv3=pv3: nc.vector.tensor_copy(QK[:, 2 * g:2 * g + 2, 0:qw], pv3[:, :, 0:qw]), p, qd)
                qe.append(e)
                for i in range(2):
                    e = dve(lambda g=g, i=i, pv3=pv3: nc.vector.tensor_copy(
                        va_view(va, D, vw // D, 2 * g + i, 1)[:, 0, :, 0:D],
                        pv3[:, i, qw:qw + vw].rearrange("p (h c) -> p h c", c=D)), p, vd)
                RC.give(ci, e)
                ve.append(e)
                yield
            XTr.give(xi, p)
            V[b] = (va, ve, vi)
            return qe

        def local_prologue(b, st, V):
            xi, xt, t = yield from b_common(b, st, 1, V)
            qi, _, qd = (yield from QKr.take())
            qe = yield from wide_qkv(b, xt, xi, t, lqkv, 192, 160, 32, 8, qd, V)
            rt = yield from rope_norm(20, 8, b, True, cgl, True, qe, None)
            yield from b_operands(b, st, rt, None)
            yield from k_operand(b, st, rt, 128, 32)
            QKr.give(qi, (pe.sem, pe.n))

        cgg = cg[:, 0]
        cgl = cg[:, 1]
        def finish_h(A):
            def finish(b, O, oi, ot):
                w = []
                yield from project(A, b, O, oi, ot, Hs[b]["buf"], Hs[b]["toks"], w)
                Hs[b]["toks"] = w
            return finish

        def finish_hx(A):
            def finish(b, O, oi, ot):
                w = []
                yield from project(A, b, O, oi, ot, Hs[b]["buf"], Hs[b]["toks"], w)
                e = pool(lambda b=b: nc.gpsimd.tensor_tensor(X[:, b, :, :], X[:, b, :, :], Hs[b]["buf"][:, :, :], ALU.add),
                         w, xtok[b])
                xtok[b] = [e]
                HBr.give(Hs[b]["i"], e)
            return finish

        A3 = dict(L=L, whole=False, D=8, group=4, kn=T, max=False, scale=RS8, chunks=causal_chunks(), units=4, wo=gwo, bias=None,
                  prologue=global_prologue, lead=0, rate=1)
        A3["finish"] = finish_h(A3)
        A4 = dict(L=L, whole=False, D=8, group=4, kn=T, max=False, scale=RS8, chunks=local_chunks(), units=4, wo=lwo, bias=None,
                  prologue=local_prologue, lead=0, rate=2)
        A4["finish"] = finish_hx(A4)

        def padded_prologue(b, st, V):
            ni, xn, nd = (yield from XNr.take())
            c = yield from layernorm(X[:, b, :, :], xn, [xtok[b], nd])
            xi, xt, xd = (yield from XTr.take())
            z = pool(lambda xt=xt: nc.gpsimd.memset(xt[:, 0:16], 0.0), xd)
            z = pool(lambda xt=xt: nc.gpsimd.memset(xt[:, T + 16:T + 32], 0.0), xd)
            t = yield from transposed(lambda i: xn[:, i, :], 128, xt, 16, c, xd)
            XNr.give(ni, (pe.sem, pe.n))
            qi, qf, qd = (yield from HBr.take())
            qff = qf[:, :, :].rearrange("p a b -> p (a b)")
            fi, ff, fd = (yield from XTr.take())
            es, ks = [], []
            ks.append(pool(lambda ff=ff: nc.gpsimd.memset(ff[0:16, 0:16], 0.0), fd))
            ks.append(pool(lambda ff=ff: nc.gpsimd.memset(ff[0:16, T + 16:T + 32], 0.0), fd))
            for g in range(2):
                ci, ps, cd = (yield from RC.take())
                p = pe(lambda g=g, ps=ps: mm(ps, aWq[:, :], xt[:, 16 + 512 * g:16 + 512 * g + 512], start=True, stop=True), t, cd, L)
                e = act(lambda g=g, ps=ps: nc.scalar.activation(qff[:, 512 * g:512 * g + 512], ps, ACT.Identity,
                                                                bias=abq[:, 0:1]), p, qd, L)
                RC.give(ci, e)
                es.append(e)
                ci, ps, cd = (yield from RC.take())
                p = pe(lambda g=g, ps=ps: mm(ps[0:16, :], aWkv[:, 0:16], xt[:, 16 + 512 * g:16 + 512 * g + 512],
                                             start=True, stop=True), t, cd, L)
                e = act(lambda g=g, ps=ps, ff=ff: nc.scalar.activation(ff[0:16, 16 + 512 * g:16 + 512 * g + 512], ps[0:16, :],
                                                                       ACT.Identity, bias=abk[:, 0:1]), p, fd, L)
                RC.give(ci, e)
                ks.append(e)
                yield
            vi, va, vd = (yield from take_v(8, 2))
            ci, ps, cd = (yield from RC.take())
            for j in range(9):
                n = 128 if j < 8 else 32
                pe.silent(lambda j=j, n=n, ps=ps: mm(ps[0:n, 16 * j:16 * j + 16], xt[:, 128 * j:128 * j + n], aWkv[:, 16:32],
                                                     start=True, stop=False), t, z, cd, L)
                valid = abv[:, 0:128] if j == 0 else abv[:, 128:160] if j == 8 else ones[0:1, :]
                p = pe(lambda j=j, n=n, ps=ps, valid=valid: mm(ps[0:n, 16 * j:16 * j + 16], valid, abv[:, 160:176],
                                                               start=False, stop=True))
            psv = ps[:, 0:144].rearrange("p (n h c) -> p n h c", n=9, c=8)
            for j in range(9):
                n = 128 if j < 8 else 32
                e = dve(lambda j=j, n=n: nc.vector.tensor_copy(va_view(va, 8, 2, j, 1)[0:n, 0, :, 0:8], psv[0:n, j]), p, vd)
            RC.give(ci, e)
            XTr.give(xi, p)
            V[b] = (va, [e], vi)
            yield
            st["ktok"][b], r = yield from split(ff[0:16, 0:T + 32], 16, T + 32, None, ks, scr_k[b, :, 0:16, 0:T + 32],
                                                sfree[b])
            XTr.give(fi, r)
            st["qtok"][b], r = yield from split(qff, 128, T, None, es, scr_q[b], sfree[b])
            HBr.give(qi, r)

        A5 = dict(L=L, whole=False, D=8, group=8, kn=T + 32, max=True, pieces=1, scores=scores_padded, scale=1.0, chunks=padded_chunks(),
                  units=4, wo=aWo, bias=96, prologue=padded_prologue, lead=2, rate=5)
        A5["finish"] = finish_into_x(A5)

        wfr = Pool([sb(f"WF{i}", [128, 8, 8]) for i in range(2)])
        Gr = Pool([None])
        LG = sb("LG", [128, 8, 8])
        MX = sb("MX", [128, 8, 8])
        IX = sb("IX", [128, 8, 8], U32)
        IXF = sb("IXF", [128, 8, 2])
        WW = sb("WW", [128, 3, 8])
        OH = sb("OH", [128, 8, 8])

        def moe(b, store):
            if True:
                hi_, hb, hd = (yield from HBr.take())
                c = (yield from layernorm(X[:, b, :, :], hb, [xtok[b], hd]))
                ni, xn, nd = (yield from XNr.take())
                c2 = (yield from rms(hb, xn, c, nd))
                xi, xt, xd = (yield from XTr.take())
                t = (yield from transposed(lambda i: xn[:, i, :], 128, xt, 0, c2, xd, scale=rmsw[:, 0:1]))
                XNr.give(ni, (pe.sem, pe.n))
                a = pool(lambda b=b, hb=hb: nc.gpsimd.tensor_tensor(X[:, b, :, :], X[:, b, :, :], hb[:, :, :], ALU.add), c, xtok[b])
                HBr.give(hi_, a, c2)
                xa = [a]
                ci, ps, cd = (yield from RC.take())
                for i in range(NT):
                    p = pe(lambda i=i, ps=ps, xt=xt: mm(ps[:, 8 * i:8 * i + 8], xt[:, 128 * i:128 * i + 128], gateT[:, :],
                                                        start=True, stop=True), t, cd, L)
                wi, WF, wd = (yield from wfr.take())
                gi, _, gd = yield from Gr.take()
                e = dve(lambda ps=ps: nc.vector.tensor_copy(LG[:, :, :].rearrange("p a b -> p (a b)"), ps[:, 0:64]), p, wd, gd)
                RC.give(ci, e)
                for i in range(NT):
                    e1 = dve(lambda i=i: nc.vector.max(MX[:, i, :], LG[:, i, :]), e)
                for i in range(NT):
                    e2 = dve(lambda i=i: nc.vector.max_index(IX[:, i, :], MX[:, i, :], LG[:, i, :]), e1)
                e2 = dve(lambda: nc.vector.tensor_copy(IXF[:, :, :], IX[:, :, 0:2]), e2)
                e1 = dve(lambda: nc.vector.tensor_tensor(WW[:, 0, :], MX[:, :, 1], MX[:, :, 0], ALU.subtract), e1)
                a1 = act(lambda: nc.scalar.activation(WW[:, 1, :], WW[:, 0, :], ACT.Exp), e1)
                e1 = dve(lambda: nc.vector.tensor_scalar(WW[:, 0, :], WW[:, 1, :], 1.0, 2.0, ALU.add, ALU.mult), a1)
                e1 = dve(lambda: nc.vector.reciprocal(WW[:, 2, :], WW[:, 0, :]), e1)
                e1 = dve(lambda: nc.vector.tensor_tensor(WW[:, 1, :], WW[:, 1, :], WW[:, 2, :], ALU.mult), e1)
                bc = [128, 8, 8]
                io = iota8[:, :].unsqueeze(1)
                e3 = dve(lambda WF=WF: nc.vector.tensor_tensor(WF[:, :, :], io.broadcast_to(bc), IXF[:, :, 0:1].broadcast_to(bc),
                                                               ALU.is_equal), e2, L)
                e3 = dve(lambda WF=WF: nc.vector.tensor_tensor(WF[:, :, :], WF[:, :, :],
                                                               WW[:, 2, :].unsqueeze(2).broadcast_to(bc), ALU.mult), e1, e3)
                e4 = dve(lambda: nc.vector.tensor_tensor(OH[:, :, :], io.broadcast_to(bc), IXF[:, :, 1:2].broadcast_to(bc),
                                                         ALU.is_equal), e2)
                e4 = dve(lambda: nc.vector.tensor_tensor(OH[:, :, :], OH[:, :, :],
                                                         WW[:, 1, :].unsqueeze(2).broadcast_to(bc), ALU.mult), e1, e4)
                wt = dve(lambda WF=WF: nc.vector.tensor_tensor(WF[:, :, :], WF[:, :, :], OH[:, :, :], ALU.add), e3, e4)
                Gr.give(gi, wt)
                fin = []
                for g in range(2):
                    prev = [None] * 4
                    for ex in range(NEXP):
                        hid, hs = [], []
                        for c in range(3):
                            if c % 2 == 0:
                                hid.append((yield from RPT.take()))
                            _, hT, hdd = hid[-1]
                            n = min(128, DE - 128 * c)
                            o = DE * ex + 128 * c
                            bi, pb, bd = yield from RB.take()
                            pu = pe(lambda o=o, n=n, pb=pb, g=g: mm(pb[0:n, 0, :], mW1[:, o:o + n], xt[:, 512 * g:512 * g + 512],
                                                                    start=True, stop=True), t, bd, L, ns=860)
                            pg = pe(lambda o=o, n=n, pb=pb, g=g: mm(pb[0:n, 1, :], mW2[:, o:o + n], xt[:, 512 * g:512 * g + 512],
                                                                    start=True, stop=True), ns=860)
                            si, sg, sd = yield from SGr.take()
                            a = act(lambda n=n, pb=pb, sg=sg: nc.scalar.activation(sg[0:n, :], pb[0:n, 0, :], ACT.Tanh, scale=0.5), pu, sd)
                            a = dve(lambda n=n, pb=pb, sg=sg: nc.vector.scalar_tensor_tensor(
                                sg[0:n, :], sg[0:n, :], 1.0, pb[0:n, 0, :], ALU.add, ALU.mult), a, ns=600)
                            e = dve(lambda n=n, pb=pb, sg=sg, hT=hT, c=c: nc.vector.tensor_tensor(
                                hT[0:n, 512 * (c % 2):512 * (c % 2) + 512], pb[0:n, 1, :], sg[0:n, :], ALU.mult), a, pg, hdd, ns=600)
                            SGr.give(si, e)
                            RB.give(bi, e)
                            hs.append(e)
                            yield
                        ci, ps, cd = yield from RP.take()
                        for i in range(4):
                            for c in range(3):
                                n = min(128, DE - 128 * c)
                                o = 512 * (c % 2) + 128 * i
                                pe.silent(lambda c=c, i=i, n=n, o=o, ex=ex, ps=ps, hT=hid[c // 2][1]:
                                          mm(ps[:, 128 * i:128 * i + 128], hT[0:n, o:o + 128],
                                             mW3[0:n, ex, c, :], start=(c == 0), stop=(c == 2)), hs, cd, L)
                            p = pe.sign()
                        for k in range(2):
                            RPT.give(hid[k][0], p)
                        for i in range(4):
                            tt = 4 * g + i
                            e = dve(lambda i=i, tt=tt, ps=ps, ex=ex: nc.vector.scalar_tensor_tensor(
                                X[:, b, tt, :], ps[:, 128 * i:128 * i + 128], WF[:, tt, ex:ex + 1], X[:, b, tt, :],
                                ALU.mult, ALU.add), p, wt, xa, prev[i])
                            prev[i] = e
                        RP.give(ci, e)
                        fin.append(e)
                        yield
                XTr.give(xi, (pe.sem, pe.n))
                wfr.give(wi, fin[-1])
                xtok[b] = [fin[-1]]
                if store:
                    dma(sp, nc.sync, out[b].rearrange("(n p) e -> p n e", p=128), X[:, b, :, :], xtok[b], store=True)


        MBD = sb("MBD", [128, 128])
        BE2 = sb("BE2", [8, 128])
        e = dve(lambda: nc.vector.tensor_scalar(BE2[:, :], bE[:, :], bS[:, 0:1], None, ALU.mult), L)
        p = pe(lambda: mm(PS[:, 0, 0:128], bE[:, :], BE2[:, :], start=True, stop=True), e)
        mbd = dve(lambda: nc.vector.scalar_tensor_tensor(MBD[:, :], ident[:, :], 0.25, PS[:, 0, 0:128], ALU.mult, ALU.add), p)
        RA.free[0] = [mbd]

        def sink_prologue(b, st, V):
            ni, xn, nd = (yield from XNr.take())
            c = yield from layernorm(X[:, b, :, :], xn, [xtok[b], nd])
            xi, xt, xd = (yield from XTr.take())
            t = yield from transposed(lambda i: xn[:, i, :], 128, xt, 0, c, xd)
            XNr.give(ni, (pe.sem, pe.n))
            qi, _, qd = (yield from QKr.take())
            qe = yield from wide_qkv(b, xt, xi, t, bqkv, 256, 192, 64, 16, qd, V)
            rt = yield from rope_norm(12, 16, b, False, cb, False, qe, None)
            yield from k_operand(b, st, rt, 128, 64)
            fi, ff, fd = (yield from XTr.take())
            t = yield from transposed(lambda i: QK[:, i, 0:128], 128, ff, 0, rt, fd)
            QKr.give(qi, (pe.sem, pe.n))
            gi, qf, gd = (yield from HBr.take())
            qff = qf[:, :, :].rearrange("p a b -> p (a b)")
            es = []
            for g in range(2):
                ci, ps, cd = (yield from RC.take())
                p = pe(lambda g=g, ps=ps: mm(ps, MBD[:, :], ff[:, 512 * g:512 * g + 512], start=True, stop=True), t, cd, mbd)
                e = act(lambda g=g, ps=ps: nc.scalar.activation(qff[:, 512 * g:512 * g + 512], ps, ACT.Copy), p, gd)
                RC.give(ci, e)
                es.append(e)
                yield
            XTr.give(fi, p)
            st["qtok"][b], r = yield from split(qff, 128, T, None, es, scr_q[b], sfree[b])
            HBr.give(gi, r)

        A7 = dict(L=L, whole=False, D=16, group=2, kn=T, max=True, pieces=1, scores=scores_sink, scale=1.0, chunks=sink_chunks(),
                  units=2, wo=bWo, bias=None, prologue=sink_prologue, lead=2, rate=5)
        A7["finish"] = finish_into_x(A7)

        def sequence(b):
            yield from attention(A1, b)
            yield from ffn(b)
            yield from attention(A3, b)
            yield from attention(A4, b)
            yield from ffn(b)
            yield from attention(A5, b)
            yield from moe(b, False)
            yield from attention(A7, b)
            yield from moe(b, True)

        waiting = [sequence(b) for b in range(NB)]
        going = [[0.0, i, waiting.pop(0)] for i in range(4)]
        turn = 4
        while going:
            going.sort(key=lambda g: g[:2])
            g = going[0]
            clock.front, before = 0.0, sum(len(q.items) for q in (pe, act, dve, pool, sp))
            if next(g[2], 0) == 0:
                going.remove(g)
                if waiting:
                    going.append([g[0], turn, waiting.pop(0)])
            elif sum(len(q.items) for q in (pe, act, dve, pool, sp)) > before:
                g[0] = clock.front
            else:
                g[0] += 100.0
            g[1] = turn
            turn += 1

        sp.items.append((sp.waits(stores), None, None, 0))

        with nc.Block() as block:
            @block.sync
            def _(eng):
                sp.play(eng)

            @block.tensor
            def _(eng):
                pe.play(eng)

            @block.vector
            def _(eng):
                dve.play(eng)

            @block.scalar
            def _(eng):
                act.play(eng)

            @block.gpsimd
            def _(eng):
                pool.play(eng)


def tables():
    import numpy as np

    def bf16(x):
        return (np.ascontiguousarray(x, np.float32).view(np.uint32) >> 16).astype(np.uint16)

    neg = np.float32(-1e30)
    i = np.arange(128)[:, None]

    def mask(allowed):
        return bf16(np.where(allowed, np.float32(0), neg))

    def rope(base, hd):
        inv = (np.float32(1.0) / np.float32(base) ** (np.arange(0, hd, 2, dtype=np.float32) / np.float32(hd))).astype(np.float32)
        f = np.arange(T, dtype=np.float32)[:, None] * inv[None, :]
        cs = np.stack([np.cos(f), np.sin(f)]).astype(np.float32)
        return np.ascontiguousarray(cs.reshape(2, NT, 128, hd // 2).transpose(2, 0, 1, 3))

    c160, c256 = np.arange(160)[None, :], np.arange(256)[None, :]
    c = {
        "ident": np.eye(128, dtype=np.float32), "identb": bf16(np.eye(128)),
        "ones": np.ones((128, 128), np.float32),
        "onesk": bf16(np.ones((3, 4, T + 32))),
        "mC": mask(np.arange(128)[None, :] >= i),
        "mL": mask((c160 - i >= 0) & (c160 - i < 32)),
        "mA": mask((i + 32 - c160 >= 0) & (i + 32 - c160 <= 31)),
        "mB": mask((c256 - i >= 0) & (c256 - i <= 127)),
        "mB0": mask((c256 - i >= 0) & ((c256 - i <= 127) | (i < 4))),
        "mBt": mask((i + 128 - c256 >= 0) & (i + 128 - c256 <= 127)),
        "mBt1": mask((i + 128 - c256 >= 0) & ((i + 128 - c256 <= 127) | (c256 < 4))),
        "cg": np.ascontiguousarray(np.stack([rope(1000000.0, 8), rope(10000.0, 8)], axis=1)),
        "cb": rope(10000.0, 16),
        "iota8": np.broadcast_to(np.arange(8, dtype=np.float32), (128, 8)).copy(),
    }
    return c


def laid_out(a):
    import numpy as np

    g = {k: np.asarray(v) for k, v in a.items()}
    f = np.float32
    o = {"x": g["L0_attn_a_x"]}
    wbd = np.zeros((128, 128), f)
    for h in range(16):
        wbd[8 * h:8 * h + 8, 8 * h:8 * h + 8] = g["L0_attn_a_w_att_val"][h]
    o["wbd"] = wbd
    o["wvT"] = g["L0_attn_a_wv_w"].T
    o["outT"] = g["L0_attn_a_out_w"].T
    rows = np.zeros((128, 512), f)
    for r, n in ((0, "L0_attn_a_wv_b"), (32, "L0_attn_a_out_b"), (64, "L0_ffn_b2"), (96, "L1_attn_a_bo")):
        for i in range(4):
            rows[r, 128 * i:128 * i + 128] = g[n]
    o["rows"] = rows
    o["fW1"] = g["L0_ffn_W1"]
    o["fb1"] = g["L0_ffn_b1"].reshape(4, 128).T
    o["fW2"] = g["L0_ffn_W2"].reshape(4, 128, 128).transpose(1, 0, 2)
    o["n1w"] = np.stack([g["L0_attn_b_norm1_w"], g["L0_attn_b_norm2_w"]], axis=1)
    o["gq"] = g["L0_attn_b_g_wq"]
    o["gdown"] = g["L0_attn_b_g_kv_down"]
    o["gup"] = np.concatenate([g["L0_attn_b_g_k_up"], g["L0_attn_b_g_v_up"]], axis=1)
    o["gwo"] = g["L0_attn_b_g_wo"]
    o["lqkv"] = np.concatenate([g["L0_attn_b_l_wq"], g["L0_attn_b_l_wk"], g["L0_attn_b_l_wv"]], axis=1)
    o["lwo"] = g["L0_attn_b_l_wo"]
    o["aWq"] = g["L1_attn_a_Wq"]
    o["aWkv"] = np.concatenate([g["L1_attn_a_Wk"], g["L1_attn_a_Wv"]], axis=1)
    o["aWo"] = g["L1_attn_a_Wo"]
    o["abq"] = g["L1_attn_a_bq"][:, None]
    o["abk"] = g["L1_attn_a_bk"][:, None]
    abv = np.zeros((1, 176), f)
    abv[0, 16:144] = 1.0
    abv[0, 160:] = g["L1_attn_a_bv"]
    o["abv"] = abv
    o["bqkv"] = np.concatenate([g["L1_attn_b_Wq"], g["L1_attn_b_Wk"], g["L1_attn_b_Wv"]], axis=1)
    o["bWo"] = g["L1_attn_b_Wo"]
    bE = np.zeros((8, 128), f)
    for h in range(8):
        bE[h, 16 * h:16 * h + 3] = g["L1_attn_b_head_dirs"][h]
    o["bE"] = bE
    o["bS"] = g["L1_attn_b_head_scales"][:, None]
    o["gateT"] = g["L1_ffn_gate_w"].T
    o["rmsw"] = g["L1_ffn_rms_w"][:, None]
    o["mW1"] = g["L1_ffn_W1"].transpose(2, 0, 1).reshape(128, NEXP * DE)
    o["mW2"] = g["L1_ffn_W2"].transpose(2, 0, 1).reshape(128, NEXP * DE)
    w3 = np.zeros((128, NEXP, 3, 128), f)
    for e in range(NEXP):
        for c in range(3):
            n = min(128, DE - 128 * c)
            w3[0:n, e, c, :] = g["L1_ffn_W3"][e][:, 128 * c:128 * c + n].T
    o["mW3"] = w3
    return o


def kernel(**inputs):
    import numpy as _np
    import concourse.bacc as _bacc
    from concourse import mybir as _mybir
    from concourse.bass_utils import run_bass_kernel_spmd as _run

    nc = _bacc.Bacc("TRN2", target_bir_lowering=False, num_devices=1)
    arrays, args = {}, {}
    for name, a in {**laid_out(inputs), **tables()}.items():
        a = _np.ascontiguousarray(a)
        arrays[f"in_{name}"] = a
        args[name] = nc.dram_tensor(f"in_{name}", a.shape, _mybir.dt.from_np(a.dtype), kind="ExternalInput").ap()
        if a.dtype == _np.uint16:
            args[name] = args[name].bitcast(_mybir.dt.bfloat16)
    out = nc.dram_tensor("out_0", (NB, T, E), _mybir.dt.float32, kind="ExternalOutput").ap()
    scr_q = nc.dram_tensor("scr_q", (NB, 3, 128, T), _mybir.dt.bfloat16, kind="Internal").ap()
    scr_k = nc.dram_tensor("scr_k", (NB, 3, 128, T + 32), _mybir.dt.bfloat16, kind="Internal").ap()
    scr_m = nc.dram_tensor("scr_m", (NB, 3, 32, 128), _mybir.dt.bfloat16, kind="Internal").ap()
    program(nc, args, out, scr_q, scr_k, scr_m)
    r = _run(nc, [arrays], core_ids=[0])
    return r.results[0]["out_0"]
```
